# Optimizing a Trainium2 kernel written in Bass

```python
import numpy as np
import jax
import jax.numpy as jnp

def _softmax(x, axis=-1):
    return jax.nn.softmax(x, axis=axis)

def _gelu(x):
    return jax.nn.gelu(x, approximate=True)

def _silu(x):
    return jax.nn.silu(x)

def _sigmoid(x):
    return jax.nn.sigmoid(x)

def _layernorm(x, axis=-1, eps=1e-05):
    m = jnp.mean(x, axis=axis, keepdims=True)
    v = jnp.var(x, axis=axis, keepdims=True)
    return (x - m) / jnp.sqrt(v + eps)

def _scatter_add(tgt, idx, src, axis=0):
    return tgt.at[idx].add(src)

def _segment_sum(src, seg, n):
    return jax.ops.segment_sum(src, seg, n)
kernel_name = 'mk_gnn_ffn_d1_gnn_r8_049f9f'

def setup_inputs(seed: int=0):
    np.random.seed(seed)
    _w = jnp.asarray

    def _rec_inputs():
        import jax
        import jax.numpy as jnp
        _gk = jax.random.key(seed)
        x = -0.0003713 + 1 * jax.random.normal(jax.random.fold_in(_gk, 1), (6250, 256), jnp.float32)
        src = jax.random.randint(jax.random.fold_in(_gk, 2), (100000,), 0, 6250, jnp.int32)
        dst = jax.random.randint(jax.random.fold_in(_gk, 3), (100000,), 0, 6250, jnp.int32)
        _o = jnp.argsort(dst, stable=True)
        src = src[_o]
        dst = dst[_o]
        edge_type_64 = jax.random.randint(jax.random.fold_in(_gk, 12), (100000,), 0, 64, jnp.int32)
        return (x, src, dst, edge_type_64)
    x, src, dst, edge_type_64 = _rec_inputs()

    def _L0_gnn_setup():
        import jax, jax.numpy as jnp
        import numpy as np
        N_NODES = 6250
        N_EDGES = 62500
        IN_DIM = 256
        HID = 64
        HEADS = 4
        N_REL = 64
        key = jax.random.key(seed)
        ks = jax.random.split(key, 16)
        s = 0.02
        return {'node_features': jax.random.normal(ks[0], (N_NODES, IN_DIM), jnp.float32), 'edge_index': jax.random.randint(ks[1], (2, N_EDGES), 0, N_NODES, jnp.int32), 'edge_relations': jax.random.randint(ks[2], (N_EDGES,), 0, N_REL, jnp.int32), 'query_emb': jax.random.normal(ks[3], (IN_DIM,), jnp.float32), 'Wq': jax.random.normal(ks[4], (IN_DIM, HID * HEADS), jnp.float32) * s, 'bq': jnp.zeros((HID * HEADS,), jnp.float32), 'Wk': jax.random.normal(ks[5], (IN_DIM, HID * HEADS), jnp.float32) * s, 'bk': jnp.zeros((HID * HEADS,), jnp.float32), 'Wv': jax.random.normal(ks[6], (IN_DIM, HID * HEADS), jnp.float32) * s, 'bv': jnp.zeros((HID * HEADS,), jnp.float32), 'rel_w': jax.random.normal(ks[7], (N_REL, HID), jnp.float32) * s, 'Wo': jax.random.normal(ks[8], (HID * HEADS, IN_DIM), jnp.float32) * s, 'bo': jnp.zeros((IN_DIM,), jnp.float32), 'gamma': jnp.ones((IN_DIM,), jnp.float32), 'beta': jnp.zeros((IN_DIM,), jnp.float32)}
    _L0_gnn_all = _L0_gnn_setup()
    _L0_gnn_in = {k: v for k, v in _L0_gnn_all.items() if k in ('query_emb', 'Wq', 'bq', 'Wk', 'bk', 'Wv', 'bv', 'rel_w', 'Wo', 'bo', 'gamma', 'beta')}
    del _L0_gnn_all

    def _L0_ffn_setup():
        import jax, jax.numpy as jnp
        import numpy as np
        TOP_K = 2
        LN_EPS = 1e-05
        key = jax.random.key(seed)
        ks = jax.random.split(key, 8)
        B, S, D, E, H = (16, 1024, 256, 8, 1024)
        x = jax.random.normal(ks[0], (B, S, D), dtype=jnp.float32)
        Wr = jax.random.normal(ks[1], (D, E), dtype=jnp.float32) * 0.1
        br = jnp.zeros((E,), dtype=jnp.float32)
        ln_g = jnp.ones((E, D), dtype=jnp.float32)
        ln_b = jnp.zeros((E, D), dtype=jnp.float32)
        W1 = jax.random.normal(ks[2], (E, D, H), dtype=jnp.float32) * (1.0 / np.sqrt(D))
        b1 = jnp.zeros((E, H), dtype=jnp.float32)
        W2 = jax.random.normal(ks[3], (E, H, D), dtype=jnp.float32) * (1.0 / np.sqrt(H))
        b2 = jnp.zeros((E, D), dtype=jnp.float32)
        return {'x': x, 'Wr': Wr, 'br': br, 'ln_g': ln_g, 'ln_b': ln_b, 'W1': W1, 'b1': b1, 'W2': W2, 'b2': b2}
    _L0_ffn_all = _L0_ffn_setup()
    _L0_ffn_in = {k: v for k, v in _L0_ffn_all.items() if k in ('Wr', 'br', 'ln_g', 'ln_b', 'W1', 'b1', 'W2', 'b2')}
    del _L0_ffn_all
    return {'x': x, 'src': src, 'dst': dst, 'edge_type_64': edge_type_64, 'L0_gnn_query_emb': _L0_gnn_in['query_emb'], 'L0_gnn_Wq': _L0_gnn_in['Wq'], 'L0_gnn_bq': _L0_gnn_in['bq'], 'L0_gnn_Wk': _L0_gnn_in['Wk'], 'L0_gnn_bk': _L0_gnn_in['bk'], 'L0_gnn_Wv': _L0_gnn_in['Wv'], 'L0_gnn_bv': _L0_gnn_in['bv'], 'L0_gnn_rel_w': _L0_gnn_in['rel_w'], 'L0_gnn_Wo': _L0_gnn_in['Wo'], 'L0_gnn_bo': _L0_gnn_in['bo'], 'L0_gnn_gamma': _L0_gnn_in['gamma'], 'L0_gnn_beta': _L0_gnn_in['beta'], 'L0_ffn_Wr': _L0_ffn_in['Wr'], 'L0_ffn_br': _L0_ffn_in['br'], 'L0_ffn_ln_g': _L0_ffn_in['ln_g'], 'L0_ffn_ln_b': _L0_ffn_in['ln_b'], 'L0_ffn_W1': _L0_ffn_in['W1'], 'L0_ffn_b1': _L0_ffn_in['b1'], 'L0_ffn_W2': _L0_ffn_in['W2'], 'L0_ffn_b2': _L0_ffn_in['b2']}

def reference(x, src, dst, edge_type_64, L0_gnn_query_emb, L0_gnn_Wq, L0_gnn_bq, L0_gnn_Wk, L0_gnn_bk, L0_gnn_Wv, L0_gnn_bv, L0_gnn_rel_w, L0_gnn_Wo, L0_gnn_bo, L0_gnn_gamma, L0_gnn_beta, L0_ffn_Wr, L0_ffn_br, L0_ffn_ln_g, L0_ffn_ln_b, L0_ffn_W1, L0_ffn_b1, L0_ffn_W2, L0_ffn_b2):
    import jax
    import jax.numpy as jnp

    def _L0_gnn_ref(node_features, edge_index, edge_relations, query_emb, Wq, bq, Wk, bk, Wv, bv, rel_w, Wo, bo, gamma, beta):
        import jax, jax.numpy as jnp
        import numpy as np
        N_NODES = 6250
        N_EDGES = 62500
        IN_DIM = 256
        HID = 64
        HEADS = 4
        N_REL = 64
        N = node_features.shape[0]
        D = rel_w.shape[1]
        H = Wq.shape[1] // D
        enh = node_features + 0.1 * query_emb[None, :]
        Q = (enh @ Wq + bq).reshape(N, H, D)
        K = (enh @ Wk + bk).reshape(N, H, D)
        V = (enh @ Wv + bv).reshape(N, H, D)
        src, dst = (edge_index[0], edge_index[1])
        rel = rel_w[edge_relations]
        mod_k = K[src] + 0.2 * rel[:, None, :]
        scores = jnp.einsum('ehd,ehd->eh', Q[dst], mod_k) / D ** 0.5
        seg_max = jax.ops.segment_max(scores, dst, num_segments=N)
        ex = jnp.exp(scores - seg_max[dst])
        denom = jax.ops.segment_sum(ex, dst, num_segments=N)
        w = ex / denom[dst]
        agg = jax.ops.segment_sum(w[:, :, None] * V[src], dst, num_segments=N)
        deg = jax.ops.segment_sum(jnp.ones((src.shape[0],), jnp.float32), dst, num_segments=N)
        msgs = jnp.where(deg[:, None, None] > 0, agg, V)
        out = msgs.reshape(N, H * D) @ Wo + bo
        x = out + node_features
        mu = jnp.mean(x, axis=-1, keepdims=True)
        var = jnp.var(x, axis=-1, keepdims=True)
        return (x - mu) / jnp.sqrt(var + 1e-05) * gamma + beta

    def _L0_ffn_ref(x, Wr, br, ln_g, ln_b, W1, b1, W2, b2):
        import jax, jax.numpy as jnp
        import numpy as np
        TOP_K = 2
        LN_EPS = 1e-05
        B, S, D = x.shape
        N = B * S
        xt = x.reshape(N, D)
        logits = xt @ Wr + br
        probs = jax.nn.softmax(logits, axis=-1)
        top_p, top_idx = jax.lax.top_k(probs, TOP_K)
        weights = top_p / top_p.sum(axis=-1, keepdims=True)
        mu = xt.mean(axis=-1, keepdims=True)
        var = ((xt - mu) ** 2).mean(axis=-1, keepdims=True)
        xn = (xt - mu) * jax.lax.rsqrt(var + LN_EPS)
        xe = xn[None, :, :] * ln_g[:, None, :] + ln_b[:, None, :]
        h = jax.nn.gelu(jnp.einsum('end,edh->enh', xe, W1) + b1[:, None, :], approximate=False)
        y = jnp.einsum('enh,ehd->end', h, W2) + b2[:, None, :]
        y_tok = jnp.transpose(y, (1, 0, 2))
        sel = jnp.take_along_axis(y_tok, top_idx[:, :, None], axis=1)
        out = (weights[:, :, None] * sel).sum(axis=1)
        return out.reshape(B, S, D)
    edge_index = jnp.stack([src, dst])
    x = x + _L0_gnn_ref(_layernorm(x, axis=-1), edge_index, edge_type_64, L0_gnn_query_emb, L0_gnn_Wq, L0_gnn_bq, L0_gnn_Wk, L0_gnn_bk, L0_gnn_Wv, L0_gnn_bv, L0_gnn_rel_w, L0_gnn_Wo, L0_gnn_bo, L0_gnn_gamma, L0_gnn_beta)
    x = x + _L0_ffn_ref(_layernorm(x, axis=-1)[None], L0_ffn_Wr, L0_ffn_br, L0_ffn_ln_g, L0_ffn_ln_b, L0_ffn_W1, L0_ffn_b1, L0_ffn_W2, L0_ffn_b2)[0]
    return x

_drawn_inputs = setup_inputs


def setup_inputs(seed=0):
    import zlib

    import numpy as np

    out = dict(_drawn_inputs(seed))
    spreads = {'L0_gnn_bq': (0.0, 0.8),
     'L0_gnn_bk': (0.0, 2.0),
     'L0_gnn_bv': (0.0, 0.287),
     'L0_gnn_bo': (0.0, 0.1),
     'L0_gnn_gamma': (1.0, 0.2),
     'L0_gnn_beta': (0.0, 0.1),
     'L0_ffn_br': (0.0, 0.1),
     'L0_ffn_ln_g': (1.0, 0.2),
     'L0_ffn_ln_b': (0.0, 0.307),
     'L0_ffn_b1': (0.0, 0.302),
     'L0_ffn_b2': (0.0, 0.1)}
    factors = {'L0_gnn_query_emb': 5.092, 'L0_gnn_Wq': 8.0, 'L0_gnn_Wk': 8.0, 'L0_gnn_rel_w': 200.0}
    for name, (base, spread) in spreads.items():
        noise = np.random.default_rng([zlib.crc32(name.encode()), seed]).standard_normal(out[name].shape)
        drawn = base * np.exp(spread * noise) if base else spread * noise
        out[name] = jnp.asarray(drawn.astype(out[name].dtype))
    for name, factor in factors.items():
        out[name] = (out[name] * factor).astype(out[name].dtype)
    return out
```

```python
import numpy as np
import concourse.bass as bass
from concourse import mybir
from contextlib import ExitStack

F32 = mybir.dt.float32
BF16 = mybir.dt.bfloat16
I32 = mybir.dt.int32
I16 = mybir.dt.int16
U32 = mybir.dt.uint32
ALU = mybir.AluOpType
ACT = mybir.ActivationFunctionType
AX = mybir.AxisListType

P = 128
N_NODES, N_EDGES = 6250, 100000
D = 256
HEADS, HD = 4, 64
N_REL = 64
NT = -(-N_NODES // P)
NPAD = NT * P
WIN = 32
NWIN = NPAD // WIN
WPT = P // WIN
ET = -(-N_EDGES // P) + 1
ET_PAD = -(-ET // P) * P
STEPS = ET + NWIN - 1
STEPS_PAD = -(-STEPS // P) * P
PAD_DST = NPAD - 1
VW = HD + 1
ROW = D + HEADS * VW
FAR = -1.0e30
FLOOR = -1.0e20
SCALE = 1.0 / np.sqrt(HD)
EPS = 1e-5
E, H = 8, 1024
KD, KH = D // P, H // P
MT = (2 * NPAD + E * (P - 1)) // P


def wait(eng, sem, value):
    if not (isinstance(value, int) and value <= 0):
        eng.wait_ge(sem, value)


class Step:

    def __init__(self, turn, at, period=4):
        self.period = period
        self.turn = turn + at // period
        self.slot = at % period
        self.n = turn * period + at
        self.par = self.slot % 2
        self.base, self.at = turn, at

    def __add__(self, k):
        return Step(self.base, self.at + k, self.period)

    def __sub__(self, k):
        return self + (-k)


def walk(eng, first, last, body, period=4, head=1):
    start = head
    lead = start * period + first
    turns = (last + 1 - lead) // period
    if turns < 2:
        for n in range(first, last + 1):
            body(Step(0, n, period))
        return
    for n in range(first, lead):
        body(Step(0, n, period))
    with eng.Fori(start, start + turns) as turn:
        for k in range(period):
            body(Step(turn, first + k, period))
    for n in range(lead + turns * period, last + 1):
        body(Step(0, n, period))


class Scope:

    def __init__(self, nc, tag):
        self.nc, self.tag, self.stack, self.sems = nc, tag, ExitStack(), []

    def __enter__(self):
        self.stack.__enter__()
        return self

    def __exit__(self, *a):
        self.nc.clear_and_free_semaphores(self.sems)
        self.nc.all_engine_barrier()
        return self.stack.__exit__(*a)

    def sb(self, name, shape, dt=F32):
        return self.stack.enter_context(self.nc.sbuf_tensor(f"{self.tag}_{name}", shape, dt))

    def ps(self, name, shape):
        bank = self.stack.enter_context(self.nc.psum_tensor(f"{self.tag}_{name}", [P, 512], F32))
        if len(shape) == 2:
            return bank[:, 0:shape[1]]
        return bank[:, 0:shape[1] * shape[2]].rearrange("p (a b) -> p a b", a=shape[1])

    def sem(self, name):
        self.sems.append(self.nc.alloc_semaphore(f"{self.tag}_{name}"))
        return self.sems[-1]

    def block(self):
        return self.nc.Block()


def rows(ap, first, count):
    return ap[bass.ds(first, count), :]


def setup(nc, a, g, s):
    sb, ps, sem = s.sb, s.ps, s.sem
    loaded, made, zeroed = sem("loaded"), sem("made"), sem("zeroed")
    tables_out, tables_in = sem("tables_out"), sem("tables_in")
    conv_in, conv = sem("conv_in"), sem("conv")
    pe_done, dve, dve0 = sem("pe_done"), sem("dve"), sem("dve0")
    relt2 = sb("relt2", [P, P])
    wqt = sb("wqt", [P, KD, D])
    qcol = sb("qcol", [P, KD])
    qwide = sb("qwide", [P, KD, P])
    bqc = sb("bqc", [P, KD])
    bkv = sb("bkv", [P, 2 * D])
    first = sb("first", [P, ET - 1], I32)
    firstw = sb("firstw", [P, ET - 1], I32)
    key = sb("key", [P, ET - 1])
    keyj = sb("keyj", [P, ET - 1])
    hit = sb("hit", [P, ET - 1])
    sno = sb("sno", [P, STEPS_PAD // P])
    jf = sb("jf", [P, STEPS_PAD // P])
    ji = sb("ji", [P, STEPS_PAD // P], I32)
    wi = sb("wi", [P, STEPS_PAD // P], I32)
    wrow = sb("wrow", [P, STEPS], I32)
    pno, noi = sb("pno", [P, 1], I32), sb("noi", [P, 1], I32)
    nof = sb("nof", [P, 1])
    raw = sb("raw", [P, 2, ET_PAD], I32)
    raw16 = sb("raw16", [P, ET_PAD // P, 2, P], I16)
    zero = sb("zero", [P, D])
    pw = ps("pw", [P, 4, P])
    pc = ps("pc", [P, 8])
    pr = ps("pr", [P, 2 * D])
    LOADS = 21

    with s.block() as block:
        @block.sync
        def _(sp):
            load = lambda dst, src: sp.dma_start(dst, src).then_inc(loaded, 16)
            sp.wait_ge(zeroed, 1)
            for hh in range(2):
                load(relt2[hh * HD:(hh + 1) * HD, hh * N_REL:(hh + 1) * N_REL], a["relT"])
            load(wqt[:], a["WqT"].rearrange("(c p) k -> p c k", p=P))
            load(g.wq[:], a["Wq"].rearrange("(c p) n -> p c n", p=P))
            load(g.wkv[:, :, 0:D], a["Wk"].rearrange("(c p) n -> p c n", p=P))
            load(g.wkv[:, :, D:2 * D], a["Wv"].rearrange("(c p) n -> p c n", p=P))
            load(qcol[:], a["q_emb"])
            load(bqc[:], a["bq"])
            load(bkv[:, 0:D], a["bk"].rearrange("(o n) -> o n", o=1).to_broadcast([P, D]))
            load(bkv[:, D:2 * D], a["bv"].rearrange("(o n) -> o n", o=1).to_broadcast([P, D]))
            load(first[:], a["first"].rearrange("(o n) -> o n", o=1).to_broadcast([P, ET - 1]))
            load(g.wo[:], a["Wo"].rearrange("(h p) n -> p h n", p=HD))
            load(g.bo[:], a["bo"].rearrange("(o n) -> o n", o=1).to_broadcast([P, D]))
            load(g.gamma[:], a["gamma"].rearrange("(o n) -> o n", o=1).to_broadcast([P, D]))
            load(g.beta[:], a["beta"].rearrange("(o n) -> o n", o=1).to_broadcast([P, D]))
            load(g.br[:], a["br"].rearrange("(o n) -> o n", o=1).to_broadcast([P, E]))
            load(g.wr[:], a["Wr"].rearrange("(c p) n -> p c n", p=P))
            load(raw[:, 0, :], a["dst2d"].rearrange("(p g) e -> p (g e)", p=P))
            load(raw[:, 1, :], a["et2d"].rearrange("(p g) e -> p (g e)", p=P))
            load(g.b1f[0:E, :], a["b1"])
            load(g.b2f[0:E, :], a["b2"])
            sp.wait_ge(made, 2)
            sp.dma_start(a["jtab"].rearrange("(p c) -> p c", p=P), ji[:]).then_inc(tables_out, 16)
            sp.dma_start(a["wtab"].rearrange("(p c) -> p c", p=P), wi[:]).then_inc(tables_out, 16)
            sp.wait_ge(tables_out, 32)
            sp.dma_start(wrow[:], a["wtab"][0:STEPS].rearrange("(o n) -> o n", o=1).to_broadcast([P, STEPS])).then_inc(tables_in, 16)
            sp.dma_start(g.jreg[0:1, :], a["jtab"][0:STEPS].rearrange("(o n) -> o n", o=1)).then_inc(tables_in, 16)
            sp.dma_start(g.wreg[0:1, :], a["wtab"][0:STEPS].rearrange("(o n) -> o n", o=1)).then_inc(tables_in, 16)
            sp.wait_ge(conv, 2)
            sp.dma_start(a["dt16"].rearrange("(p g) k e -> p (g k e)", p=P), raw16[:].rearrange("p g k e -> p (g k e)")).then_inc(conv_in, 16)
            sp.wait_ge(conv_in, 16)
            sp.wait_ge(tables_in, 48)

        @block.gpsimd
        def _(pool):
            pool.memset(g.ident[:], 0.0).then_inc(g.gp, 1)
            pool.memset(g.tri[:], 1.0).then_inc(g.gp, 1)
            pool.iota(sno[:], pattern=[[1, STEPS_PAD // P]], base=0, channel_multiplier=STEPS_PAD // P,
                      allow_small_or_imprecise_dtypes=True).then_inc(g.gp, 1)
            pool.iota(keyj[:], pattern=[[1, ET - 1]], base=1, channel_multiplier=0,
                      allow_small_or_imprecise_dtypes=True).then_inc(g.gp, 1)
            pool.iota(g.tileno[:], pattern=[[1, MT]], base=0, channel_multiplier=0,
                      allow_small_or_imprecise_dtypes=True).then_inc(g.gp, 1)
            pool.iota(g.iota8[:], pattern=[[1, E]], base=0, channel_multiplier=0,
                      allow_small_or_imprecise_dtypes=True).then_inc(g.gp, 1)
            pool.iota(g.rno[:], pattern=[[0, 1]], base=0, channel_multiplier=1,
                      allow_small_or_imprecise_dtypes=True).then_inc(g.gp, 1)
            pool.wait_ge(g.gp, 7)
            pool.affine_select(out=g.ident[:], in_=g.ident[:], compare_op=ALU.not_equal, fill=1.0, base=0,
                               pattern=[[-1, P]], channel_multiplier=1).then_inc(g.gp, 1)
            pool.affine_select(out=g.tri[:], in_=g.tri[:], compare_op=ALU.is_gt, fill=0.0, base=0,
                               pattern=[[1, P]], channel_multiplier=-1).then_inc(g.gp, 1)
            pool.iota(pno[:], pattern=[[0, 1]], base=0, channel_multiplier=1).then_inc(g.gp, 1)

        @block.vector
        def _(v):
            v.memset(relt2[:], 0.0).then_inc(zeroed, 1)
            v.memset(zero[:], 0.0).then_inc(zeroed, 1)
            v.memset(g.ones[:], 1.0).then_inc(dve0, 1)
            v.memset(g.eps[:], EPS).then_inc(dve0, 1)
            v.wait_ge(dve0, 2)
            v.wait_ge(zeroed, 2)
            v.wait_ge(loaded, 16 * LOADS)
            v.wait_ge(g.gp, 10)
            v.tensor_single_scalar(firstw[:], first[:], 5, ALU.arith_shift_right).then_inc(dve, 1)
            v.wait_ge(dve, 1)
            v.tensor_tensor(key[:], firstw[:], keyj[:], ALU.add).then_inc(dve, 1)
            for c in range(STEPS_PAD // P):
                v.wait_ge(dve, 2 + c)
                v.tensor_scalar(hit[:], key[:], sno[:, c:c + 1], 0.0, ALU.is_le, ALU.add,
                                accum_out=jf[:, c:c + 1]).then_inc(dve, 1)
            v.wait_ge(dve, 2 + STEPS_PAD // P)
            v.tensor_copy(ji[:], jf[:]).then_inc(made, 1)
            v.tensor_tensor(wi[:], sno[:], jf[:], ALU.subtract).then_inc(made, 1)
            v.tensor_single_scalar(noi[:], pno[:], WIN - 1, ALU.bitwise_and).then_inc(dve, 1)
            v.wait_ge(dve, 3 + STEPS_PAD // P)
            v.tensor_copy(nof[:], noi[:]).then_inc(dve, 1)
            for k in range(2):
                v.tensor_copy(raw16[:, :, k, :], raw[:, k, :].rearrange("p (g e) -> p g e", e=P)).then_inc(conv, 1)
            v.tensor_scalar(relt2[:], relt2[:], 0.2, None, ALU.mult).then_inc(zeroed, 1)
            for c in range(KD):
                v.tensor_scalar(qwide[:, c, :], g.ones[:], qcol[:, c:c + 1], 0.1, ALU.mult, ALU.mult).then_inc(zeroed, 1)
            v.wait_ge(pe_done, 1)
            v.tensor_copy(g.wqr[:].rearrange("p k (c n) -> p k c n", c=2),
                          pw[:].rearrange("p (k c) n -> p k c n", c=2)).then_inc(dve, 1)
            v.wait_ge(pe_done, 2)
            v.tensor_tensor(g.cq[:], pc[:, 0:2], bqc[:], ALU.add).then_inc(made, 1)
            v.wait_ge(pe_done, 3)
            v.tensor_copy(g.cqr[:], pc[:, 4:6])
            v.tensor_tensor(g.ckv[:], pr[:], bkv[:], ALU.add)
            v.wait_ge(tables_in, 48)
            v.wait_ge(dve, 5 + STEPS_PAD // P)
            v.tensor_scalar(g.nabs[:], wrow[:], float(WIN), nof[:, 0:1], ALU.mult, ALU.add)

        @block.tensor
        def _(pe):
            pe.wait_ge(zeroed, 5)
            for k in range(KD):
                for c in range(2):
                    last = nc.tensor.matmul(pw[:, 2 * k + c, :], wqt[:, c, k * P:(k + 1) * P], relt2[:], start=True, stop=True)
            last.then_inc(pe_done, 1)
            for c in range(2):
                for k in range(KD):
                    last = nc.tensor.matmul(pc[:, c:c + 1], g.wq[:, k, c * P:(c + 1) * P], qwide[:, k, 0:1], start=(k == 0), stop=(k == KD - 1))
            last.then_inc(pe_done, 1)
            for k in range(KD):
                nc.tensor.matmul(pr[:], qwide[:, k, :], g.wkv[:, k, :], start=(k == 0), stop=(k == KD - 1))
            pe.wait_ge(made, 3)
            for c in range(2):
                last = nc.tensor.matmul(pc[:, 4 + c:5 + c], relt2[:], g.cq[:, c:c + 1], start=True, stop=True)
            last.then_inc(pe_done, 1)

        @block.scalar
        def _(act):
            act.wait_ge(zeroed, 2)
            xs = a["xs"].rearrange("(t p) d -> p t d", p=P)
            CH = 15
            for t in range(0, MT, CH):
                n = min(CH, MT - t)
                act.dma_start(xs[:, t:t + n, :], zero[:, None, :].to_broadcast([P, n, D])).then_inc(g.xs_clear, 16)
            act.wait_ge(g.xs_clear, 16 * (-(-MT // CH)))


def nodes(nc, a, g, s):
    sb, ps, sem = s.sb, s.ps, s.sem
    xin = [sb(f"xin{i}", [P, D]) for i in range(2)]
    x1s = [sb(f"x1s{i}", [P, D]) for i in range(2)]
    stats = [sb(f"stats{i}", [P, 6]) for i in range(2)]
    mv = [sb(f"mv{i}", [P, 2]) for i in range(2)]
    sd = [sb(f"sd{i}", [P, 1]) for i in range(2)]
    rs = [sb(f"rs{i}", [P, 1]) for i in range(2)]
    xT = [sb(f"xT{i}", [P, KD, P]) for i in range(2)]
    kv = [sb(f"kv{i}", [P, ROW]) for i in range(2)]
    qo = [sb(f"qo{i}", [P, 4, P]) for i in range(2)]
    pT = [ps(f"pT{i}", [P, KD, P]) for i in range(2)]
    pkv = [ps(f"pkv{i}", [P, 2 * D]) for i in range(2)]
    pq = [ps(f"pq{i}", [P, 4, P]) for i in range(2)]
    x_in = [sem(f"x_in{i}") for i in range(2)]
    stats_ok, mv_ok, sd_ok, rs_ok, x1_ok = sem("stats_ok"), sem("mv_ok"), sem("sd_ok"), sem("rs_ok"), sem("x1_ok")
    pT_ok, xT_ok, pkv_ok, pq_ok = sem("pT_ok"), sem("xT_ok"), sem("pkv_ok"), sem("pq_ok")
    kv_ok, qo_ok, ones_ok, x1_kept = sem("kv_ok"), sem("qo_ok"), sem("ones_ok"), sem("x1_kept")
    x1_seen = sem("x1_seen")
    kv_out = [sem(f"kv_out{i}") for i in range(2)]
    qo_out = [sem(f"qo_out{i}") for i in range(2)]
    dve_seen = sem("dve_seen")
    QD = 6

    with s.block() as block:
        @block.sync
        def _(sp):
            def load(t):
                wait(sp, x1_ok, t.n - 1)
                sp.dma_start(xin[t.slot][:], rows(a["x"], t.n * P, P)).then_inc(x_in[t.slot], 16)

            def store(t):
                sp.wait_ge(kv_ok, t.n + 1)
                sp.dma_start(rows(a["kvtab"], t.n * P, P), kv[t.slot][:]).then_inc(kv_out[t.slot], 16)
                sp.wait_ge(qo_ok, t.n + 1)
                for c in range(2):
                    sp.dma_start(a["qtab"][bass.ds(t.n * WPT, WPT), :, c, :].rearrange("w p n -> p w n"),
                                 qo[t.slot][:, c, :].rearrange("p (w n) -> p w n", n=WIN)).then_inc(qo_out[t.slot], 16)
                for c in range(2):
                    for hh in range(2):
                        sp.dma_start(a["qrtab"][bass.ds(t.n * WPT, WPT), :, 2 * c + hh, :].rearrange("w r n -> r w n"),
                                     qo[t.slot][hh * HD:(hh + 1) * HD, 2 + c, :].rearrange("p (w n) -> p w n", n=WIN)).then_inc(qo_out[t.slot], 16)

            load(Step(0, 0, 2))
            load(Step(0, 1, 2))

            def both(t):
                load(t + 2)
                store(t)
            walk(sp, 0, NT - 3, both, period=2)
            store(Step(0, NT - 2, 2))
            store(Step(0, NT - 1, 2))
            for i in range(2):
                n = (NT + 1 - i) // 2
                sp.wait_ge(kv_out[i], 16 * n)
                sp.wait_ge(qo_out[i], 16 * QD * n)

        @block.vector
        def _(v):
            for i in range(2):
                v.memset(kv[i][:, D:ROW], 1.0).then_inc(ones_ok, 1)
            v.wait_ge(ones_ok, 2)

            def norm(t):
                b = t.slot
                v.wait_ge(x_in[b], t.turn * 16 + 16)
                v.bn_stats(stats[b][:], xin[b][:]).then_inc(stats_ok, 1)
                v.wait_ge(stats_ok, t.n + 1)
                v.sem_inc(dve_seen, 1)
                v.bn_aggr(mv[b][:], stats[b][:]).then_inc(mv_ok, 1)
                v.wait_ge(sd_ok, t.n + 1)
                v.reciprocal(rs[b][:], sd[b][:]).then_inc(rs_ok, 1)
                v.wait_ge(rs_ok, t.n + 1)
                wait(v, pT_ok, t.n - 1)
                wait(v, x1_kept, t.n - 1)
                v.tensor_scalar(x1s[b][:], xin[b][:], mv[b][:, 0:1], rs[b][:, 0:1],
                                ALU.subtract, ALU.mult).then_inc(x1_ok, 1)

            def keep(t):
                b = t.slot
                v.wait_ge(pkv_ok, t.n + 1)
                wait_out = t.turn * 16
                wait(v, kv_out[b], wait_out)
                v.tensor_tensor(kv[b][:, 0:D], pkv[b][:, 0:D], g.ckv[:, 0:D], ALU.add)
                v.tensor_tensor(kv[b][:, D:ROW].rearrange("p (h e) -> p h e", e=VW)[:, :, 0:HD],
                                pkv[b][:, D:2 * D].rearrange("p (h d) -> p h d", d=HD),
                                g.ckv[:, D:2 * D].rearrange("p (h d) -> p h d", d=HD), ALU.add).then_inc(kv_ok, 1)

            norm(Step(0, 0, 2))

            def both(t):
                norm(t + 1)
                keep(t)
            walk(v, 0, NT - 2, both, period=2)
            keep(Step(0, NT - 1, 2))

        @block.gpsimd
        def _(pool):
            def keep(t):
                pool.wait_ge(x1_ok, t.n + 1)
                pool.sem_inc(x1_seen, 1)
                pool.tensor_copy(g.x1[:, bass.ds(t.n * D, D)], x1s[t.slot][:]).then_inc(x1_kept, 1)
            walk(pool, 0, NT - 1, keep, period=2)

        @block.scalar
        def _(act):
            def sd_of(t):
                act.wait_ge(mv_ok, t.n + 1)
                act.activation(sd[t.slot][:], mv[t.slot][:, 1:2], ACT.Sqrt, bias=g.eps[:, 0:1]).then_inc(sd_ok, 1)

            def xT_of(t):
                act.wait_ge(pT_ok, t.n + 1)
                wait(act, pq_ok, t.n - 1)
                act.activation(xT[t.slot][:], pT[t.slot][:], ACT.Copy).then_inc(xT_ok, 1)

            def q_of(t):
                b = t.slot
                act.wait_ge(pq_ok, t.n + 1)
                wait(act, qo_out[b], t.turn * (16 * QD))
                for c in range(2):
                    act.activation(qo[b][:, c, :], pq[b][:, c, :], ACT.Identity, bias=g.cq[:, c:c + 1])
                    last = act.activation(qo[b][:, 2 + c, :], pq[b][:, 2 + c, :], ACT.Identity, bias=g.cqr[:, c:c + 1])
                last.then_inc(qo_ok, 1)

            sd_of(Step(0, 0, 2))
            xT_of(Step(0, 0, 2))

            def body(t):
                sd_of(t + 1)
                xT_of(t + 1)
                q_of(t)
            walk(act, 0, NT - 2, body, period=2)
            q_of(Step(0, NT - 1, 2))

        @block.tensor
        def _(pe):
            def turn_x(t):
                pe.wait_ge(x1_ok, t.n + 1)
                wait(pe, xT_ok, t.n - 1)
                for c in range(KD):
                    last = nc.tensor.transpose(pT[t.slot][:, c, :], x1s[t.slot][:, c * P:(c + 1) * P], g.ident[:])
                last.then_inc(pT_ok, 1)

            def products(t):
                b = t.slot
                pe.wait_ge(xT_ok, t.n + 1)
                wait(pe, kv_ok, t.n - 1)
                for k in range(KD):
                    last = nc.tensor.matmul(pkv[b][:], xT[b][:, k, :], g.wkv[:, k, :], start=(k == 0), stop=(k == KD - 1))
                last.then_inc(pkv_ok, 1)
                wait(pe, qo_ok, t.n - 1)
                for m in range(4):
                    w = g.wq if m < 2 else g.wqr
                    for k in range(KD):
                        last = nc.tensor.matmul(pq[b][:, m, :], w[:, k, (m % 2) * P:(m % 2 + 1) * P], xT[b][:, k, :],
                                                start=(k == 0), stop=(k == KD - 1))
                last.then_inc(pq_ok, 1)

            turn_x(Step(0, 0, 2))

            def both(t):
                turn_x(t + 1)
                products(t)
            walk(pe, 0, NT - 2, both, period=2)
            products(Step(0, NT - 1, 2))


def edges(nc, a, g, s):
    sb, ps, sem = s.sb, s.ps, s.sem
    idx = [sb(f"idx{i}", [P, 1], I32) for i in range(4)]
    dt = [sb(f"dt{i}", [P, 2, P], I16) for i in range(4)]
    qb = [sb(f"qb{i}", [P, 3 * P]) for i in range(4)]
    qr = [sb(f"qr{i}", [N_REL, P]) for i in range(4)]
    kv = [sb(f"kv{i}", [P, ROW]) for i in range(4)]
    kT = [sb(f"kT{i}", [P, KD, P]) for i in range(2)]
    rel = [sb(f"rel{i}", [N_REL, P]) for i in range(2)]
    far = [sb(f"far{i}", [P, P]) for i in range(2)]
    msk = [sb(f"msk{i}", [P, P]) for i in range(2)]
    mx = [sb(f"mx{i}", [P, 1]) for i in range(2)]
    mn = [sb(f"mn{i}", [P, 1]) for i in range(2)]
    nb = [sb(f"nb{i}", [P, 1]) for i in range(2)]
    dm = [sb(f"dm{i}", [P, 1]) for i in range(2)]
    cor = [sb(f"cor{i}", [P, 1]) for i in range(4)]
    pr = [sb(f"pr{i}", [P, P]) for i in range(2)]
    prT = [sb(f"prT{i}", [P, P]) for i in range(2)]
    top = sb("top", [P, NWIN])
    pk = [ps(f"pk{i}", [P, KD, P]) for i in range(2)]
    psc = [ps(f"psc{i}", [P, P]) for i in range(2)]
    ppT = [ps(f"ppT{i}", [P, P]) for i in range(2)]
    pav = [ps(f"pav{i}", [P, VW]) for i in range(2)]
    idx_in = [sem(f"idx_in{i}") for i in range(4)]
    dt_in = [sem(f"dt_in{i}") for i in range(4)]
    q_in = [sem(f"q_in{i}") for i in range(4)]
    kv_in = [sem(f"kv_in{i}") for i in range(4)]
    (cleared, pool_seen, pk_ok, kT_ok, rel_ok, far_ok, sc_ok, msk_ok, mn_ok, nb_ok, dm_ok, top_ok,
     pr_ok, ppT_ok, prT_ok, av_ok, acc_ok, cor_ok) = (sem(x) for x in (
         "cleared", "pool_seen", "pk_ok", "kT_ok", "rel_ok", "far_ok", "sc_ok", "msk_ok", "mn_ok", "nb_ok", "dm_ok",
         "top_ok", "pr_ok", "ppT_ok", "prT_ok", "av_ok", "acc_ok", "cor_ok"))
    dve_seen = sem("dve_seen")
    LAST = STEPS - 1

    with s.block() as block:
        @block.sync
        def _(sp):
            sp.wait_ge(cleared, 4)

            def load(t):
                b = t.slot
                j = sp.value_load(g.jreg[0:1, bass.ds(t.n, 1)], min_val=0, max_val=ET - 1)
                w = sp.value_load(g.wreg[0:1, bass.ds(t.n, 1)], min_val=0, max_val=NWIN - 1)
                wait(sp, kv_in[b], t.turn * 16)
                sp.dma_start(idx[b][:], a["src2d"][bass.ds(j, 1), :].rearrange("o p -> p o")).then_inc(idx_in[b], 16)
                wait(sp, far_ok, t.n - 3)
                sp.dma_start(dt[b][:].rearrange("p k e -> p (k e)"),
                             a["dt16"][bass.ds(j, 1), :, :].rearrange("o k e -> o (k e)").to_broadcast([P, 2 * P])).then_inc(dt_in[b], 16)
                wait(sp, sc_ok, t.n - 3)
                for hh in range(2):
                    sp.dma_start(qb[b][hh * HD:(hh + 1) * HD, :].rearrange("p (c y) -> p c y", c=2)[:, :, hh * WIN:(hh + 1) * WIN],
                                 a["qtab"][bass.ds(w, 1), hh * HD:(hh + 1) * HD, :, :].rearrange("o p c n -> p (o c) n")).then_inc(q_in[b], 16)
                sp.dma_start(qr[b][:], a["qrtab"][bass.ds(w, 1), :, :, :].rearrange("o r h n -> r (o h n)")).then_inc(q_in[b], 16)
            walk(sp, 0, LAST, load)

        @block.gpsimd
        def _(pool):
            def gather(t):
                b = t.slot
                wait(pool, av_ok, t.n - 3)
                pool.sem_inc(pool_seen, 1)
                pool.wait_ge(idx_in[b], t.turn * 16 + 16)
                pool.sem_inc(pool_seen, 1)
                pool.indirect_dma_start(out=kv[b][:], out_offset=None, in_=a["kvtab"],
                                        in_offset=bass.IndirectOffsetOnAxis(ap=idx[b][:, 0:1], axis=0)).then_inc(kv_in[b], 16)
            walk(pool, 0, LAST, gather)

        @block.vector
        def _(v):
            for i in range(4):
                v.memset(qb[i][:], 0.0).then_inc(cleared, 1)
            v.memset(top[:], FLOOR).then_inc(top_ok, 1)
            v.memset(g.acc[:], 0.0).then_inc(acc_ok, 1)

            def masks(t):
                b, p = t.slot, t.par
                v.wait_ge(dt_in[b], t.turn * 16 + 16)
                wait(v, sc_ok, t.n - 1)
                v.tensor_scalar(rel[p][:], dt[b][0:N_REL, 1, :], g.rno[0:N_REL, 0:1], None, ALU.is_equal).then_inc(rel_ok, 1)
                v.tensor_scalar(far[p][:], dt[b][:, 0, :], g.nabs[:, bass.ds(t.n, 1)], FAR, ALU.not_equal, ALU.mult).then_inc(far_ok, 1)

            def maxima(t, w):
                p = t.par
                v.wait_ge(sc_ok, t.n + 1)
                v.wait_ge(far_ok, t.n + 1)
                wait(v, pr_ok, t.n - 1)
                v.sem_inc(dve_seen, 1)
                v.tensor_tensor_reduce(out=msk[p][:], in0=psc[p][:], in1=far[p][:], scale=1.0, scalar=FAR,
                                       op0=ALU.add, op1=ALU.max, accum_out=mx[p][:]).then_inc(msk_ok, 1)
                v.wait_ge(msk_ok, t.n + 1)
                v.wait_ge(top_ok, t.n + 1)
                v.tensor_tensor(mn[p][:], mx[p][:], top[:, bass.ds(w, 1)], ALU.max).then_inc(mn_ok, 1)
                v.wait_ge(mn_ok, t.n + 1)
                v.tensor_scalar(nb[p][:], mn[p][:], -SCALE, None, ALU.mult).then_inc(nb_ok, 1)
                wait(v, cor_ok, t.n - 1)
                v.tensor_tensor(dm[p][:], top[:, bass.ds(w, 1)], mn[p][:], ALU.subtract).then_inc(dm_ok, 1)
                v.wait_ge(dm_ok, t.n + 1)
                v.tensor_tensor(top[:, bass.ds(w, 1)], mx[p][:], top[:, bass.ds(w, 1)], ALU.max).then_inc(top_ok, 1)

            def add(t, w):
                p = t.par
                v.wait_ge(av_ok, t.n + 1)
                v.wait_ge(acc_ok, t.n + 1)
                v.wait_ge(cor_ok, t.n + 1)
                st = g.acc[:, bass.ds(w * VW, VW)]
                v.scalar_tensor_tensor(out=st, in0=st, scalar=cor[t.slot][:, 0:1], in1=pav[p][:], op0=ALU.mult, op1=ALU.add).then_inc(acc_ok, 1)

            def window(t):
                return v.value_load(g.wreg[0:1, bass.ds(t.n, 1)], min_val=0, max_val=NWIN - 1)

            masks(Step(0, 0))
            masks(Step(0, 1))
            maxima(Step(0, 0), window(Step(0, 0)))
            masks(Step(0, 2))
            maxima(Step(0, 1), window(Step(0, 1)))

            def body(t):
                masks(t + 1)
                maxima(t, window(t))
                add(t - 2, window(t - 2))
            walk(v, 2, LAST - 1, body)
            maxima(Step(0, LAST), window(Step(0, LAST)))
            for n in range(LAST - 2, LAST + 1):
                add(Step(0, n), window(Step(0, n)))

        @block.scalar
        def _(act):
            def k_of(t):
                act.wait_ge(pk_ok, t.n + 1)
                wait(act, sc_ok, t.n - 1)
                act.activation(kT[t.par][:], pk[t.par][:], ACT.Copy).then_inc(kT_ok, 1)

            def weights(t):
                p = t.par
                act.wait_ge(nb_ok, t.n + 1)
                wait(act, ppT_ok, t.n - 1)
                act.activation(pr[p][:], msk[p][:], ACT.Exp, bias=nb[p][:, 0:1], scale=SCALE).then_inc(pr_ok, 1)
                act.wait_ge(dm_ok, t.n + 1)
                wait(act, acc_ok, t.n - 2)
                act.activation(cor[t.slot][:], dm[p][:], ACT.Exp, scale=SCALE).then_inc(cor_ok, 1)

            def w_of(t):
                act.wait_ge(ppT_ok, t.n + 1)
                wait(act, av_ok, t.n - 1)
                act.activation(prT[t.par][:], ppT[t.par][:], ACT.Copy).then_inc(prT_ok, 1)

            k_of(Step(0, 0))
            k_of(Step(0, 1))
            weights(Step(0, 0))

            def body(t):
                k_of(t + 1)
                weights(t)
                w_of(t - 1)
            walk(act, 1, LAST - 1, body)
            weights(Step(0, LAST))
            w_of(Step(0, LAST - 1))
            w_of(Step(0, LAST))

        @block.tensor
        def _(pe):
            def turn_k(t):
                pe.wait_ge(kv_in[t.slot], t.turn * 16 + 16)
                wait(pe, kT_ok, t.n - 1)
                for c in range(KD):
                    last = nc.tensor.transpose(pk[t.par][:, c, :], kv[t.slot][:, c * P:(c + 1) * P], g.ident[:])
                last.then_inc(pk_ok, 1)

            def scores(t):
                b, p = t.slot, t.par
                pe.wait_ge(q_in[b], t.turn * 48 + 48)
                pe.wait_ge(rel_ok, t.n + 1)
                wait(pe, msk_ok, t.n - 1)
                nc.tensor.matmul(psc[p][:], qr[b][:], rel[p][:], start=True, stop=False)
                pe.wait_ge(kT_ok, t.n + 1)
                for c in range(KD):
                    last = nc.tensor.matmul(psc[p][:], qb[b][:, c * P:(c + 1) * P], kT[p][:, c, :], start=False, stop=(c == KD - 1))
                last.then_inc(sc_ok, 1)

            def turn_w(t):
                pe.wait_ge(pr_ok, t.n + 1)
                wait(pe, prT_ok, t.n - 1)
                nc.tensor.transpose(ppT[t.par][:], pr[t.par][:], g.ident[:]).then_inc(ppT_ok, 1)

            def sums(t):
                p = t.par
                pe.wait_ge(prT_ok, t.n + 1)
                wait(pe, acc_ok, t.n)
                for h in range(HEADS):
                    last = nc.tensor.matmul(pav[p][h * WIN:(h + 1) * WIN, :], prT[p][:, h * WIN:(h + 1) * WIN],
                                            kv[t.slot][:, D + h * VW:D + (h + 1) * VW], start=True, stop=True,
                                            tile_position=(0, h * WIN))
                last.then_inc(av_ok, 1)

            turn_k(Step(0, 0))
            turn_k(Step(0, 1))
            scores(Step(0, 0))
            turn_k(Step(0, 2))
            scores(Step(0, 1))
            turn_w(Step(0, 0))

            def body(t):
                turn_k(t + 1)
                scores(t)
                turn_w(t - 1)
                sums(t - 2)
            walk(pe, 2, LAST - 1, body)
            scores(Step(0, LAST))
            turn_w(Step(0, LAST - 1))
            sums(Step(0, LAST - 2))
            turn_w(Step(0, LAST))
            sums(Step(0, LAST - 1))
            sums(Step(0, LAST))


def post(nc, a, g, s):
    sb, ps, sem = s.sb, s.ps, s.sem
    two = range(2)
    xin = [sb(f"xin{i}", [P, D]) for i in two]
    vin = [sb(f"vin{i}", [P, WPT, HD]) for i in two]
    x1s = [sb(f"x1s{i}", [P, D]) for i in two]
    none = [sb(f"none{i}", [P, WPT]) for i in two]
    den = [sb(f"den{i}", [P, WPT]) for i in two]
    rden = [sb(f"rden{i}", [P, WPT]) for i in two]
    msg = [sb(f"msg{i}", [P, WPT, HD]) for i in two]
    alt = [sb(f"alt{i}", [P, WPT, HD]) for i in two]
    mT = [sb(f"mT{i}", [HD, HEADS, P]) for i in two]
    y = [sb(f"y{i}", [P, D]) for i in two]
    yn = [sb(f"yn{i}", [P, D]) for i in two]
    yg = [sb(f"yg{i}", [P, D]) for i in two]
    x2 = [sb(f"x2{i}", [P, D]) for i in two]
    z = [sb(f"z{i}", [P, D]) for i in two]
    zT = [sb(f"zT{i}", [P, KD, P]) for i in two]
    stats = [sb(f"stats{i}", [P, 6]) for i in two]
    mv = [sb(f"mv{i}", [P, 2]) for i in two]
    sd = [sb(f"sd{i}", [P, 1]) for i in two]
    rs = [sb(f"rs{i}", [P, 1]) for i in two]
    stats2 = [sb(f"stats2{i}", [P, 6]) for i in two]
    mv2 = [sb(f"mv2{i}", [P, 2]) for i in two]
    sd2 = [sb(f"sd2{i}", [P, 1]) for i in two]
    rs2 = [sb(f"rs2{i}", [P, 1]) for i in two]
    sd3 = [sb(f"sd3{i}", [P, 1]) for i in two]
    rs3 = [sb(f"rs3{i}", [P, 1]) for i in two]
    vz = [sb(f"vz{i}", [P, 1]) for i in two]
    lg = [sb(f"lg{i}", [P, E]) for i in two]
    t8 = [sb(f"t8{i}", [P, E]) for i in two]
    i8 = [sb(f"i8{i}", [P, E], U32) for i in two]
    pm = [ps(f"pm{i}", [P, 4, P]) for i in two]
    po = [ps(f"po{i}", [P, D]) for i in two]
    pz = [ps(f"pz{i}", [P, KD, P]) for i in two]
    pl = [ps(f"pl{i}", [P, E]) for i in two]
    x_in = [sem(f"x_in{i}") for i in two]
    x2_out = [sem(f"x2_out{i}") for i in two]
    names = ("none", "den", "rden", "msg", "alt", "mix", "pm", "mT", "po", "y", "yb", "stats", "mv", "sd", "rs", "yn", "yg",
             "yb2", "x2", "stats2", "mv2", "sd2", "rs2", "z", "vz", "sd3", "rs3", "xn", "pz", "zT", "pl", "lg", "t8", "i8", "keep", "x1s", "seen")
    o = {n: sem(n + "_ok") for n in names}
    dve_seen, pe_seen = sem("dve_seen"), sem("pe_seen")

    with s.block() as block:
        @block.sync
        def _(sp):
            def load(t):
                wait(sp, o["x2"], t.n - 1)
                sp.dma_start(xin[t.slot][:], rows(a["x"], t.n * P, P)).then_inc(x_in[t.slot], 16)
                wait(sp, o["alt"], t.n - 1)
                for h in range(HEADS):
                    sp.dma_start(vin[t.slot][h * WIN:(h + 1) * WIN, :, :],
                                 rows(a["kvtab"], t.n * P, P)[:, D + h * VW:D + h * VW + HD].rearrange("(w n) d -> n w d", n=WIN)).then_inc(x_in[t.slot], 16)

            def store(t):
                sp.wait_ge(o["x2"], t.n + 1)
                sp.dma_start(rows(a["x2tab"], t.n * P, P), x2[t.slot][:]).then_inc(x2_out[t.slot], 16)

            load(Step(0, 0, 2))
            load(Step(0, 1, 2))

            def both(t):
                load(t + 2)
                store(t)
            walk(sp, 0, NT - 3, both, period=2)
            store(Step(0, NT - 2, 2))
            store(Step(0, NT - 1, 2))
            for i in two:
                sp.wait_ge(x2_out[i], 16 * ((NT + 1 - i) // 2))

        @block.vector
        def _(v):
            def messages(t):
                b = t.slot
                st = g.acc[:, bass.ds(t.n * (WPT * VW), WPT * VW)].rearrange("p (w e) -> p w e", e=VW)
                v.tensor_scalar(none[b][:], st[:, :, HD], 0.0, None, ALU.is_equal).then_inc(o["none"], 1)
                v.wait_ge(o["none"], t.n + 1)
                v.tensor_tensor(den[b][:], st[:, :, HD], none[b][:], ALU.add).then_inc(o["den"], 1)
                v.wait_ge(o["den"], t.n + 1)
                v.reciprocal(rden[b][:], den[b][:]).then_inc(o["rden"], 1)
                v.wait_ge(x_in[b], t.turn * 80 + 80)
                v.tensor_tensor(alt[b][:], vin[b][:], none[b][:, :, None].to_broadcast([P, WPT, HD]), ALU.mult).then_inc(o["alt"], 1)
                v.wait_ge(o["rden"], t.n + 1)
                wait(v, o["pm"], t.n - 1)
                v.tensor_tensor(msg[b][:], st[:, :, 0:HD], rden[b][:, :, None].to_broadcast([P, WPT, HD]), ALU.mult).then_inc(o["msg"], 1)
                v.wait_ge(o["msg"], t.n + 1)
                v.wait_ge(o["alt"], t.n + 1)
                v.tensor_tensor(msg[b][:], msg[b][:], alt[b][:], ALU.add).then_inc(o["mix"], 1)

            def rest(t):
                b = t.slot
                n1 = t.n + 1
                v.wait_ge(o["po"], n1)
                v.tensor_tensor(y[b][:], po[b][:], g.x1[:, bass.ds(t.n * D, D)], ALU.add).then_inc(o["y"], 1)
                v.wait_ge(o["y"], n1)
                v.tensor_tensor(y[b][:], y[b][:], g.bo[:], ALU.add).then_inc(o["yb"], 1)
                v.wait_ge(o["yb"], n1)
                v.bn_stats(stats[b][:], y[b][:]).then_inc(o["stats"], 1)
                v.wait_ge(o["stats"], n1)
                v.sem_inc(dve_seen, 1)
                v.bn_aggr(mv[b][:], stats[b][:]).then_inc(o["mv"], 1)
                v.wait_ge(o["sd"], n1)
                v.reciprocal(rs[b][:], sd[b][:]).then_inc(o["rs"], 1)
                v.wait_ge(o["rs"], n1)
                v.tensor_scalar(yn[b][:], y[b][:], mv[b][:, 0:1], rs[b][:, 0:1], ALU.subtract, ALU.mult).then_inc(o["yn"], 1)
                v.wait_ge(o["x2"], n1)
                v.bn_stats(stats2[b][:], x2[b][:]).then_inc(o["stats2"], 1)
                v.wait_ge(o["stats2"], n1)
                v.sem_inc(dve_seen, 1)
                v.bn_aggr(mv2[b][:], stats2[b][:]).then_inc(o["mv2"], 1)
                v.wait_ge(o["sd2"], n1)
                v.reciprocal(rs2[b][:], sd2[b][:]).then_inc(o["rs2"], 1)
                v.wait_ge(o["rs2"], n1)
                wait(v, o["pz"], t.n - 1)
                v.tensor_scalar(z[b][:], x2[b][:], mv2[b][:, 0:1], rs2[b][:, 0:1], ALU.subtract, ALU.mult).then_inc(o["z"], 1)
                v.tensor_scalar(vz[b][:], mv2[b][:, 1:2], rs2[b][:, 0:1], rs2[b][:, 0:1], ALU.mult, ALU.mult).then_inc(o["vz"], 1)
                v.wait_ge(o["sd3"], n1)
                v.reciprocal(rs3[b][:], sd3[b][:]).then_inc(o["rs3"], 1)
                v.wait_ge(o["rs3"], n1)
                v.tensor_scalar(g.x1[:, bass.ds(t.n * D, D)], z[b][:], rs3[b][:, 0:1], None, ALU.mult).then_inc(o["xn"], 1)

            def top2(t):
                b = t.slot
                n1 = t.n + 1
                v.wait_ge(o["pl"], n1)
                v.tensor_tensor(lg[b][:], pl[b][:], g.br[:], ALU.add).then_inc(o["lg"], 1)
                v.wait_ge(o["lg"], n1)
                v.sem_inc(dve_seen, 1)
                v.max(t8[b][:], lg[b][:]).then_inc(o["t8"], 1)
                v.wait_ge(o["t8"], n1)
                v.sem_inc(dve_seen, 1)
                v.max_index(i8[b][:], t8[b][:], lg[b][:]).then_inc(o["i8"], 1)
                v.tensor_copy(g.top_l[:, bass.ds(t.n * 2, 2)], t8[b][:, 0:2])
                v.wait_ge(o["i8"], n1)
                v.tensor_copy(g.top_i[:, bass.ds(t.n * 2, 2)], i8[b][:, 0:2]).then_inc(o["keep"], 1)

            messages(Step(0, 0, 2))

            def body(t):
                messages(t + 1)
                rest(t)
                top2(t)
            walk(v, 0, NT - 2, body, period=2)
            rest(Step(0, NT - 1, 2))
            top2(Step(0, NT - 1, 2))

        @block.gpsimd
        def _(pool):
            def residual(t):
                b = t.slot
                n1 = t.n + 1
                pool.wait_ge(o["yn"], n1)
                pool.tensor_tensor(yg[b][:], yn[b][:], g.gamma[:], ALU.mult).then_inc(o["yg"], 1)
                pool.wait_ge(o["yg"], n1)
                pool.tensor_tensor(yg[b][:], yg[b][:], g.beta[:], ALU.add).then_inc(o["yb2"], 1)
                pool.wait_ge(o["yb2"], n1)
                pool.sem_inc(o["seen"], 1)
                wait(pool, x2_out[b], t.turn * 16)
                pool.sem_inc(o["seen"], 1)
                wait(pool, o["z"], t.n - 1)
                pool.tensor_tensor(x2[b][:], yg[b][:], xin[b][:], ALU.add).then_inc(o["x2"], 1)
            walk(pool, 0, NT - 1, residual, period=2)

        @block.scalar
        def _(act):
            def mT_of(t):
                act.wait_ge(o["pm"], t.n + 1)
                wait(act, o["po"], t.n - 1)
                act.activation(mT[t.slot][:].rearrange("d h (w n) -> d w h n", n=WIN),
                               pm[t.slot][0:HD, :, :].rearrange("d w (h n) -> d w h n", n=WIN), ACT.Copy).then_inc(o["mT"], 1)

            def body(t):
                b = t.slot
                n1 = t.n + 1
                act.wait_ge(o["mv"], n1)
                act.activation(sd[b][:], mv[b][:, 1:2], ACT.Sqrt, bias=g.eps[:, 0:1]).then_inc(o["sd"], 1)
                act.wait_ge(o["mv2"], n1)
                act.activation(sd2[b][:], mv2[b][:, 1:2], ACT.Sqrt, bias=g.eps[:, 0:1]).then_inc(o["sd2"], 1)
                act.wait_ge(o["vz"], n1)
                act.activation(sd3[b][:], vz[b][:], ACT.Sqrt, bias=g.eps[:, 0:1]).then_inc(o["sd3"], 1)
                act.wait_ge(o["pz"], n1)
                wait(act, o["pl"], t.n - 1)
                act.activation(zT[b][:], pz[b][:], ACT.Copy).then_inc(o["zT"], 1)

            mT_of(Step(0, 0, 2))

            def both(t):
                mT_of(t + 1)
                body(t)
            walk(act, 0, NT - 2, both, period=2)
            body(Step(0, NT - 1, 2))

        @block.tensor
        def _(pe):
            def out(t):
                b = t.slot
                pe.wait_ge(o["mix"], t.n + 1)
                wait(pe, o["mT"], t.n - 1)
                pe.sem_inc(pe_seen, 1)
                for w in range(WPT):
                    last = nc.tensor.transpose(pm[b][0:HD, w, :], msg[b][:, w, :], g.ident[:])
                last.then_inc(o["pm"], 1)
                pe.wait_ge(o["mT"], t.n + 1)
                wait(pe, o["y"], t.n - 1)
                for h in range(HEADS):
                    last = nc.tensor.matmul(po[b][:], mT[b][:, h, :], g.wo[:, h, :], start=(h == 0), stop=(h == HEADS - 1))
                last.then_inc(o["po"], 1)

            def router(t):
                b = t.slot
                pe.wait_ge(o["z"], t.n + 1)
                wait(pe, o["zT"], t.n - 1)
                for c in range(KD):
                    last = nc.tensor.transpose(pz[b][:, c, :], z[b][:, c * P:(c + 1) * P], g.ident[:])
                last.then_inc(o["pz"], 1)
                pe.wait_ge(o["zT"], t.n + 1)
                wait(pe, o["lg"], t.n - 1)
                for c in range(KD):
                    last = nc.tensor.matmul(pl[b][:], zT[b][:, c, :], g.wr[:, c, :], start=(c == 0), stop=(c == KD - 1))
                last.then_inc(o["pl"], 1)

            out(Step(0, 0, 2))

            def both(t):
                out(t + 1)
                router(t)
            walk(pe, 0, NT - 2, both, period=2)
            router(Step(0, NT - 1, 2))


def route(nc, a, g, s):
    sb, ps, sem = s.sb, s.ps, s.sem
    C = NT * E
    m1, m2, both_m = sb("m1", [P, NT, E]), sb("m2", [P, NT, E]), sb("both", [P, NT, E])
    tot, run, off = sb("tot", [P, NT, E]), sb("run", [P, NT, E]), sb("off", [P, NT, E])
    sel = sb("sel", [P, NT, E])
    one = sb("one", [P, NT])
    cnt, cnti, tiles_i = sb("cnt", [P, E]), sb("cnti", [P, E], I32), sb("tiles_i", [P, E], I32)
    tiles, cum, base = sb("tiles", [P, E]), sb("cum", [P, E]), sb("base", [P, E])
    posf = sb("posf", [P, 2, NT])
    eof = [sb(f"eof{i}", [P, MT]) for i in range(2)]
    dif = sb("dif", [P, NT])
    ex = sb("ex", [P, NT])
    row = [sb(f"row{i}", [P, D]) for i in range(4)]
    ix = [sb(f"ix{i}", [P, 2], I32) for i in range(4)]
    pin, ptot = ps("pin", [P, C]), ps("ptot", [P, C])
    chain, masks_ok, counts_ok, dif_ok, ex_ok = (sem(x) for x in ("chain", "masks_ok", "counts_ok", "dif_ok", "ex_ok"))
    row_ok, ix_ok, seen = sem("row_ok"), sem("ix_ok"), sem("seen")
    out = [sem(f"out{i}") for i in range(4)]

    with s.block() as block:
        @block.vector
        def _(v):
            done = [0]

            def link(ins):
                done[0] += 1
                ins.then_inc(chain, 1)
                v.wait_ge(chain, done[0])

            iota = g.iota8[:, None, :].to_broadcast([P, NT, E])
            choice = g.top_i[:].rearrange("p (t k) -> p k t", k=2)
            logit = g.top_l[:].rearrange("p (t k) -> p k t", k=2)
            v.tensor_tensor(dif[:], logit[:, 1, :], logit[:, 0, :], ALU.subtract).then_inc(dif_ok, 1)
            v.memset(one[:], 1.0)
            v.tensor_tensor(m1[:], iota, choice[:, 0, :, None].to_broadcast([P, NT, E]), ALU.is_equal)
            link(v.tensor_tensor(m2[:], iota, choice[:, 1, :, None].to_broadcast([P, NT, E]), ALU.is_equal))
            v.tensor_tensor(both_m[:], m1[:], m2[:], ALU.add).then_inc(masks_ok, 1)
            v.wait_ge(counts_ok, 1)
            link(v.tensor_copy(tot[:], ptot.rearrange("p (t e) -> p t e", e=E)))
            for e in range(E):
                last = v.tensor_tensor_scan(out=run[:, :, e], data0=one[:], data1=tot[:, :, e], initial=0.0, op0=ALU.mult, op1=ALU.add)
            link(last)
            link(v.tensor_copy(cnt[:], run[:, NT - 1, :]))
            link(v.tensor_tensor(run[:], run[:], tot[:], ALU.subtract))
            link(v.tensor_tensor(off[:], run[:], pin.rearrange("p (t e) -> p t e", e=E), ALU.add))
            link(v.tensor_scalar(cnti[:], cnt[:], float(P - 1), None, ALU.add))
            link(v.tensor_single_scalar(tiles_i[:], cnti[:], 7, ALU.arith_shift_right))
            link(v.tensor_copy(tiles[:], tiles_i[:]))
            link(v.tensor_tensor_scan(out=cum[:], data0=one[:, 0:E], data1=tiles[:], initial=0.0, op0=ALU.mult, op1=ALU.add))
            link(v.tensor_tensor(base[:], cum[:], tiles[:], ALU.subtract))
            link(v.tensor_scalar(base[:], base[:], float(P), None, ALU.mult))
            link(v.tensor_tensor(off[:], off[:], base[:, None, :].to_broadcast([P, NT, E]), ALU.add))
            for k, m in enumerate((m1, m2)):
                link(v.tensor_tensor(sel[:], m[:], off[:], ALU.mult))
                link(v.reduce_sum(posf[:, k, :], sel[:], AX.X))
            link(v.tensor_copy(g.pos[:].rearrange("p (t k) -> p k t", k=2), posf[:]))
            link(v.tensor_scalar(eof[0][:], g.tileno[:], cum[:, 0:1], None, ALU.is_ge))
            for e in range(1, E - 1):
                link(v.scalar_tensor_tensor(out=eof[e % 2][:], in0=g.tileno[:], scalar=cum[:, e:e + 1], in1=eof[(e + 1) % 2][:],
                                            op0=ALU.is_ge, op1=ALU.add))
            link(v.tensor_copy(g.expert[:], eof[(E - 2) % 2][:]))
            v.wait_ge(ex_ok, 1)
            link(v.tensor_scalar(dif[:], ex[:], 1.0, None, ALU.add))
            link(v.reciprocal(g.w1[:], dif[:]))
            link(v.tensor_tensor(g.w2[:], ex[:], g.w1[:], ALU.mult))

            def stage(t):
                b = t.slot
                wait(v, out[b], t.turn * 32)
                v.tensor_scalar(row[b][:], g.x1[:, bass.ds(t.n * D, D)], 1.0, None, ALU.mult).then_inc(row_ok, 1)
                v.tensor_scalar(ix[b][:], g.pos[:, bass.ds(t.n * 2, 2)], 1.0, None, ALU.mult).then_inc(ix_ok, 1)
            walk(v, 0, NT - 1, stage)

        @block.scalar
        def _(act):
            act.wait_ge(dif_ok, 1)
            act.activation(ex[:], dif[:], ACT.Exp).then_inc(ex_ok, 1)

        @block.tensor
        def _(pe):
            pe.wait_ge(masks_ok, 1)
            flat = both_m[:].rearrange("p t e -> p (t e)")
            nc.tensor.matmul(pin, g.tri[:], flat, start=True, stop=True)
            nc.tensor.matmul(ptot, g.ones[:], flat, start=True, stop=True).then_inc(counts_ok, 1)

        @block.gpsimd
        def _(pool):
            def scatter(t):
                b = t.slot
                pool.wait_ge(row_ok, t.n + 1)
                pool.sem_inc(seen, 1)
                pool.wait_ge(ix_ok, t.n + 1)
                pool.sem_inc(seen, 1)
                for k in range(2):
                    pool.indirect_dma_start(out=a["xs"], out_offset=bass.IndirectOffsetOnAxis(ap=ix[b][:, k:k + 1], axis=0),
                                            in_=row[b][:], in_offset=None).then_inc(out[b], 16)
            walk(pool, 0, NT - 1, scatter)
            for i in range(4):
                pool.wait_ge(out[i], 32 * ((NT + 3 - i) // 4))


def experts(nc, a, g, s):
    sb, ps, sem = s.sb, s.ps, s.sem
    two = range(2)
    w1 = sb("w1", [P, E * KD * H])
    w2 = sb("w2", [P, E * KH * D])
    pick = sb("pick", [P, E * P], BF16)
    b1s, b2s = sb("b1s", [P, H], BF16), sb("b2s", [P, D], BF16)
    xs = [sb(f"xs{i}", [P, D]) for i in two]
    gb = [sb(f"gb{i}", [P, 2 * KD]) for i in two]
    xT = [sb(f"xT{i}", [P, KD, P]) for i in two]
    h = [sb(f"h{i}", [P, H]) for i in two]
    hT = [sb(f"hT{i}", [P, KH, P]) for i in two]
    y = [sb(f"y{i}", [P, D]) for i in two]
    pieces = sb("pieces", [E, 3, H + D], BF16)
    left = [sb(f"left{i}", [E, H + D]) for i in two]
    whole = sb("whole", [E, H + D])
    px = ps("px", [P, KD, P])
    ph = [[ps(f"ph{i}{j}", [P, 512]) for j in two] for i in two]
    pt = [ps(f"pt{i}", [P, 4, P]) for i in two]
    py = ps("py", [P, D])
    w_in, cleared, chain, split_ok, pieces_in, pick_ok = (sem(x) for x in ("w_in", "cleared", "chain", "split_ok", "pieces_in", "pick_ok"))
    x_in = [sem(f"x_in{i}") for i in two]
    y_out = [sem(f"y_out{i}") for i in two]
    px_ok, xT_ok, ph_ok, h_ok, pt_ok0, pt_ok1, hT_ok0, hT_ok1, py_ok, y_ok = (sem(x) for x in (
        "px_ok", "xT_ok", "ph_ok", "h_ok", "pt_ok0", "pt_ok1", "hT_ok0", "hT_ok1", "py_ok", "y_ok"))

    with s.block() as block:
        @block.sync
        def _(sp):
            for e in range(E):
                sp.dma_start(w1[:, e * KD * H:(e + 1) * KD * H].rearrange("p (c n) -> p c n", c=KD),
                             a["W1"][e, :, :].rearrange("(c p) n -> p c n", p=P)).then_inc(w_in, 16)
                sp.dma_start(w2[:, e * KH * D:(e + 1) * KH * D].rearrange("p (c n) -> p c n", c=KH),
                             a["W2"][e, :, :].rearrange("(c p) n -> p c n", p=P)).then_inc(w_in, 16)
            sp.wait_ge(split_ok, 1)
            sp.wait_ge(cleared, 2)
            for k in range(3):
                sp.dma_start(b1s[k * E:(k + 1) * E, :], pieces[:, k, 0:H]).then_inc(pieces_in, 16)
                sp.dma_start(b2s[k * E:(k + 1) * E, :], pieces[:, k, H:H + D]).then_inc(pieces_in, 16)

            def load(t):
                e = sp.value_load(g.expert[0:1, bass.ds(t.n, 1)], min_val=0, max_val=E - 1)
                wait(sp, px_ok, t.n - 1)
                sp.dma_start(xs[t.slot][:], rows(a["xs"], t.n * P, P)).then_inc(x_in[t.slot], 16)
                wait(sp, xT_ok, t.n - 1)
                sp.dma_start(gb[t.slot][:], a["lngb"][bass.ds(e, 1), :, :].rearrange("o p k -> p (o k)")).then_inc(x_in[t.slot], 16)

            def store(t):
                sp.wait_ge(y_ok, t.n + 1)
                sp.dma_start(rows(a["ys"], t.n * P, P), y[t.slot][:]).then_inc(y_out[t.slot], 16)

            load(Step(0, 0, 2))
            load(Step(0, 1, 2))

            def both(t):
                load(t + 2)
                store(t)
            walk(sp, 0, MT - 3, both, period=2)
            store(Step(0, MT - 2, 2))
            store(Step(0, MT - 1, 2))
            for i in two:
                sp.wait_ge(y_out[i], 16 * ((MT + 1 - i) // 2))

        @block.gpsimd
        def _(pool):
            pool.memset(pick[:], 0.0).then_inc(pick_ok, 1)
            for k in range(3):
                pool.wait_ge(pick_ok, k + 1)
                pool.affine_select(out=pick[:].rearrange("p (e n) -> p e n", e=E), in_=pick[:].rearrange("p (e n) -> p e n", e=E),
                                   compare_op=ALU.not_equal, fill=1.0, base=-k * E, pattern=[[-1, E], [0, P]],
                                   channel_multiplier=1).then_inc(pick_ok, 1)

        @block.vector
        def _(v):
            v.memset(b1s[:], 0.0).then_inc(cleared, 1)
            v.memset(b2s[:], 0.0).then_inc(cleared, 1)
            done = [0]

            def link(ins):
                done[0] += 1
                ins.then_inc(chain, 1)
                v.wait_ge(chain, done[0])
            link(v.tensor_copy(whole[:, 0:H], g.b1f[:]))
            link(v.tensor_copy(whole[:, H:H + D], g.b2f[:]))
            rest = whole
            for k in range(3):
                last = v.tensor_copy(pieces[:, k, :], rest[:])
                if k < 2:
                    link(last)
                    link(v.tensor_tensor(left[k][:], rest[:], pieces[:, k, :], ALU.subtract))
                    rest = left[k]
            last.then_inc(split_ok, 1)

            def xT_of(t):
                b = t.slot
                v.wait_ge(x_in[b], t.turn * 32 + 32)
                v.wait_ge(px_ok, t.n + 1)
                wait(v, ph_ok, t.n - 1)
                for c in range(KD):
                    last = v.tensor_scalar(xT[b][:, c, :], px[:, c, :], gb[b][:, c:c + 1], gb[b][:, KD + c:KD + c + 1], ALU.mult, ALU.add)
                last.then_inc(xT_ok, 1)

            def hT_of(t):
                v.wait_ge(pt_ok0, t.n + 1)
                wait(v, py_ok, t.n - 1)
                v.tensor_copy(hT[t.slot][:, 0:4, :], pt[0][:]).then_inc(hT_ok0, 1)

            def y_of(t):
                b = t.slot
                v.wait_ge(py_ok, t.n + 1)
                wait(v, y_out[b], t.turn * 16)
                v.tensor_copy(y[b][:], py[:]).then_inc(y_ok, 1)

            xT_of(Step(0, 0, 2))
            xT_of(Step(0, 1, 2))

            def body(t):
                xT_of(t + 1)
                hT_of(t - 1)
                y_of(t - 1)
            walk(v, 1, MT - 2, body, period=2)
            for n in (MT - 2, MT - 1):
                hT_of(Step(0, n, 2))
                y_of(Step(0, n, 2))

        @block.scalar
        def _(act):
            def h_of(t):
                b = t.slot
                act.wait_ge(ph_ok, t.n + 1)
                wait(act, pt_ok1, t.n - 1)
                act.activation(h[b][:, 0:512], ph[b][0][:], ACT.Gelu)
                act.activation(h[b][:, 512:H], ph[b][1][:], ACT.Gelu).then_inc(h_ok, 1)

            def hT_of(t):
                act.wait_ge(pt_ok1, t.n + 1)
                wait(act, py_ok, t.n - 1)
                act.activation(hT[t.slot][:, 4:8, :], pt[1][:], ACT.Copy).then_inc(hT_ok1, 1)

            h_of(Step(0, 0, 2))

            def body(t):
                hT_of(t - 1)
                h_of(t)
            walk(act, 1, MT - 1, body, period=2)
            hT_of(Step(0, MT - 1, 2))

        @block.tensor
        def _(pe):
            def turn_x(t):
                pe.wait_ge(x_in[t.slot], t.turn * 32 + 32)
                wait(pe, xT_ok, t.n)
                for c in range(KD):
                    last = nc.tensor.transpose(px[:, c, :], xs[t.slot][:, c * P:(c + 1) * P], g.ident[:])
                last.then_inc(px_ok, 1)

            def hidden(t, e):
                b = t.slot
                pe.wait_ge(xT_ok, t.n + 1)
                wait(pe, h_ok, t.n - 1)
                for j in two:
                    nc.tensor.matmul(ph[b][j][:], pick[:, bass.ds(e * P, P)], b1s[:, j * 512:(j + 1) * 512], start=True, stop=False)
                    for c in range(KD):
                        last = nc.tensor.matmul(ph[b][j][:], xT[b][:, c, :], w1[:, bass.ds(e * (KD * H) + (c * H + j * 512), 512)],
                                                start=False, stop=(c == KD - 1))
                last.then_inc(ph_ok, 1)

            def back(t, e):
                b = t.slot
                pe.wait_ge(h_ok, t.n + 1)
                for j, (pt_ok, hT_ok) in enumerate(((pt_ok0, hT_ok0), (pt_ok1, hT_ok1))):
                    wait(pe, hT_ok, t.n)
                    for c in range(4):
                        last = nc.tensor.transpose(pt[j][:, c, :], h[b][:, (4 * j + c) * P:(4 * j + c + 1) * P], g.ident[:])
                    last.then_inc(pt_ok, 1)
                wait(pe, y_ok, t.n)
                nc.tensor.matmul(py[:], pick[:, bass.ds(e * P, P)], b2s[:], start=True, stop=False)
                for c in range(KH):
                    if c % 4 == 0:
                        pe.wait_ge((hT_ok0, hT_ok1)[c // 4], t.n + 1)
                    last = nc.tensor.matmul(py[:], hT[b][:, c, :], w2[:, bass.ds(e * (KH * D) + c * D, D)], start=False, stop=(c == KH - 1))
                last.then_inc(py_ok, 1)

            def expert(t):
                return pe.value_load(g.expert[0:1, bass.ds(t.n, 1)], min_val=0, max_val=E - 1)

            pe.wait_ge(w_in, 16 * 2 * E)
            pe.wait_ge(pick_ok, 4)
            pe.wait_ge(pieces_in, 16 * 6)
            turn_x(Step(0, 0, 2))
            turn_x(Step(0, 1, 2))
            hidden(Step(0, 0, 2), expert(Step(0, 0, 2)))

            def body(t):
                turn_x(t + 1)
                hidden(t, expert(t))
                back(t - 1, expert(t - 1))
            walk(pe, 1, MT - 2, body, period=2)
            hidden(Step(0, MT - 1, 2), expert(Step(0, MT - 1, 2)))
            back(Step(0, MT - 2, 2), expert(Step(0, MT - 2, 2)))
            back(Step(0, MT - 1, 2), expert(Step(0, MT - 1, 2)))


def combine(nc, a, g, s):
    sb, sem = s.sb, s.sem
    four = range(4)
    ix = [sb(f"ix{i}", [P, 2], I32) for i in four]
    y1 = [sb(f"y1{i}", [P, D]) for i in four]
    y2 = [sb(f"y2{i}", [P, D]) for i in four]
    x2 = [sb(f"x2{i}", [P, D]) for i in four]
    m = [sb(f"m{i}", [P, D]) for i in four]
    o = [sb(f"o{i}", [P, D]) for i in four]
    y_in = [sem(f"y_in{i}") for i in four]
    x_in = [sem(f"x_in{i}") for i in four]
    stored = [sem(f"stored{i}") for i in four]
    ix_ok, m_ok, o_ok, seen = sem("ix_ok"), sem("m_ok"), sem("o_ok"), sem("seen")

    with s.block() as block:
        @block.sync
        def _(sp):
            def load(t):
                wait(sp, m_ok, t.n - 3)
                sp.dma_start(x2[t.slot][:], rows(a["x2tab"], t.n * P, P)).then_inc(x_in[t.slot], 16)
            walk(sp, 0, NT - 1, load)

        @block.gpsimd
        def _(pool):
            def gather(t):
                b = t.slot
                wait(pool, o_ok, t.n - 3)
                pool.sem_inc(seen, 1)
                pool.wait_ge(ix_ok, t.n + 1)
                pool.sem_inc(seen, 1)
                for k, y in enumerate((y1, y2)):
                    pool.indirect_dma_start(out=y[b][:], out_offset=None, in_=a["ys"],
                                            in_offset=bass.IndirectOffsetOnAxis(ap=ix[b][:, k:k + 1], axis=0)).then_inc(y_in[b], 16)
            walk(pool, 0, NT - 1, gather)

        @block.vector
        def _(v):
            def index(t):
                wait(v, y_in[t.slot], t.turn * 32)
                v.tensor_scalar(ix[t.slot][:], g.pos[:, bass.ds(t.n * 2, 2)], 1.0, None, ALU.mult).then_inc(ix_ok, 1)

            def add(t):
                b = t.slot
                v.wait_ge(y_in[b], t.turn * 32 + 32)
                v.wait_ge(x_in[b], t.turn * 16 + 16)
                v.scalar_tensor_tensor(out=m[b][:], in0=y1[b][:], scalar=g.w1[:, bass.ds(t.n, 1)], in1=x2[b][:], op0=ALU.mult, op1=ALU.add).then_inc(m_ok, 1)
                v.wait_ge(m_ok, t.n + 1)
                wait(v, stored[b], t.turn * 16)
                v.scalar_tensor_tensor(out=o[b][:], in0=y2[b][:], scalar=g.w2[:, bass.ds(t.n, 1)], in1=m[b][:], op0=ALU.mult, op1=ALU.add).then_inc(o_ok, 1)

            for n in range(3):
                index(Step(0, n))

            def body(t):
                index(t + 3)
                add(t)
            walk(v, 0, NT - 4, body)
            for n in range(NT - 3, NT):
                add(Step(0, n))

        @block.scalar
        def _(act):
            def store(t):
                act.wait_ge(o_ok, t.n + 1)
                act.dma_start(rows(a["out"], t.n * P, P), o[t.slot][:]).then_inc(stored[t.slot], 16)
            walk(act, 0, NT - 1, store)
            for i in four:
                act.wait_ge(stored[i], 16 * ((NT + 3 - i) // 4))


class Kept:
    pass


def program(nc, a):
    with ExitStack() as whole:
        g = Kept()

        def buf(stack, name, shape, dt=F32):
            return stack.enter_context(nc.sbuf_tensor("g_" + name, shape, dt))

        g.gp = whole.enter_context(nc.semaphore("gp"))
        g.xs_clear = whole.enter_context(nc.semaphore("xs_clear"))
        g.ident = buf(whole, "ident", [P, P])
        g.tri = buf(whole, "tri", [P, P])
        g.ones = buf(whole, "ones", [P, P])
        g.eps = buf(whole, "eps", [P, 1])
        g.iota8 = buf(whole, "iota8", [P, E])
        g.rno = buf(whole, "rno", [P, 1])
        g.tileno = buf(whole, "tileno", [P, MT])
        g.bo = buf(whole, "bo", [P, D])
        g.gamma = buf(whole, "gamma", [P, D])
        g.beta = buf(whole, "beta", [P, D])
        g.br = buf(whole, "br", [P, E])
        g.wr = buf(whole, "wr", [P, KD, E])
        g.wo = buf(whole, "wo", [HD, HEADS, D])
        g.b1f = buf(whole, "b1f", [E, H])
        g.b2f = buf(whole, "b2f", [E, D])
        g.top_l = buf(whole, "top_l", [P, NT * 2])
        g.top_i = buf(whole, "top_i", [P, NT * 2])
        g.pos = buf(whole, "pos", [P, NT * 2])
        g.w1 = buf(whole, "w1", [P, NT])
        g.w2 = buf(whole, "w2", [P, NT])
        g.expert = buf(whole, "expert", [P, MT], I32)
        with ExitStack() as rows_kept:
            g.x1 = buf(rows_kept, "x1", [P, NT * D])
            with ExitStack() as graph:
                g.acc = buf(graph, "acc", [P, NWIN * VW])
                g.jreg = buf(graph, "jreg", [1, STEPS], I32)
                g.wreg = buf(graph, "wreg", [1, STEPS], I32)
                g.nabs = buf(graph, "nabs", [P, STEPS])
                with ExitStack() as proj:
                    g.wq = buf(proj, "wq", [P, KD, D])
                    g.wkv = buf(proj, "wkv", [P, KD, 2 * D])
                    g.wqr = buf(proj, "wqr", [P, KD, D])
                    g.cq = buf(proj, "cq", [P, 2])
                    g.cqr = buf(proj, "cqr", [P, 2])
                    g.ckv = buf(proj, "ckv", [P, 2 * D])
                    with Scope(nc, "setup") as s:
                        setup(nc, a, g, s)
                    with Scope(nc, "nodes") as s:
                        nodes(nc, a, g, s)
                with Scope(nc, "edges") as s:
                    edges(nc, a, g, s)
                with Scope(nc, "post") as s:
                    post(nc, a, g, s)
            with Scope(nc, "route") as s:
                route(nc, a, g, s)
        with Scope(nc, "experts") as s:
            experts(nc, a, g, s)
        with Scope(nc, "combine") as s:
            combine(nc, a, g, s)


def kernel(**inputs):
    import concourse.bacc as bacc
    from concourse.bass_utils import run_bass_kernel_spmd as run

    nc = bacc.Bacc("TRN2", target_bir_lowering=False, num_devices=1)
    raw = {k: np.asarray(v) for k, v in inputs.items()}

    def padded(v, n, fill):
        out = np.full((n,) + v.shape[1:], fill, v.dtype)
        out[:len(v)] = v
        return out

    dst = padded(raw["dst"], ET_PAD * P, PAD_DST)
    ins = {
        "x": padded(raw["x"], NPAD, 0),
        "src2d": padded(raw["src"], ET_PAD * P, 0).reshape(ET_PAD, P),
        "dst2d": dst.reshape(ET_PAD, P),
        "et2d": padded(raw["edge_type_64"], ET_PAD * P, 0).reshape(ET_PAD, P),
        "first": dst[P:ET * P:P],
        "q_emb": raw["L0_gnn_query_emb"].reshape(KD, P).T,
        "bq": raw["L0_gnn_bq"].reshape(KD, P).T,
        "WqT": raw["L0_gnn_Wq"].T,
        "relT": raw["L0_gnn_rel_w"].T,
    }
    for name in ("Wq", "Wk", "bk", "Wv", "bv", "Wo", "bo", "gamma", "beta"):
        ins[name] = raw["L0_gnn_" + name]
    for name in ("Wr", "br", "W1", "b1", "W2", "b2"):
        ins[name] = raw["L0_ffn_" + name]
    ins["lngb"] = np.stack([raw["L0_ffn_ln_g"], raw["L0_ffn_ln_b"]], 1).reshape(E, 2 * KD, P).transpose(0, 2, 1)
    ins = {k: np.ascontiguousarray(v) for k, v in ins.items()}
    a = {k: nc.dram_tensor(k, v.shape, mybir.dt.from_np(v.dtype), kind="ExternalInput").ap() for k, v in ins.items()}
    a["out"] = nc.dram_tensor("out", (NPAD, D), F32, kind="ExternalOutput").ap()
    for name, shape, dt in (("kvtab", (NPAD, ROW), F32), ("qtab", (NWIN, P, 2, WIN), F32), ("qrtab", (NWIN, N_REL, HEADS, WIN), F32),
                            ("dt16", (ET_PAD, 2, P), I16), ("jtab", (STEPS_PAD,), I32), ("wtab", (STEPS_PAD,), I32),
                            ("x2tab", (NPAD, D), F32), ("xs", (MT * P, D), F32), ("ys", (MT * P, D), F32)):
        a[name] = nc.dram_tensor(name, shape, dt, kind="Internal").ap()
    program(nc, a)
    r = run(nc, [ins], core_ids=[0])
    return r.results[0]["out"][:N_NODES]
```

```python
import numpy as np
import concourse.bass as bass
from concourse import mybir
from contextlib import ExitStack

F32 = mybir.dt.float32
BF16 = mybir.dt.bfloat16
I32 = mybir.dt.int32
I16 = mybir.dt.int16
U32 = mybir.dt.uint32
ALU = mybir.AluOpType
ACT = mybir.ActivationFunctionType
AX = mybir.AxisListType

P = 128
N_NODES, N_EDGES = 6250, 100000
D = 256
HEADS, HD = 4, 64
N_REL = 64
NT = -(-N_NODES // P)
NPAD = NT * P
WIN = 32
NWIN = NPAD // WIN
WPT = P // WIN
ET = -(-N_EDGES // P) + 1
ET_PAD = -(-ET // P) * P
STEPS = ET + NWIN - 1
STEPS_PAD = -(-STEPS // P) * P
PAD_DST = NPAD - 1
VW = HD + 1
ROW = D + HEADS * VW
QREC = 2 * P
FAR = 1.0e30
FLOOR = 1.0e20
SCALE = 1.0 / HD ** 0.5
SPC = STEPS_PAD // P
EPS = 1e-5
E, H = 8, 1024
KD, KH = D // P, H // P
MT = (2 * NPAD + E * (P - 1)) // P


def wait(eng, sem, value):
    if not (isinstance(value, int) and value <= 0):
        eng.wait_ge(sem, value)


class Step:

    def __init__(self, turn, at, period=4):
        self.period = period
        self.turn = turn + at // period
        self.slot = at % period
        self.n = turn * period + at
        self.par = self.slot % 2
        self.base, self.at = turn, at

    @property
    def quad(self):
        return 2 * self.turn + self.slot // 4

    def __add__(self, k):
        return Step(self.base, self.at + k, self.period)

    def __sub__(self, k):
        return self + (-k)


def walk(eng, first, last, body, period=4, head=1):
    start = head
    lead = start * period + first
    turns = (last + 1 - lead) // period
    if turns < 2:
        for n in range(first, last + 1):
            body(Step(0, n, period))
        return
    for n in range(first, lead):
        body(Step(0, n, period))
    with eng.Fori(start, start + turns) as turn:
        for k in range(period):
            body(Step(turn, first + k, period))
    for n in range(lead + turns * period, last + 1):
        body(Step(0, n, period))


class Scope:

    def __init__(self, nc, tag):
        self.nc, self.tag, self.stack, self.sems = nc, tag, ExitStack(), []

    def __enter__(self):
        self.stack.__enter__()
        return self

    def __exit__(self, *a):
        self.nc.clear_and_free_semaphores(self.sems)
        self.nc.all_engine_barrier()
        return self.stack.__exit__(*a)

    def sb(self, name, shape, dt=F32):
        return self.stack.enter_context(self.nc.sbuf_tensor(f"{self.tag}_{name}", shape, dt))

    def ps(self, name, shape):
        bank = self.stack.enter_context(self.nc.psum_tensor(f"{self.tag}_{name}", [P, 512], F32))
        if len(shape) == 2:
            return bank[:, 0:shape[1]]
        return bank[:, 0:shape[1] * shape[2]].rearrange("p (a b) -> p a b", a=shape[1])

    def sem(self, name):
        self.sems.append(self.nc.alloc_semaphore(f"{self.tag}_{name}"))
        return self.sems[-1]

    def block(self):
        return self.nc.Block()


def rows(ap, first, count):
    return ap[bass.ds(first, count), :]


def setup(nc, a, g, s):
    sb, ps, sem = s.sb, s.ps, s.sem
    relt2 = sb("relt2", [P, P])
    wqt = sb("wqt", [P, KD, D])
    wqp = sb("wqp", [P, KD, D])
    qcol = sb("qcol", [P, KD])
    qwide = sb("qwide", [P, KD, P])
    bqc = sb("bqc", [P, 2 * KD])
    bkv = sb("bkv", [P, 2 * D])
    cq = sb("cq", [P, 2 * KD])
    first = sb("first", [P, ET - 1], I32)
    firstw = sb("firstw", [P, ET - 1], I32)
    key = sb("key", [P, ET - 1])
    keyj = sb("keyj", [P, ET - 1])
    hit = sb("hit", [P, STEPS])
    sno = sb("sno", [P, SPC])
    wno = sb("wno", [P, 2])
    jf = sb("jf", [P, SPC])
    ji = sb("ji", [P, SPC], I32)
    wi = sb("wi", [P, SPC], I32)
    wrow = sb("wrow", [P, STEPS], I32)
    wf = sb("wf", [P, STEPS])
    lastf = sb("lastf", [P, 2])
    lasti = sb("lasti", [P, 2], I32)
    pno, noi, rmi = sb("pno", [P, 1], I32), sb("noi", [P, 1], I32), sb("rmi", [P, 1], I32)
    nof = sb("nof", [P, 1])
    rec = sb("rec", [P, SPC, 3 * P], I32)
    rec16 = sb("rec16", [P, SPC, 2 * P], I16)
    srcf = sb("srcf", [P, SPC, P])
    zero = sb("zero", [P, D])
    pw = ps("pw", [P, 4, P])
    pc = ps("pc", [P, 8])
    pr = ps("pr", [P, 2 * D])
    pidx = [ps(f"pidx{i}", [P, 4, P]) for i in range(2)]
    loaded, first_in, made, zeroed = sem("loaded"), sem("first_in"), sem("made"), sem("zeroed")
    tables_out, tables_in, last_out = sem("tables_out"), sem("tables_in"), sem("last_out")
    recs_in, dt_out, src_ok, r16_ok, pidx_ok = sem("recs_in"), sem("dt_out"), sem("src_ok"), sem("r16_ok"), sem("pidx_ok")
    pe_done, chain, last_ok = sem("pe_done"), sem("chain"), sem("last_ok")
    LOADS = 19
    CH = 15

    with s.block() as block:
        @block.sync
        def _(sp):
            load = lambda dst, src: sp.dma_start(dst, src).then_inc(loaded, 16)
            spread = lambda v: v.rearrange("(o n) -> o n", o=1).to_broadcast([P, v.shape[0]])
            sp.dma_start(first[:], spread(a["first"])).then_inc(first_in, 16)
            sp.wait_ge(zeroed, 1)
            for c in range(2):
                load(relt2[c * HD:(c + 1) * HD, c * N_REL:(c + 1) * N_REL], a["relT"])
            load(wqt[:], a["WqT"].rearrange("(c p) k -> p c k", p=P))
            load(wqp[:], a["WqP"].rearrange("(c p) n -> p c n", p=P))
            load(g.wq[:], a["Wq"].rearrange("(c p) n -> p c n", p=P))
            load(g.wkv[:, :, 0:D], a["Wk"].rearrange("(c p) n -> p c n", p=P))
            load(g.wkv[:, :, D:2 * D], a["Wv"].rearrange("(c p) n -> p c n", p=P))
            load(qcol[:], a["q_emb"])
            load(bqc[:], a["bq"])
            load(bkv[:, 0:D], spread(a["bk"]))
            load(bkv[:, D:2 * D], spread(a["bv"]))
            load(g.wo[:], a["Wo"].rearrange("(h p) n -> p h n", p=HD))
            load(g.bo[:], spread(a["bo"]))
            load(g.gamma[:], spread(a["gamma"]))
            load(g.beta[:], spread(a["beta"]))
            load(g.br[:], spread(a["br"]))
            load(g.wr[:], a["Wr"].rearrange("(c p) n -> p c n", p=P))
            load(g.b1f[:], a["b1"])
            load(g.b2f[:], a["b2"])
            sp.wait_ge(made, 2)
            sp.dma_start(a["wtab"].rearrange("(p c) -> p c", p=P), wi[:]).then_inc(tables_out, 16)
            sp.wait_ge(tables_out, 16)
            sp.dma_start(wrow[:], spread(a["wtab"][0:STEPS])).then_inc(tables_in, 16)
            sp.dma_start(g.wreg[0:1, :], a["wtab"].rearrange("(o n) -> o n", o=1)).then_inc(tables_in, 16)
            sp.wait_ge(last_ok, 1)
            sp.dma_start(a["lasttab"].rearrange("(p c) -> p c", p=P), lasti[:]).then_inc(last_out, 16)
            sp.wait_ge(last_out, 16)
            sp.dma_start(g.lastreg[0:1, :], a["lasttab"][0:NWIN].rearrange("(o n) -> o n", o=1)).then_inc(tables_in, 16)
            sp.wait_ge(r16_ok, 1)
            sp.dma_start(a["dts"].rearrange("(p c) k -> p (c k)", p=P), rec16[:].rearrange("p c k -> p (c k)")).then_inc(dt_out, 16)
            sp.wait_ge(dt_out, 16)
            sp.wait_ge(tables_in, 48)

        @block.gpsimd
        def _(pool):
            made_of = [0]

            def link(ins):
                made_of[0] += 1
                ins.then_inc(g.gp, 1)
                pool.wait_ge(g.gp, made_of[0])
            imprecise = dict(allow_small_or_imprecise_dtypes=True)
            link(pool.iota(sno[:], pattern=[[1, SPC]], base=0, channel_multiplier=SPC, **imprecise))
            link(pool.iota(keyj[:], pattern=[[1, ET - 1]], base=1, channel_multiplier=0, **imprecise))
            link(pool.iota(wno[:], pattern=[[1, 2]], base=0, channel_multiplier=2, **imprecise))
            link(pool.iota(pno[:], pattern=[[0, 1]], base=0, channel_multiplier=1))
            link(pool.iota(g.tileno[:], pattern=[[1, MT]], base=0, channel_multiplier=0, **imprecise))
            link(pool.iota(g.iota8[:], pattern=[[1, E]], base=0, channel_multiplier=0, **imprecise))
            link(pool.memset(g.ident[:], 0.0))
            link(pool.memset(g.tri[:], 1.0))
            link(pool.affine_select(out=g.ident[:], in_=g.ident[:], compare_op=ALU.not_equal, fill=1.0, base=0,
                                    pattern=[[-1, P]], channel_multiplier=1))
            link(pool.affine_select(out=g.tri[:], in_=g.tri[:], compare_op=ALU.is_gt, fill=0.0, base=0,
                                    pattern=[[1, P]], channel_multiplier=-1))
            pool.wait_ge(made, 1)
            for c in range(SPC):
                pool.indirect_dma_start(out=rec[:, c, :], out_offset=None, in_=a["edges"],
                                        in_offset=bass.IndirectOffsetOnAxis(ap=ji[:, c:c + 1], axis=0)).then_inc(recs_in, 16)

        @block.vector
        def _(v):
            v.memset(relt2[:], 0.0).then_inc(zeroed, 1)
            v.memset(zero[:], 0.0).then_inc(zeroed, 1)
            v.memset(g.ones[:], 1.0).then_inc(zeroed, 1)
            v.memset(g.eps[:], EPS).then_inc(zeroed, 1)
            done = [0]

            def link(ins):
                done[0] += 1
                ins.then_inc(chain, 1)
                v.wait_ge(chain, done[0])
            v.wait_ge(first_in, 16)
            v.wait_ge(g.gp, 10)
            link(v.tensor_single_scalar(firstw[:], first[:], 5, ALU.arith_shift_right))
            link(v.tensor_tensor(key[:], firstw[:], keyj[:], ALU.add))
            for c in range(SPC):
                link(v.tensor_scalar(hit[:, 0:ET - 1], key[:], sno[:, c:c + 1], 0.0, ALU.is_le, ALU.add, accum_out=jf[:, c:c + 1]))
            v.tensor_copy(ji[:], jf[:]).then_inc(made, 1)
            v.tensor_tensor(wi[:], sno[:], jf[:], ALU.subtract).then_inc(made, 1)
            link(v.tensor_single_scalar(noi[:], pno[:], WIN - 1, ALU.bitwise_and))
            link(v.tensor_single_scalar(rmi[:], pno[:], N_REL - 1, ALU.bitwise_and))
            link(v.tensor_copy(nof[:], noi[:]))
            link(v.tensor_copy(g.rmod[:], rmi[:]))
            v.wait_ge(loaded, 16 * LOADS)
            v.wait_ge(zeroed, 4)
            v.tensor_scalar(relt2[:], relt2[:], 0.2, None, ALU.mult).then_inc(zeroed, 1)
            for c in range(KD):
                v.tensor_scalar(qwide[:, c, :], g.ones[:], qcol[:, c:c + 1], 0.1, ALU.mult, ALU.mult).then_inc(zeroed, 1)
            v.wait_ge(pe_done, 1)
            link(v.tensor_copy(g.wqr[:].rearrange("p k (c n) -> p k c n", c=2),
                               pw[:].rearrange("p (k c) n -> p k c n", c=2)))
            v.wait_ge(pe_done, 2)
            link(v.tensor_tensor(cq[:], pc[:, 0:4], bqc[:], ALU.add))
            v.tensor_scalar(g.ncq[:], cq[:, 0:2], -SCALE, None, ALU.mult).then_inc(made, 1)
            link(v.tensor_tensor(g.ckv[:], pr[:], bkv[:], ALU.add))
            v.wait_ge(pe_done, 3)
            link(v.tensor_scalar(g.ncqr[:], pc[:, 4:6], -SCALE, None, ALU.mult))
            v.wait_ge(tables_in, 32)
            link(v.tensor_scalar(g.nabs[:], wrow[:], float(WIN), nof[:, 0:1], ALU.mult, ALU.add))
            link(v.tensor_copy(wf[:], wrow[:]))
            link(v.tensor_tensor(hit[:, 1:STEPS], wf[:, 1:STEPS], wf[:, 0:STEPS - 1], ALU.not_equal))
            link(v.tensor_scalar(g.fresh[:, 1:STEPS], hit[:, 1:STEPS], FAR, None, ALU.mult))
            link(v.memset(g.fresh[:, 0:1], FAR))
            for c in range(2):
                link(v.tensor_scalar(hit[:], wf[:], wno[:, c:c + 1], -1.0, ALU.is_le, ALU.add, accum_out=lastf[:, c:c + 1]))
            v.tensor_copy(lasti[:], lastf[:]).then_inc(last_ok, 1)
            v.wait_ge(recs_in, 16 * SPC)
            v.tensor_copy(srcf[:], rec[:, :, 0:P]).then_inc(src_ok, 1)
            v.tensor_copy(rec16[:], rec[:, :, P:3 * P]).then_inc(r16_ok, 1)
            for i in range(2):
                v.wait_ge(pidx_ok, i + 1)
                v.tensor_copy(g.idx[:].rearrange("e (p c) -> e c p", c=SPC)[:, 4 * i:4 * i + 4, :], pidx[i])

        @block.tensor
        def _(pe):
            pe.wait_ge(zeroed, 7)
            for k in range(KD):
                for c in range(2):
                    last = nc.tensor.matmul(pw[:, 2 * k + c, :], wqt[:, c, k * P:(k + 1) * P], relt2[:], start=True, stop=True)
            last.then_inc(pe_done, 1)
            for c in range(4):
                for k in range(KD):
                    w = g.wq if c < 2 else wqp
                    last = nc.tensor.matmul(pc[:, c:c + 1], w[:, k, (c % 2) * P:(c % 2 + 1) * P], qwide[:, k, 0:1],
                                            start=(k == 0), stop=(k == KD - 1))
            for k in range(KD):
                last = nc.tensor.matmul(pr[:], qwide[:, k, :], g.wkv[:, k, :], start=(k == 0), stop=(k == KD - 1))
            last.then_inc(pe_done, 1)
            pe.wait_ge(made, 3)
            for c in range(2):
                last = nc.tensor.matmul(pc[:, 4 + c:5 + c], relt2[:], cq[:, 2 + c:3 + c], start=True, stop=True)
            last.then_inc(pe_done, 1)
            pe.wait_ge(src_ok, 1)
            for c in range(SPC):
                last = nc.tensor.transpose(pidx[c // 4][:, c % 4, :], srcf[:, c, :], g.ident[:])
                if c % 4 == 3:
                    last.then_inc(pidx_ok, 1)

        @block.scalar
        def _(act):
            act.wait_ge(zeroed, 2)
            xs = a["xs"].rearrange("(t p) d -> p t d", p=P)
            for t in range(0, MT, CH):
                n = min(CH, MT - t)
                act.dma_start(xs[:, t:t + n, :], zero[:, None, :].to_broadcast([P, n, D])).then_inc(g.xs_clear, 16)
            act.wait_ge(g.xs_clear, 16 * (-(-MT // CH)))


def nodes(nc, a, g, s):
    sb, ps, sem = s.sb, s.ps, s.sem
    xin = [sb(f"xin{i}", [P, D]) for i in range(2)]
    x1s = [sb(f"x1s{i}", [P, D]) for i in range(2)]
    stats = [sb(f"stats{i}", [P, 6]) for i in range(2)]
    mv = [sb(f"mv{i}", [P, 2]) for i in range(2)]
    sd = [sb(f"sd{i}", [P, 1]) for i in range(2)]
    rs = [sb(f"rs{i}", [P, 1]) for i in range(2)]
    xT = [sb(f"xT{i}", [P, KD, P]) for i in range(2)]
    kv = [sb(f"kv{i}", [P, ROW]) for i in range(2)]
    qo = [sb(f"qo{i}", [P, WPT, QREC]) for i in range(2)]
    pT = [ps(f"pT{i}", [P, KD, P]) for i in range(2)]
    pkv = [ps(f"pkv{i}", [P, 2 * D]) for i in range(2)]
    pq = [ps(f"pq{i}", [P, 4, P]) for i in range(2)]
    x_in = [sem(f"x_in{i}") for i in range(2)]
    stats_ok, mv_ok, sd_ok, rs_ok, x1_ok = sem("stats_ok"), sem("mv_ok"), sem("sd_ok"), sem("rs_ok"), sem("x1_ok")
    pT_ok, xT_ok, pkv_ok, pq_ok = sem("pT_ok"), sem("xT_ok"), sem("pkv_ok"), sem("pq_ok")
    kv_ok, qo_ok, ones_ok, x1_kept = sem("kv_ok"), sem("qo_ok"), sem("ones_ok"), sem("x1_kept")
    x1_seen = sem("x1_seen")
    kv_out = [sem(f"kv_out{i}") for i in range(2)]
    qo_out = [sem(f"qo_out{i}") for i in range(2)]
    dve_seen = sem("dve_seen")

    with s.block() as block:
        @block.sync
        def _(sp):
            def load(t):
                wait(sp, x1_ok, t.n - 1)
                sp.dma_start(xin[t.slot][:], rows(a["x"], t.n * P, P)).then_inc(x_in[t.slot], 16)

            def store(t):
                sp.wait_ge(kv_ok, t.n + 1)
                sp.dma_start(rows(a["kvtab"], t.n * P, P), kv[t.slot][:]).then_inc(kv_out[t.slot], 16)
                sp.wait_ge(qo_ok, t.n + 1)
                sp.dma_start(a["qtab"][bass.ds(t.n * WPT, WPT), :, :].rearrange("w p n -> p w n"), qo[t.slot][:]).then_inc(qo_out[t.slot], 16)

            load(Step(0, 0, 2))
            load(Step(0, 1, 2))

            def both(t):
                load(t + 2)
                store(t)
            walk(sp, 0, NT - 3, both, period=2)
            store(Step(0, NT - 2, 2))
            store(Step(0, NT - 1, 2))
            for i in range(2):
                n = (NT + 1 - i) // 2
                sp.wait_ge(kv_out[i], 16 * n)
                sp.wait_ge(qo_out[i], 16 * n)

        @block.vector
        def _(v):
            for i in range(2):
                v.memset(kv[i][:, D:ROW], 1.0).then_inc(ones_ok, 1)
                v.memset(qo[i][:], 0.0).then_inc(ones_ok, 1)
            v.wait_ge(ones_ok, 4)

            def norm(t):
                b = t.slot
                v.wait_ge(x_in[b], t.turn * 16 + 16)
                v.bn_stats(stats[b][:], xin[b][:]).then_inc(stats_ok, 1)
                v.wait_ge(stats_ok, t.n + 1)
                v.sem_inc(dve_seen, 1)
                v.bn_aggr(mv[b][:], stats[b][:]).then_inc(mv_ok, 1)
                v.wait_ge(sd_ok, t.n + 1)
                v.reciprocal(rs[b][:], sd[b][:]).then_inc(rs_ok, 1)
                v.wait_ge(rs_ok, t.n + 1)
                wait(v, pT_ok, t.n - 1)
                wait(v, x1_kept, t.n - 1)
                v.tensor_scalar(x1s[b][:], xin[b][:], mv[b][:, 0:1], rs[b][:, 0:1],
                                ALU.subtract, ALU.mult).then_inc(x1_ok, 1)

            def keep(t):
                b = t.slot
                v.wait_ge(pkv_ok, t.n + 1)
                wait_out = t.turn * 16
                wait(v, kv_out[b], wait_out)
                v.tensor_tensor(kv[b][:, 0:D], pkv[b][:, 0:D], g.ckv[:, 0:D], ALU.add)
                v.tensor_tensor(kv[b][:, D:ROW].rearrange("p (h e) -> p h e", e=VW)[:, :, 0:HD],
                                pkv[b][:, D:2 * D].rearrange("p (h d) -> p h d", d=HD),
                                g.ckv[:, D:2 * D].rearrange("p (h d) -> p h d", d=HD), ALU.add).then_inc(kv_ok, 1)

            norm(Step(0, 0, 2))

            def both(t):
                norm(t + 1)
                keep(t)
            walk(v, 0, NT - 2, both, period=2)
            keep(Step(0, NT - 1, 2))

        @block.gpsimd
        def _(pool):
            def keep(t):
                pool.wait_ge(x1_ok, t.n + 1)
                pool.sem_inc(x1_seen, 1)
                pool.tensor_copy(g.x1[:, bass.ds(t.n * D, D)], x1s[t.slot][:]).then_inc(x1_kept, 1)
            walk(pool, 0, NT - 1, keep, period=2)

        @block.scalar
        def _(act):
            def sd_of(t):
                act.wait_ge(mv_ok, t.n + 1)
                act.activation(sd[t.slot][:], mv[t.slot][:, 1:2], ACT.Sqrt, bias=g.eps[:, 0:1]).then_inc(sd_ok, 1)

            def xT_of(t):
                act.wait_ge(pT_ok, t.n + 1)
                wait(act, pq_ok, t.n - 1)
                act.activation(xT[t.slot][:], pT[t.slot][:], ACT.Copy).then_inc(xT_ok, 1)

            def q_of(t):
                b = t.slot
                wait(act, ones_ok, 4)
                act.wait_ge(pq_ok, t.n + 1)
                wait(act, qo_out[b], t.turn * 16)
                for c in range(2):
                    for hh in range(2):
                        half = slice(hh * HD, (hh + 1) * HD)
                        at = c * HD + hh * WIN
                        act.activation(qo[b][half, :, at:at + WIN], pq[b][half, c, :].rearrange("p (w n) -> p w n", n=WIN),
                                       ACT.Identity, bias=g.ncq[half, c:c + 1], scale=-SCALE)
                        half = slice(c * HD, (c + 1) * HD)
                        last = act.activation(qo[b][half, :, P + at:P + at + WIN],
                                              pq[b][half, 2 + hh, :].rearrange("p (w n) -> p w n", n=WIN),
                                              ACT.Identity, bias=g.ncqr[half, hh:hh + 1], scale=-SCALE)
                last.then_inc(qo_ok, 1)

            sd_of(Step(0, 0, 2))
            xT_of(Step(0, 0, 2))

            def body(t):
                sd_of(t + 1)
                xT_of(t + 1)
                q_of(t)
            walk(act, 0, NT - 2, body, period=2)
            q_of(Step(0, NT - 1, 2))

        @block.tensor
        def _(pe):
            def turn_x(t):
                pe.wait_ge(x1_ok, t.n + 1)
                wait(pe, xT_ok, t.n - 1)
                for c in range(KD):
                    last = nc.tensor.transpose(pT[t.slot][:, c, :], x1s[t.slot][:, c * P:(c + 1) * P], g.ident[:])
                last.then_inc(pT_ok, 1)

            def products(t):
                b = t.slot
                pe.wait_ge(xT_ok, t.n + 1)
                wait(pe, kv_ok, t.n - 1)
                for k in range(KD):
                    last = nc.tensor.matmul(pkv[b][:], xT[b][:, k, :], g.wkv[:, k, :], start=(k == 0), stop=(k == KD - 1))
                last.then_inc(pkv_ok, 1)
                wait(pe, qo_ok, t.n - 1)
                for m in range(4):
                    w = g.wq if m < 2 else g.wqr
                    for k in range(KD):
                        last = nc.tensor.matmul(pq[b][:, m, :], w[:, k, (m % 2) * P:(m % 2 + 1) * P], xT[b][:, k, :],
                                                start=(k == 0), stop=(k == KD - 1))
                last.then_inc(pq_ok, 1)

            turn_x(Step(0, 0, 2))

            def both(t):
                turn_x(t + 1)
                products(t)
            walk(pe, 0, NT - 2, both, period=2)
            products(Step(0, NT - 1, 2))


def edges(nc, a, g, s):
    sb, ps, sem = s.sb, s.ps, s.sem
    two, four, eight = range(2), range(4), range(8)
    ix = [sb(f"ix{i}", [P, 4], I32) for i in two]
    dt = [sb(f"dt{i}", [P, 4, 2, P], I16) for i in two]
    q = [sb(f"q{i}", [P, QREC]) for i in eight]
    kv = [sb(f"kv{i}", [P, ROW]) for i in eight]
    kT = [sb(f"kT{i}", [P, KD, P]) for i in two]
    rel = [sb(f"rel{i}", [P, P]) for i in two]
    far = [sb(f"far{i}", [P, P]) for i in two]
    msk = [sb(f"msk{i}", [P, P]) for i in two]
    mx = [sb(f"mx{i}", [P, 1]) for i in two]
    nm = [sb(f"nm{i}", [P, 1]) for i in two]
    old = [sb(f"old{i}", [P, 1]) for i in two]
    cor = [sb(f"cor{i}", [P, 1]) for i in four]
    pr = [sb(f"pr{i}", [P, P]) for i in two]
    prT = [sb(f"prT{i}", [P, P]) for i in two]
    acc = sb("acc", [P, 8, VW])
    pk = [ps(f"pk{i}", [P, KD, P]) for i in two]
    psc = [ps(f"psc{i}", [P, P]) for i in two]
    ppT = [ps(f"ppT{i}", [P, P]) for i in two]
    pav = [ps(f"pav{i}", [P, VW]) for i in two]
    dt_in = [sem(f"dt_in{i}") for i in two]
    acc_out = [sem(f"acc_out{i}") for i in two]
    q_in = [sem(f"q_in{i}") for i in eight]
    kv_in = [sem(f"kv_in{i}") for i in eight]
    ix_ok, pool_seen, pk_ok, kT_ok, rel_ok, far_ok, sc_ok = (sem(x) for x in (
        "ix_ok", "pool_seen", "pk_ok", "kT_ok", "rel_ok", "far_ok", "sc_ok"))
    msk_ok, nm_ok, old_ok, pr_ok, ppT_ok, prT_ok, av_ok, acc_ok, cor_ok, dve_seen = (sem(x) for x in (
        "msk_ok", "nm_ok", "old_ok", "pr_ok", "ppT_ok", "prT_ok", "av_ok", "acc_ok", "cor_ok", "dve_seen"))
    LAST = STEPS - 1

    with s.block() as block:
        @block.sync
        def _(sp):
            def load_dt(t):
                b = t.slot // 4
                wait(sp, far_ok, t.n - 4)
                sp.dma_start(dt[b][:].rearrange("p s k e -> p (s k e)"),
                             a["dts"][bass.ds(t.n, 4), :].rearrange("(o s) k -> o (s k)", o=1).to_broadcast([P, 4 * 2 * P])).then_inc(dt_in[b], 16)

            def load_q(t):
                w = sp.value_load(g.wreg[0:1, bass.ds(t.n, 1)], min_val=0, max_val=NWIN - 1)
                wait(sp, sc_ok, t.n - 7)
                sp.dma_start(q[t.slot][:], a["qtab"][bass.ds(w, 1), :, :].rearrange("o p k -> p (o k)")).then_inc(q_in[t.slot], 16)

            def store(t, n=4):
                b = t.slot // 4
                sp.wait_ge(acc_ok, t.n + 1 + n)
                sp.dma_start(a["acctab"][bass.ds(t.n, n), :, :].rearrange("s p e -> p s e"), acc[:, 4 * b:4 * b + n, :]).then_inc(acc_out[b], 16)

            def body(t):
                if t.slot % 4 == 0:
                    load_dt(t)
                load_q(t)
                if t.slot % 4 == 3 and not (isinstance(t.n, int) and t.n < 11):
                    store(t - 11)
            walk(sp, 0, LAST, body, period=8)
            tail = LAST - (LAST % 4) - 8
            assert LAST % 4 == 1
            store(Step(0, tail, 8))
            store(Step(0, tail + 4, 8))
            store(Step(0, tail + 8, 8), LAST + 1 - (tail + 8))
            for b in two:
                sp.wait_ge(acc_out[b], 16 * ((LAST // 4 + 2 - b) // 2))

        @block.gpsimd
        def _(pool):
            def gather(t):
                b, half = t.slot, t.slot // 4
                if t.slot % 4 == 0:
                    wait(pool, kv_in[b + 3], t.turn * 16)
                    if not (isinstance(t.n, int) and t.n < 8):
                        pool.sem_inc(pool_seen, 1)
                    pool.tensor_copy(ix[half][:], g.idx[:, bass.ds(t.n, 4)]).then_inc(ix_ok, 1)
                    pool.wait_ge(ix_ok, t.quad + 1)
                    pool.sem_inc(pool_seen, 1)
                wait(pool, av_ok, t.n - 7)
                if not (isinstance(t.n, int) and t.n < 8):
                    pool.sem_inc(pool_seen, 1)
                pool.indirect_dma_start(out=kv[b][:], out_offset=None, in_=a["kvtab"],
                                        in_offset=bass.IndirectOffsetOnAxis(ap=ix[half][:, b % 4:b % 4 + 1], axis=0)).then_inc(kv_in[b], 16)
            walk(pool, 0, LAST, gather, period=8)

        @block.vector
        def _(v):
            v.memset(acc[:, 7, :], 0.0).then_inc(acc_ok, 1)
            v.memset(nm[1][:], 0.0).then_inc(nm_ok, 1)

            def masks(t):
                b, p = t.slot // 4, t.par
                if t.slot % 4 == 0:
                    v.wait_ge(dt_in[b], t.turn * 16 + 16)
                wait(v, sc_ok, t.n - 1)
                v.tensor_scalar(rel[p][:], dt[b][:, t.slot % 4, 1, :], g.rmod[:, 0:1], None, ALU.is_equal).then_inc(rel_ok, 1)
                v.tensor_scalar(far[p][:], dt[b][:, t.slot % 4, 0, :], g.nabs[:, bass.ds(t.n, 1)], FAR, ALU.not_equal, ALU.mult).then_inc(far_ok, 1)

            def maxima(t):
                p = t.par
                wait(v, cor_ok, t.n - 1)
                v.wait_ge(nm_ok, t.n + 1)
                v.tensor_scalar(old[p][:], nm[1 - p][:], g.fresh[:, bass.ds(t.n, 1)], None, ALU.add).then_inc(old_ok, 1)
                v.wait_ge(sc_ok, t.n + 1)
                v.wait_ge(far_ok, t.n + 1)
                v.sem_inc(dve_seen, 1)
                v.tensor_tensor_reduce(out=msk[p][:], in0=psc[p][:], in1=far[p][:], scale=1.0, scalar=FLOOR,
                                       op0=ALU.add, op1=ALU.min, accum_out=mx[p][:]).then_inc(msk_ok, 1)
                v.wait_ge(msk_ok, t.n + 1)
                v.tensor_tensor(nm[p][:], mx[p][:], old[p][:], ALU.min).then_inc(nm_ok, 1)

            def add(t):
                p = t.par
                if t.slot % 4 == 0:
                    wait(v, acc_out[t.slot // 4], t.turn * 16)
                v.wait_ge(av_ok, t.n + 1)
                v.wait_ge(acc_ok, t.n + 1)
                v.scalar_tensor_tensor(out=acc[:, t.slot, :], in0=acc[:, (t.slot - 1) % 8, :], scalar=cor[t.slot % 4][:, 0:1],
                                       in1=pav[p][:], op0=ALU.mult, op1=ALU.add).then_inc(acc_ok, 1)

            at = lambda n: Step(0, n, 8)
            masks(at(0))
            masks(at(1))
            maxima(at(0))
            masks(at(2))
            maxima(at(1))

            def body(t):
                masks(t + 1)
                maxima(t)
                add(t - 2)
            walk(v, 2, LAST - 1, body, period=8)
            maxima(at(LAST))
            for n in range(LAST - 2, LAST + 1):
                add(at(n))

        @block.scalar
        def _(act):
            def k_of(t):
                act.wait_ge(pk_ok, t.n + 1)
                wait(act, sc_ok, t.n - 1)
                act.activation(kT[t.par][:], pk[t.par][:], ACT.Copy).then_inc(kT_ok, 1)

            def weights(t):
                p = t.par
                act.wait_ge(nm_ok, t.n + 2)
                wait(act, ppT_ok, t.n - 1)
                act.activation(pr[p][:], msk[p][:], ACT.Exp, bias=nm[p][:, 0:1], scale=-1.0).then_inc(pr_ok, 1)
                wait(act, acc_ok, t.n - 2)
                act.activation(cor[t.slot % 4][:], old[p][:], ACT.Exp, bias=nm[p][:, 0:1], scale=-1.0).then_inc(cor_ok, 1)

            def w_of(t):
                act.wait_ge(ppT_ok, t.n + 1)
                wait(act, av_ok, t.n - 1)
                act.activation(prT[t.par][:], ppT[t.par][:], ACT.Copy).then_inc(prT_ok, 1)

            at = lambda n: Step(0, n, 8)
            k_of(at(0))
            k_of(at(1))
            weights(at(0))

            def body(t):
                k_of(t + 1)
                weights(t)
                w_of(t - 1)
            walk(act, 1, LAST - 1, body, period=8)
            weights(at(LAST))
            w_of(at(LAST - 1))
            w_of(at(LAST))

        @block.tensor
        def _(pe):
            def turn_k(t):
                b = t.slot
                pe.wait_ge(kv_in[b], t.turn * 16 + 16)
                wait(pe, kT_ok, t.n - 1)
                for c in range(KD):
                    last = nc.tensor.transpose(pk[t.par][:, c, :], kv[b][:, c * P:(c + 1) * P], g.ident[:])
                last.then_inc(pk_ok, 1)

            def scores(t):
                b, p = t.slot, t.par
                pe.wait_ge(q_in[b], t.turn * 16 + 16)
                pe.wait_ge(rel_ok, t.n + 1)
                wait(pe, msk_ok, t.n - 1)
                nc.tensor.matmul(psc[p][:], q[b][:, P:2 * P], rel[p][:], start=True, stop=True)
                pe.wait_ge(kT_ok, t.n + 1)
                for c in range(KD):
                    last = nc.tensor.matmul(psc[p][c * HD:(c + 1) * HD, :], q[b][:, c * HD:(c + 1) * HD], kT[p][:, c, :],
                                            start=False, stop=True, tile_position=(0, c * HD), skip_group_check=True)
                last.then_inc(sc_ok, 1)

            def turn_w(t):
                pe.wait_ge(pr_ok, t.n + 1)
                wait(pe, prT_ok, t.n - 1)
                nc.tensor.transpose(ppT[t.par][:], pr[t.par][:], g.ident[:]).then_inc(ppT_ok, 1)

            def sums(t):
                p = t.par
                pe.wait_ge(prT_ok, t.n + 1)
                wait(pe, acc_ok, t.n)
                for h in range(HEADS):
                    last = nc.tensor.matmul(pav[p][h * WIN:(h + 1) * WIN, :], prT[p][:, h * WIN:(h + 1) * WIN],
                                            kv[t.slot][:, D + h * VW:D + (h + 1) * VW], start=True, stop=True,
                                            tile_position=(0, h * WIN))
                last.then_inc(av_ok, 1)

            at = lambda n: Step(0, n, 8)
            turn_k(at(0))
            turn_k(at(1))
            scores(at(0))
            turn_k(at(2))
            scores(at(1))
            turn_w(at(0))

            def body(t):
                turn_k(t + 1)
                scores(t)
                turn_w(t - 1)
                sums(t - 2)
            walk(pe, 2, LAST - 1, body, period=8)
            scores(at(LAST))
            turn_w(at(LAST - 1))
            sums(at(LAST - 2))
            turn_w(at(LAST))
            sums(at(LAST - 1))
            sums(at(LAST))


def post(nc, a, g, s):
    sb, ps, sem = s.sb, s.ps, s.sem
    two = range(2)
    xin = [sb(f"xin{i}", [P, D]) for i in two]
    vin = [sb(f"vin{i}", [P, WPT, HD]) for i in two]
    st = [sb(f"st{i}", [P, WPT, VW]) for i in two]
    none = [sb(f"none{i}", [P, WPT]) for i in two]
    den = [sb(f"den{i}", [P, WPT]) for i in two]
    rden = [sb(f"rden{i}", [P, WPT]) for i in two]
    msg = [sb(f"msg{i}", [P, WPT, HD]) for i in two]
    alt = [sb(f"alt{i}", [P, WPT, HD]) for i in two]
    mT = [sb(f"mT{i}", [HD, HEADS, P]) for i in two]
    y = [sb(f"y{i}", [P, D]) for i in two]
    yn = [sb(f"yn{i}", [P, D]) for i in two]
    yg = [sb(f"yg{i}", [P, D]) for i in two]
    x2 = [sb(f"x2{i}", [P, D]) for i in two]
    z = [sb(f"z{i}", [P, D]) for i in two]
    zT = [sb(f"zT{i}", [P, KD, P]) for i in two]
    stats = [sb(f"stats{i}", [P, 6]) for i in two]
    mv = [sb(f"mv{i}", [P, 2]) for i in two]
    sd = [sb(f"sd{i}", [P, 1]) for i in two]
    rs = [sb(f"rs{i}", [P, 1]) for i in two]
    stats2 = [sb(f"stats2{i}", [P, 6]) for i in two]
    mv2 = [sb(f"mv2{i}", [P, 2]) for i in two]
    sd2 = [sb(f"sd2{i}", [P, 1]) for i in two]
    rs2 = [sb(f"rs2{i}", [P, 1]) for i in two]
    sd3 = [sb(f"sd3{i}", [P, 1]) for i in two]
    rs3 = [sb(f"rs3{i}", [P, 1]) for i in two]
    vz = [sb(f"vz{i}", [P, 1]) for i in two]
    lg = [sb(f"lg{i}", [P, E]) for i in two]
    t8 = [sb(f"t8{i}", [P, E]) for i in two]
    i8 = [sb(f"i8{i}", [P, E], U32) for i in two]
    pm = [ps(f"pm{i}", [P, 4, P]) for i in two]
    po = [ps(f"po{i}", [P, D]) for i in two]
    pz = [ps(f"pz{i}", [P, KD, P]) for i in two]
    pl = [ps(f"pl{i}", [P, E]) for i in two]
    x_in = [sem(f"x_in{i}") for i in two]
    v_in = [sem(f"v_in{i}") for i in two]
    st_in = [sem(f"st_in{i}") for i in two]
    x2_out = [sem(f"x2_out{i}") for i in two]
    names = ("none", "den", "rden", "msg", "alt", "mix", "pm", "mT", "po", "y", "yb", "stats", "mv", "sd", "rs", "yn", "yg",
             "yb2", "x2", "stats2", "mv2", "sd2", "rs2", "z", "vz", "sd3", "rs3", "xn", "pz", "zT", "pl", "lg", "t8", "i8", "keep", "x1s", "seen")
    o = {n: sem(n + "_ok") for n in names}
    dve_seen, pe_seen = sem("dve_seen"), sem("pe_seen")

    with s.block() as block:
        @block.sync
        def _(sp):
            def load(t):
                wait(sp, o["x2"], t.n - 1)
                sp.dma_start(xin[t.slot][:], rows(a["x"], t.n * P, P)).then_inc(x_in[t.slot], 16)
                wait(sp, o["msg"], t.n - 1)
                for w in range(WPT):
                    last = sp.value_load(g.lastreg[0:1, bass.ds(t.n * WPT + w, 1)], min_val=0, max_val=STEPS - 1)
                    sp.dma_start(st[t.slot][:, w, :], a["acctab"][bass.ds(last, 1), :, :].rearrange("o p e -> p (o e)")).then_inc(st_in[t.slot], 16)


            def store(t):
                sp.wait_ge(o["x2"], t.n + 1)
                sp.dma_start(rows(a["x2tab"], t.n * P, P), x2[t.slot][:]).then_inc(x2_out[t.slot], 16)

            load(Step(0, 0, 2))
            load(Step(0, 1, 2))

            def both(t):
                load(t + 2)
                store(t)
            walk(sp, 0, NT - 3, both, period=2)
            store(Step(0, NT - 2, 2))
            store(Step(0, NT - 1, 2))
            for i in two:
                sp.wait_ge(x2_out[i], 16 * ((NT + 1 - i) // 2))

        @block.vector
        def _(v):
            def messages(t):
                b = t.slot
                v.wait_ge(st_in[b], t.turn * (16 * WPT) + 16 * WPT)
                v.tensor_scalar(none[b][:], st[b][:, :, HD], 0.0, None, ALU.is_equal).then_inc(o["none"], 1)
                v.wait_ge(o["none"], t.n + 1)
                v.tensor_tensor(den[b][:], st[b][:, :, HD], none[b][:], ALU.add).then_inc(o["den"], 1)
                v.wait_ge(o["den"], t.n + 1)
                v.reciprocal(rden[b][:], den[b][:]).then_inc(o["rden"], 1)
                v.wait_ge(v_in[b], t.turn * (16 * HEADS) + 16 * HEADS)
                v.tensor_tensor(alt[b][:], vin[b][:], none[b][:, :, None].to_broadcast([P, WPT, HD]), ALU.mult).then_inc(o["alt"], 1)
                v.wait_ge(o["rden"], t.n + 1)
                wait(v, o["pm"], t.n - 1)
                v.tensor_tensor(msg[b][:], st[b][:, :, 0:HD], rden[b][:, :, None].to_broadcast([P, WPT, HD]), ALU.mult).then_inc(o["msg"], 1)
                v.wait_ge(o["msg"], t.n + 1)
                v.wait_ge(o["alt"], t.n + 1)
                v.tensor_tensor(msg[b][:], msg[b][:], alt[b][:], ALU.add).then_inc(o["mix"], 1)

            def rest(t):
                b = t.slot
                n1 = t.n + 1
                v.wait_ge(o["po"], n1)
                v.tensor_tensor(y[b][:], po[b][:], g.x1[:, bass.ds(t.n * D, D)], ALU.add).then_inc(o["y"], 1)
                v.wait_ge(o["y"], n1)
                v.tensor_tensor(y[b][:], y[b][:], g.bo[:], ALU.add).then_inc(o["yb"], 1)
                v.wait_ge(o["yb"], n1)
                v.bn_stats(stats[b][:], y[b][:]).then_inc(o["stats"], 1)
                v.wait_ge(o["stats"], n1)
                v.sem_inc(dve_seen, 1)
                v.bn_aggr(mv[b][:], stats[b][:]).then_inc(o["mv"], 1)
                v.wait_ge(o["sd"], n1)
                v.reciprocal(rs[b][:], sd[b][:]).then_inc(o["rs"], 1)
                v.wait_ge(o["rs"], n1)
                v.tensor_scalar(yn[b][:], y[b][:], mv[b][:, 0:1], rs[b][:, 0:1], ALU.subtract, ALU.mult).then_inc(o["yn"], 1)
                v.wait_ge(o["x2"], n1)
                v.bn_stats(stats2[b][:], x2[b][:]).then_inc(o["stats2"], 1)
                v.wait_ge(o["stats2"], n1)
                v.sem_inc(dve_seen, 1)
                v.bn_aggr(mv2[b][:], stats2[b][:]).then_inc(o["mv2"], 1)
                v.wait_ge(o["sd2"], n1)
                v.reciprocal(rs2[b][:], sd2[b][:]).then_inc(o["rs2"], 1)
                v.wait_ge(o["rs2"], n1)
                wait(v, o["pz"], t.n - 1)
                v.tensor_scalar(z[b][:], x2[b][:], mv2[b][:, 0:1], rs2[b][:, 0:1], ALU.subtract, ALU.mult).then_inc(o["z"], 1)
                v.tensor_scalar(vz[b][:], mv2[b][:, 1:2], rs2[b][:, 0:1], rs2[b][:, 0:1], ALU.mult, ALU.mult).then_inc(o["vz"], 1)
                v.wait_ge(o["sd3"], n1)
                v.reciprocal(rs3[b][:], sd3[b][:]).then_inc(o["rs3"], 1)
                v.wait_ge(o["rs3"], n1)
                v.tensor_scalar(g.x1[:, bass.ds(t.n * D, D)], z[b][:], rs3[b][:, 0:1], None, ALU.mult).then_inc(o["xn"], 1)

            def top2(t):
                b = t.slot
                n1 = t.n + 1
                v.wait_ge(o["pl"], n1)
                v.tensor_tensor(lg[b][:], pl[b][:], g.br[:], ALU.add).then_inc(o["lg"], 1)
                v.wait_ge(o["lg"], n1)
                v.sem_inc(dve_seen, 1)
                v.max(t8[b][:], lg[b][:]).then_inc(o["t8"], 1)
                v.wait_ge(o["t8"], n1)
                v.sem_inc(dve_seen, 1)
                v.max_index(i8[b][:], t8[b][:], lg[b][:]).then_inc(o["i8"], 1)
                v.tensor_copy(g.top_l[:, bass.ds(t.n * 2, 2)], t8[b][:, 0:2])
                v.wait_ge(o["i8"], n1)
                v.tensor_copy(g.top_i[:, bass.ds(t.n * 2, 2)], i8[b][:, 0:2]).then_inc(o["keep"], 1)

            messages(Step(0, 0, 2))

            def body(t):
                messages(t + 1)
                rest(t)
                top2(t)
            walk(v, 0, NT - 2, body, period=2)
            rest(Step(0, NT - 1, 2))
            top2(Step(0, NT - 1, 2))

        @block.gpsimd
        def _(pool):
            def residual(t):
                b = t.slot
                n1 = t.n + 1
                pool.wait_ge(o["yn"], n1)
                pool.tensor_tensor(yg[b][:], yn[b][:], g.gamma[:], ALU.mult).then_inc(o["yg"], 1)
                pool.wait_ge(o["yg"], n1)
                pool.tensor_tensor(yg[b][:], yg[b][:], g.beta[:], ALU.add).then_inc(o["yb2"], 1)
                pool.wait_ge(o["yb2"], n1)
                pool.sem_inc(o["seen"], 1)
                wait(pool, x2_out[b], t.turn * 16)
                pool.sem_inc(o["seen"], 1)
                wait(pool, o["z"], t.n - 1)
                pool.wait_ge(x_in[b], t.turn * 16 + 16)
                pool.sem_inc(o["seen"], 1)
                pool.tensor_tensor(x2[b][:], yg[b][:], xin[b][:], ALU.add).then_inc(o["x2"], 1)
            walk(pool, 0, NT - 1, residual, period=2)

        @block.scalar
        def _(act):
            def load_v(t):
                wait(act, o["alt"], t.n - 1)
                for h in range(HEADS):
                    act.dma_start(vin[t.slot][h * WIN:(h + 1) * WIN, :, :],
                                  rows(a["kvtab"], t.n * P, P)[:, D + h * VW:D + h * VW + HD].rearrange("(w n) d -> n w d", n=WIN)).then_inc(v_in[t.slot], 16)

            load_v(Step(0, 0, 2))
            load_v(Step(0, 1, 2))

            def mT_of(t):
                act.wait_ge(o["pm"], t.n + 1)
                wait(act, o["po"], t.n - 1)
                act.activation(mT[t.slot][:].rearrange("d h (w n) -> d w h n", n=WIN),
                               pm[t.slot][0:HD, :, :].rearrange("d w (h n) -> d w h n", n=WIN), ACT.Copy).then_inc(o["mT"], 1)

            def body(t):
                b = t.slot
                n1 = t.n + 1
                act.wait_ge(o["mv"], n1)
                act.activation(sd[b][:], mv[b][:, 1:2], ACT.Sqrt, bias=g.eps[:, 0:1]).then_inc(o["sd"], 1)
                act.wait_ge(o["mv2"], n1)
                act.activation(sd2[b][:], mv2[b][:, 1:2], ACT.Sqrt, bias=g.eps[:, 0:1]).then_inc(o["sd2"], 1)
                act.wait_ge(o["vz"], n1)
                act.activation(sd3[b][:], vz[b][:], ACT.Sqrt, bias=g.eps[:, 0:1]).then_inc(o["sd3"], 1)
                act.wait_ge(o["pz"], n1)
                wait(act, o["pl"], t.n - 1)
                act.activation(zT[b][:], pz[b][:], ACT.Copy).then_inc(o["zT"], 1)

            mT_of(Step(0, 0, 2))

            def both(t):
                mT_of(t + 1)
                load_v(t + 2)
                body(t)
            walk(act, 0, NT - 3, both, period=2)
            mT_of(Step(0, NT - 1, 2))
            body(Step(0, NT - 2, 2))
            body(Step(0, NT - 1, 2))

        @block.tensor
        def _(pe):
            def out(t):
                b = t.slot
                pe.wait_ge(o["mix"], t.n + 1)
                wait(pe, o["mT"], t.n - 1)
                pe.sem_inc(pe_seen, 1)
                for w in range(WPT):
                    last = nc.tensor.transpose(pm[b][0:HD, w, :], msg[b][:, w, :], g.ident[:])
                last.then_inc(o["pm"], 1)
                pe.wait_ge(o["mT"], t.n + 1)
                wait(pe, o["y"], t.n - 1)
                for h in range(HEADS):
                    last = nc.tensor.matmul(po[b][:], mT[b][:, h, :], g.wo[:, h, :], start=(h == 0), stop=(h == HEADS - 1))
                last.then_inc(o["po"], 1)

            def router(t):
                b = t.slot
                pe.wait_ge(o["z"], t.n + 1)
                wait(pe, o["zT"], t.n - 1)
                for c in range(KD):
                    last = nc.tensor.transpose(pz[b][:, c, :], z[b][:, c * P:(c + 1) * P], g.ident[:])
                last.then_inc(o["pz"], 1)
                pe.wait_ge(o["zT"], t.n + 1)
                wait(pe, o["lg"], t.n - 1)
                for c in range(KD):
                    last = nc.tensor.matmul(pl[b][:], zT[b][:, c, :], g.wr[:, c, :], start=(c == 0), stop=(c == KD - 1))
                last.then_inc(o["pl"], 1)

            out(Step(0, 0, 2))

            def both(t):
                out(t + 1)
                router(t)
            walk(pe, 0, NT - 2, both, period=2)
            router(Step(0, NT - 1, 2))


def route(nc, a, g, s):
    sb, ps, sem = s.sb, s.ps, s.sem
    C = NT * E
    m1, m2, both_m = sb("m1", [P, NT, E]), sb("m2", [P, NT, E]), sb("both", [P, NT, E])
    tot, run, off = sb("tot", [P, NT, E]), sb("run", [P, NT, E]), sb("off", [P, NT, E])
    sel = sb("sel", [P, NT, E])
    one = sb("one", [P, NT])
    cnt, cnti, tiles_i = sb("cnt", [P, E]), sb("cnti", [P, E], I32), sb("tiles_i", [P, E], I32)
    tiles, cum, base = sb("tiles", [P, E]), sb("cum", [P, E]), sb("base", [P, E])
    posf = sb("posf", [P, 2, NT])
    eof = [sb(f"eof{i}", [P, MT]) for i in range(2)]
    dif = sb("dif", [P, NT])
    ex = sb("ex", [P, NT])
    row = [sb(f"row{i}", [P, D]) for i in range(4)]
    ix = [sb(f"ix{i}", [P, 2], I32) for i in range(4)]
    pin, ptot = ps("pin", [P, C]), ps("ptot", [P, C])
    chain, masks_ok, counts_ok, dif_ok, ex_ok = (sem(x) for x in ("chain", "masks_ok", "counts_ok", "dif_ok", "ex_ok"))
    row_ok, ix_ok, seen = sem("row_ok"), sem("ix_ok"), sem("seen")
    out = [sem(f"out{i}") for i in range(4)]

    with s.block() as block:
        @block.vector
        def _(v):
            done = [0]

            def link(ins):
                done[0] += 1
                ins.then_inc(chain, 1)
                v.wait_ge(chain, done[0])

            iota = g.iota8[:, None, :].to_broadcast([P, NT, E])
            choice = g.top_i[:].rearrange("p (t k) -> p k t", k=2)
            logit = g.top_l[:].rearrange("p (t k) -> p k t", k=2)
            v.tensor_tensor(dif[:], logit[:, 1, :], logit[:, 0, :], ALU.subtract).then_inc(dif_ok, 1)
            v.memset(one[:], 1.0)
            v.tensor_tensor(m1[:], iota, choice[:, 0, :, None].to_broadcast([P, NT, E]), ALU.is_equal)
            link(v.tensor_tensor(m2[:], iota, choice[:, 1, :, None].to_broadcast([P, NT, E]), ALU.is_equal))
            v.tensor_tensor(both_m[:], m1[:], m2[:], ALU.add).then_inc(masks_ok, 1)
            v.wait_ge(counts_ok, 1)
            link(v.tensor_copy(tot[:], ptot.rearrange("p (t e) -> p t e", e=E)))
            for e in range(E):
                last = v.tensor_tensor_scan(out=run[:, :, e], data0=one[:], data1=tot[:, :, e], initial=0.0, op0=ALU.mult, op1=ALU.add)
            link(last)
            link(v.tensor_copy(cnt[:], run[:, NT - 1, :]))
            link(v.tensor_tensor(run[:], run[:], tot[:], ALU.subtract))
            link(v.tensor_tensor(off[:], run[:], pin.rearrange("p (t e) -> p t e", e=E), ALU.add))
            link(v.tensor_scalar(cnti[:], cnt[:], float(P - 1), None, ALU.add))
            link(v.tensor_single_scalar(tiles_i[:], cnti[:], 7, ALU.arith_shift_right))
            link(v.tensor_copy(tiles[:], tiles_i[:]))
            link(v.tensor_tensor_scan(out=cum[:], data0=one[:, 0:E], data1=tiles[:], initial=0.0, op0=ALU.mult, op1=ALU.add))
            link(v.tensor_tensor(base[:], cum[:], tiles[:], ALU.subtract))
            link(v.tensor_scalar(base[:], base[:], float(P), None, ALU.mult))
            link(v.tensor_tensor(off[:], off[:], base[:, None, :].to_broadcast([P, NT, E]), ALU.add))
            for k, m in enumerate((m1, m2)):
                link(v.tensor_tensor(sel[:], m[:], off[:], ALU.mult))
                link(v.reduce_sum(posf[:, k, :], sel[:], AX.X))
            link(v.tensor_copy(g.pos[:].rearrange("p (t k) -> p k t", k=2), posf[:]))
            link(v.tensor_scalar(eof[0][:], g.tileno[:], cum[:, 0:1], None, ALU.is_ge))
            for e in range(1, E - 1):
                link(v.scalar_tensor_tensor(out=eof[e % 2][:], in0=g.tileno[:], scalar=cum[:, e:e + 1], in1=eof[(e + 1) % 2][:],
                                            op0=ALU.is_ge, op1=ALU.add))
            link(v.tensor_copy(g.expert[:], eof[(E - 2) % 2][:]))
            v.wait_ge(ex_ok, 1)
            link(v.tensor_scalar(dif[:], ex[:], 1.0, None, ALU.add))
            link(v.reciprocal(g.w1[:], dif[:]))
            link(v.tensor_tensor(g.w2[:], ex[:], g.w1[:], ALU.mult))

            def stage(t):
                b = t.slot
                wait(v, out[b], t.turn * 32)
                v.tensor_scalar(row[b][:], g.x1[:, bass.ds(t.n * D, D)], 1.0, None, ALU.mult).then_inc(row_ok, 1)
                v.tensor_scalar(ix[b][:], g.pos[:, bass.ds(t.n * 2, 2)], 1.0, None, ALU.mult).then_inc(ix_ok, 1)
            walk(v, 0, NT - 1, stage)

        @block.scalar
        def _(act):
            act.wait_ge(dif_ok, 1)
            act.activation(ex[:], dif[:], ACT.Exp).then_inc(ex_ok, 1)

        @block.tensor
        def _(pe):
            pe.wait_ge(masks_ok, 1)
            flat = both_m[:].rearrange("p t e -> p (t e)")
            nc.tensor.matmul(pin, g.tri[:], flat, start=True, stop=True)
            nc.tensor.matmul(ptot, g.ones[:], flat, start=True, stop=True).then_inc(counts_ok, 1)

        @block.gpsimd
        def _(pool):
            def scatter(t):
                b = t.slot
                pool.wait_ge(row_ok, t.n + 1)
                pool.sem_inc(seen, 1)
                pool.wait_ge(ix_ok, t.n + 1)
                pool.sem_inc(seen, 1)
                for k in range(2):
                    pool.indirect_dma_start(out=a["xs"], out_offset=bass.IndirectOffsetOnAxis(ap=ix[b][:, k:k + 1], axis=0),
                                            in_=row[b][:], in_offset=None).then_inc(out[b], 16)
            walk(pool, 0, NT - 1, scatter)
            for i in range(4):
                pool.wait_ge(out[i], 32 * ((NT + 3 - i) // 4))


def experts(nc, a, g, s):
    sb, ps, sem = s.sb, s.ps, s.sem
    two = range(2)
    w1 = sb("w1", [P, E * KD * H])
    w2 = sb("w2", [P, E * KH * D])
    pick = sb("pick", [P, E * P], BF16)
    b1s, b2s = sb("b1s", [P, H], BF16), sb("b2s", [P, D], BF16)
    xs = [sb(f"xs{i}", [P, D]) for i in two]
    gb = [sb(f"gb{i}", [P, 2 * KD]) for i in two]
    xT = [sb(f"xT{i}", [P, KD, P]) for i in two]
    h = [sb(f"h{i}", [P, H]) for i in two]
    hT = [sb(f"hT{i}", [P, KH, P]) for i in two]
    y = [sb(f"y{i}", [P, D]) for i in two]
    pieces = sb("pieces", [E, 3, H + D], BF16)
    left = [sb(f"left{i}", [E, H + D]) for i in two]
    whole = sb("whole", [E, H + D])
    px = ps("px", [P, KD, P])
    ph = [[ps(f"ph{i}{j}", [P, 512]) for j in two] for i in two]
    pt = [ps(f"pt{i}", [P, 4, P]) for i in two]
    py = ps("py", [P, D])
    w_in, cleared, chain, split_ok, pieces_in, pick_ok = (sem(x) for x in ("w_in", "cleared", "chain", "split_ok", "pieces_in", "pick_ok"))
    x_in = [sem(f"x_in{i}") for i in two]
    y_out = [sem(f"y_out{i}") for i in two]
    px_ok, xT_ok, ph_ok, h_ok, pt_ok0, pt_ok1, hT_ok0, hT_ok1, py_ok, y_ok = (sem(x) for x in (
        "px_ok", "xT_ok", "ph_ok", "h_ok", "pt_ok0", "pt_ok1", "hT_ok0", "hT_ok1", "py_ok", "y_ok"))

    with s.block() as block:
        @block.sync
        def _(sp):
            for e in range(E):
                sp.dma_start(w1[:, e * KD * H:(e + 1) * KD * H].rearrange("p (c n) -> p c n", c=KD),
                             a["W1"][e, :, :].rearrange("(c p) n -> p c n", p=P)).then_inc(w_in, 16)
                sp.dma_start(w2[:, e * KH * D:(e + 1) * KH * D].rearrange("p (c n) -> p c n", c=KH),
                             a["W2"][e, :, :].rearrange("(c p) n -> p c n", p=P)).then_inc(w_in, 16)
            sp.wait_ge(split_ok, 1)
            sp.wait_ge(cleared, 2)
            for k in range(3):
                sp.dma_start(b1s[k * E:(k + 1) * E, :], pieces[:, k, 0:H]).then_inc(pieces_in, 16)
                sp.dma_start(b2s[k * E:(k + 1) * E, :], pieces[:, k, H:H + D]).then_inc(pieces_in, 16)

            def load(t):
                e = sp.value_load(g.expert[0:1, bass.ds(t.n, 1)], min_val=0, max_val=E - 1)
                wait(sp, px_ok, t.n - 1)
                sp.dma_start(xs[t.slot][:], rows(a["xs"], t.n * P, P)).then_inc(x_in[t.slot], 16)
                wait(sp, xT_ok, t.n - 1)
                sp.dma_start(gb[t.slot][:], a["lngb"][bass.ds(e, 1), :, :].rearrange("o p k -> p (o k)")).then_inc(x_in[t.slot], 16)

            def store(t):
                sp.wait_ge(y_ok, t.n + 1)
                sp.dma_start(rows(a["ys"], t.n * P, P), y[t.slot][:]).then_inc(y_out[t.slot], 16)

            load(Step(0, 0, 2))
            load(Step(0, 1, 2))

            def both(t):
                load(t + 2)
                store(t)
            walk(sp, 0, MT - 3, both, period=2)
            store(Step(0, MT - 2, 2))
            store(Step(0, MT - 1, 2))
            for i in two:
                sp.wait_ge(y_out[i], 16 * ((MT + 1 - i) // 2))

        @block.gpsimd
        def _(pool):
            pool.memset(pick[:], 0.0).then_inc(pick_ok, 1)
            for k in range(3):
                pool.wait_ge(pick_ok, k + 1)
                pool.affine_select(out=pick[:].rearrange("p (e n) -> p e n", e=E), in_=pick[:].rearrange("p (e n) -> p e n", e=E),
                                   compare_op=ALU.not_equal, fill=1.0, base=-k * E, pattern=[[-1, E], [0, P]],
                                   channel_multiplier=1).then_inc(pick_ok, 1)

        @block.vector
        def _(v):
            v.memset(b1s[:], 0.0).then_inc(cleared, 1)
            v.memset(b2s[:], 0.0).then_inc(cleared, 1)
            done = [0]

            def link(ins):
                done[0] += 1
                ins.then_inc(chain, 1)
                v.wait_ge(chain, done[0])
            link(v.tensor_copy(whole[:, 0:H], g.b1f[:]))
            link(v.tensor_copy(whole[:, H:H + D], g.b2f[:]))
            rest = whole
            for k in range(3):
                last = v.tensor_copy(pieces[:, k, :], rest[:])
                if k < 2:
                    link(last)
                    link(v.tensor_tensor(left[k][:], rest[:], pieces[:, k, :], ALU.subtract))
                    rest = left[k]
            last.then_inc(split_ok, 1)

            def xT_of(t):
                b = t.slot
                v.wait_ge(x_in[b], t.turn * 32 + 32)
                v.wait_ge(px_ok, t.n + 1)
                wait(v, ph_ok, t.n - 1)
                for c in range(KD):
                    last = v.tensor_scalar(xT[b][:, c, :], px[:, c, :], gb[b][:, c:c + 1], gb[b][:, KD + c:KD + c + 1], ALU.mult, ALU.add)
                last.then_inc(xT_ok, 1)

            def hT_of(t):
                v.wait_ge(pt_ok0, t.n + 1)
                wait(v, py_ok, t.n - 1)
                v.tensor_copy(hT[t.slot][:, 0:4, :], pt[0][:]).then_inc(hT_ok0, 1)

            def y_of(t):
                b = t.slot
                v.wait_ge(py_ok, t.n + 1)
                wait(v, y_out[b], t.turn * 16)
                v.tensor_copy(y[b][:], py[:]).then_inc(y_ok, 1)

            xT_of(Step(0, 0, 2))
            xT_of(Step(0, 1, 2))

            def body(t):
                xT_of(t + 1)
                hT_of(t - 1)
                y_of(t - 1)
            walk(v, 1, MT - 2, body, period=2)
            for n in (MT - 2, MT - 1):
                hT_of(Step(0, n, 2))
                y_of(Step(0, n, 2))

        @block.scalar
        def _(act):
            def h_of(t):
                b = t.slot
                act.wait_ge(ph_ok, t.n + 1)
                wait(act, pt_ok1, t.n - 1)
                act.activation(h[b][:, 0:512], ph[b][0][:], ACT.Gelu)
                act.activation(h[b][:, 512:H], ph[b][1][:], ACT.Gelu).then_inc(h_ok, 1)

            def hT_of(t):
                act.wait_ge(pt_ok1, t.n + 1)
                wait(act, py_ok, t.n - 1)
                act.activation(hT[t.slot][:, 4:8, :], pt[1][:], ACT.Copy).then_inc(hT_ok1, 1)

            h_of(Step(0, 0, 2))

            def body(t):
                hT_of(t - 1)
                h_of(t)
            walk(act, 1, MT - 1, body, period=2)
            hT_of(Step(0, MT - 1, 2))

        @block.tensor
        def _(pe):
            def turn_x(t):
                pe.wait_ge(x_in[t.slot], t.turn * 32 + 32)
                wait(pe, xT_ok, t.n)
                for c in range(KD):
                    last = nc.tensor.transpose(px[:, c, :], xs[t.slot][:, c * P:(c + 1) * P], g.ident[:])
                last.then_inc(px_ok, 1)

            def hidden(t, e):
                b = t.slot
                pe.wait_ge(xT_ok, t.n + 1)
                wait(pe, h_ok, t.n - 1)
                for j in two:
                    nc.tensor.matmul(ph[b][j][:], pick[:, bass.ds(e * P, P)], b1s[:, j * 512:(j + 1) * 512], start=True, stop=False)
                    for c in range(KD):
                        last = nc.tensor.matmul(ph[b][j][:], xT[b][:, c, :], w1[:, bass.ds(e * (KD * H) + (c * H + j * 512), 512)],
                                                start=False, stop=(c == KD - 1))
                last.then_inc(ph_ok, 1)

            def back(t, e):
                b = t.slot
                pe.wait_ge(h_ok, t.n + 1)
                for j, (pt_ok, hT_ok) in enumerate(((pt_ok0, hT_ok0), (pt_ok1, hT_ok1))):
                    wait(pe, hT_ok, t.n)
                    for c in range(4):
                        last = nc.tensor.transpose(pt[j][:, c, :], h[b][:, (4 * j + c) * P:(4 * j + c + 1) * P], g.ident[:])
                    last.then_inc(pt_ok, 1)
                wait(pe, y_ok, t.n)
                nc.tensor.matmul(py[:], pick[:, bass.ds(e * P, P)], b2s[:], start=True, stop=False)
                for c in range(KH):
                    if c % 4 == 0:
                        pe.wait_ge((hT_ok0, hT_ok1)[c // 4], t.n + 1)
                    last = nc.tensor.matmul(py[:], hT[b][:, c, :], w2[:, bass.ds(e * (KH * D) + c * D, D)], start=False, stop=(c == KH - 1))
                last.then_inc(py_ok, 1)

            def expert(t):
                return pe.value_load(g.expert[0:1, bass.ds(t.n, 1)], min_val=0, max_val=E - 1)

            pe.wait_ge(w_in, 16 * 2 * E)
            pe.wait_ge(pick_ok, 4)
            pe.wait_ge(pieces_in, 16 * 6)
            turn_x(Step(0, 0, 2))
            turn_x(Step(0, 1, 2))
            hidden(Step(0, 0, 2), expert(Step(0, 0, 2)))

            def body(t):
                turn_x(t + 1)
                hidden(t, expert(t))
                back(t - 1, expert(t - 1))
            walk(pe, 1, MT - 2, body, period=2)
            hidden(Step(0, MT - 1, 2), expert(Step(0, MT - 1, 2)))
            back(Step(0, MT - 2, 2), expert(Step(0, MT - 2, 2)))
            back(Step(0, MT - 1, 2), expert(Step(0, MT - 1, 2)))


def combine(nc, a, g, s):
    sb, sem = s.sb, s.sem
    four = range(4)
    ix = [sb(f"ix{i}", [P, 2], I32) for i in four]
    y1 = [sb(f"y1{i}", [P, D]) for i in four]
    y2 = [sb(f"y2{i}", [P, D]) for i in four]
    x2 = [sb(f"x2{i}", [P, D]) for i in four]
    m = [sb(f"m{i}", [P, D]) for i in four]
    o = [sb(f"o{i}", [P, D]) for i in four]
    y_in = [sem(f"y_in{i}") for i in four]
    x_in = [sem(f"x_in{i}") for i in four]
    stored = [sem(f"stored{i}") for i in four]
    ix_ok, m_ok, o_ok, seen = sem("ix_ok"), sem("m_ok"), sem("o_ok"), sem("seen")

    with s.block() as block:
        @block.sync
        def _(sp):
            def load(t):
                wait(sp, m_ok, t.n - 3)
                sp.dma_start(x2[t.slot][:], rows(a["x2tab"], t.n * P, P)).then_inc(x_in[t.slot], 16)
            walk(sp, 0, NT - 1, load)

        @block.gpsimd
        def _(pool):
            def gather(t):
                b = t.slot
                wait(pool, o_ok, t.n - 3)
                pool.sem_inc(seen, 1)
                pool.wait_ge(ix_ok, t.n + 1)
                pool.sem_inc(seen, 1)
                for k, y in enumerate((y1, y2)):
                    pool.indirect_dma_start(out=y[b][:], out_offset=None, in_=a["ys"],
                                            in_offset=bass.IndirectOffsetOnAxis(ap=ix[b][:, k:k + 1], axis=0)).then_inc(y_in[b], 16)
            walk(pool, 0, NT - 1, gather)

        @block.vector
        def _(v):
            def index(t):
                wait(v, y_in[t.slot], t.turn * 32)
                v.tensor_scalar(ix[t.slot][:], g.pos[:, bass.ds(t.n * 2, 2)], 1.0, None, ALU.mult).then_inc(ix_ok, 1)

            def add(t):
                b = t.slot
                v.wait_ge(y_in[b], t.turn * 32 + 32)
                v.wait_ge(x_in[b], t.turn * 16 + 16)
                v.scalar_tensor_tensor(out=m[b][:], in0=y1[b][:], scalar=g.w1[:, bass.ds(t.n, 1)], in1=x2[b][:], op0=ALU.mult, op1=ALU.add).then_inc(m_ok, 1)
                v.wait_ge(m_ok, t.n + 1)
                wait(v, stored[b], t.turn * 16)
                v.scalar_tensor_tensor(out=o[b][:], in0=y2[b][:], scalar=g.w2[:, bass.ds(t.n, 1)], in1=m[b][:], op0=ALU.mult, op1=ALU.add).then_inc(o_ok, 1)

            for n in range(3):
                index(Step(0, n))

            def body(t):
                index(t + 3)
                add(t)
            walk(v, 0, NT - 4, body)
            for n in range(NT - 3, NT):
                add(Step(0, n))

        @block.scalar
        def _(act):
            def store(t):
                act.wait_ge(o_ok, t.n + 1)
                act.dma_start(rows(a["out"], t.n * P, P), o[t.slot][:]).then_inc(stored[t.slot], 16)
            walk(act, 0, NT - 1, store)
            for i in four:
                act.wait_ge(stored[i], 16 * ((NT + 3 - i) // 4))


class Kept:
    pass


def program(nc, a):
    with ExitStack() as whole:
        g = Kept()

        def buf(stack, name, shape, dt=F32):
            return stack.enter_context(nc.sbuf_tensor("g_" + name, shape, dt))

        g.gp = whole.enter_context(nc.semaphore("gp"))
        g.xs_clear = whole.enter_context(nc.semaphore("xs_clear"))
        g.ident = buf(whole, "ident", [P, P])
        g.tri = buf(whole, "tri", [P, P])
        g.ones = buf(whole, "ones", [P, P])
        g.eps = buf(whole, "eps", [P, 1])
        g.iota8 = buf(whole, "iota8", [P, E])
        g.tileno = buf(whole, "tileno", [P, MT])
        g.bo = buf(whole, "bo", [P, D])
        g.gamma = buf(whole, "gamma", [P, D])
        g.beta = buf(whole, "beta", [P, D])
        g.br = buf(whole, "br", [P, E])
        g.wr = buf(whole, "wr", [P, KD, E])
        g.wo = buf(whole, "wo", [HD, HEADS, D])
        g.b1f = buf(whole, "b1f", [E, H])
        g.b2f = buf(whole, "b2f", [E, D])
        g.top_l = buf(whole, "top_l", [P, NT * 2])
        g.top_i = buf(whole, "top_i", [P, NT * 2])
        g.pos = buf(whole, "pos", [P, NT * 2])
        g.w1 = buf(whole, "w1", [P, NT])
        g.w2 = buf(whole, "w2", [P, NT])
        g.expert = buf(whole, "expert", [P, MT], I32)
        with ExitStack() as rows_kept:
            g.x1 = buf(rows_kept, "x1", [P, NT * D])
            with ExitStack() as graph:
                g.idx = buf(graph, "idx", [P, STEPS_PAD], I32)
                g.wreg = buf(graph, "wreg", [1, STEPS_PAD], I32)
                g.lastreg = buf(graph, "lastreg", [1, NWIN], I32)
                g.fresh = buf(graph, "fresh", [P, STEPS])
                g.rmod = buf(graph, "rmod", [P, 1])
                g.nabs = buf(graph, "nabs", [P, STEPS])
                with ExitStack() as proj:
                    g.wq = buf(proj, "wq", [P, KD, D])
                    g.wkv = buf(proj, "wkv", [P, KD, 2 * D])
                    g.wqr = buf(proj, "wqr", [P, KD, D])
                    g.ncq = buf(proj, "ncq", [P, 2])
                    g.ncqr = buf(proj, "ncqr", [P, 2])
                    g.ckv = buf(proj, "ckv", [P, 2 * D])
                    with Scope(nc, "setup") as s:
                        setup(nc, a, g, s)
                    with Scope(nc, "nodes") as s:
                        nodes(nc, a, g, s)
                with Scope(nc, "edges") as s:
                    edges(nc, a, g, s)
                with Scope(nc, "post") as s:
                    post(nc, a, g, s)
            with Scope(nc, "route") as s:
                route(nc, a, g, s)
        with Scope(nc, "experts") as s:
            experts(nc, a, g, s)
        with Scope(nc, "combine") as s:
            combine(nc, a, g, s)


def kernel(**inputs):
    import concourse.bacc as bacc
    from concourse.bass_utils import run_bass_kernel_spmd as run

    nc = bacc.Bacc("TRN2", target_bir_lowering=False, num_devices=1)
    raw = {k: np.asarray(v) for k, v in inputs.items()}

    def padded(v, n, fill):
        out = np.full((n,) + v.shape[1:], fill, v.dtype)
        out[:len(v)] = v
        return out

    def swapped(v):
        return np.moveaxis(v.reshape(v.shape[:-1] + (2, 2, HD)), -3, -2).reshape(v.shape)

    dst = padded(raw["dst"], ET_PAD * P, PAD_DST)
    ins = {
        "x": padded(raw["x"], NPAD, 0),
        "edges": np.stack([e.reshape(ET_PAD, P) for e in (
            padded(raw["src"], ET_PAD * P, 0), dst, padded(raw["edge_type_64"], ET_PAD * P, 0))], 1).reshape(ET_PAD, 3 * P),
        "first": dst[P:ET * P:P],
        "q_emb": raw["L0_gnn_query_emb"].reshape(KD, P).T,
        "bq": np.concatenate([raw["L0_gnn_bq"], swapped(raw["L0_gnn_bq"])]).reshape(2 * KD, P).T,
        "WqP": swapped(raw["L0_gnn_Wq"]),
        "WqT": swapped(raw["L0_gnn_Wq"]).T,
        "relT": raw["L0_gnn_rel_w"].T,
    }
    for name in ("Wq", "Wk", "bk", "Wv", "bv", "Wo", "bo", "gamma", "beta"):
        ins[name] = raw["L0_gnn_" + name]
    for name in ("Wr", "br", "W1", "b1", "W2", "b2"):
        ins[name] = raw["L0_ffn_" + name]
    ins["lngb"] = np.stack([raw["L0_ffn_ln_g"], raw["L0_ffn_ln_b"]], 1).reshape(E, 2 * KD, P).transpose(0, 2, 1)
    ins = {k: np.ascontiguousarray(v) for k, v in ins.items()}
    a = {k: nc.dram_tensor(k, v.shape, mybir.dt.from_np(v.dtype), kind="ExternalInput").ap() for k, v in ins.items()}
    a["out"] = nc.dram_tensor("out", (NPAD, D), F32, kind="ExternalOutput").ap()
    for name, shape, dt in (("kvtab", (NPAD, ROW), F32), ("qtab", (NWIN, P, QREC), F32), ("acctab", (STEPS, P, VW), F32),
                            ("dts", (STEPS_PAD, 2 * P), I16), ("wtab", (STEPS_PAD,), I32), ("lasttab", (2 * P,), I32),
                            ("x2tab", (NPAD, D), F32), ("xs", (MT * P, D), F32), ("ys", (MT * P, D), F32)):
        a[name] = nc.dram_tensor(name, shape, dt, kind="Internal").ap()
    program(nc, a)
    r = run(nc, [ins], core_ids=[0])
    return r.results[0]["out"][:N_NODES]
```

```python
import numpy as np
import concourse.bass as bass
from concourse import mybir
from contextlib import ExitStack

F32 = mybir.dt.float32
BF16 = mybir.dt.bfloat16
I32 = mybir.dt.int32
I8 = mybir.dt.int8
U32 = mybir.dt.uint32
ALU = mybir.AluOpType
ACT = mybir.ActivationFunctionType
AX = mybir.AxisListType

P = 128
N_NODES, N_EDGES = 6250, 100000
D = 256
HEADS, HD = 4, 64
N_REL = 64
NT = -(-N_NODES // P)
NPAD = NT * P
WIN = 32
NWIN = NPAD // WIN
WPT = P // WIN
ET = -(-N_EDGES // P) + 1
ET_PAD = -(-ET // P) * P
STEPS = ET + NWIN - 1
STEPS_PAD = -(-STEPS // P) * P
PAD_DST = NPAD - 1
VW = HD + 1
ROW = D + HEADS * VW
QREC = HD + P
FAR = 1.0e30
FLOOR = 1.0e20
SCALE = 1.0 / HD ** 0.5
SPC = STEPS_PAD // P
EPS = 1e-5
E, H = 8, 1024
KD, KH = D // P, H // P
GREC = 2 * KD + KH
MT = (2 * NPAD + E * (P - 1)) // P


def wait(eng, sem, value):
    if not (isinstance(value, int) and value <= 0):
        eng.wait_ge(sem, value)


class Step:

    def __init__(self, turn, at, period=4):
        self.period = period
        self.turn = turn + at // period
        self.slot = at % period
        self.n = turn * period + at
        self.par = self.slot % 2
        self.base, self.at = turn, at

    @property
    def quad(self):
        return self.period // 4 * self.turn + self.slot // 4

    @property
    def half(self):
        return 2 * self.turn + self.slot // 2

    def __add__(self, k):
        return Step(self.base, self.at + k, self.period)

    def __sub__(self, k):
        return self + (-k)


def tiles(op):
    return lambda t: op(t) if not isinstance(t.n, int) or 0 <= t.n < NT else None


def walk(eng, first, last, body, period=4, head=1, tail=0):
    start = head
    lead = start * period + first
    turns = (last + 1 - tail - lead) // period
    if turns < 2:
        for n in range(first, last + 1):
            body(Step(0, n, period))
        return
    for n in range(first, lead):
        body(Step(0, n, period))
    with eng.Fori(start, start + turns) as turn:
        for k in range(period):
            body(Step(turn, first + k, period))
    for n in range(lead + turns * period, last + 1):
        body(Step(0, n, period))


def four_values(nc, row, largest):
    return nc.values_load_multi_w_load_instructions(
        row, engines=[mybir.EngineType.SP], min_val=0, max_val=largest,
        skip_runtime_bounds_check_because="the stage that makes the table keeps it in the range")[1]


class Scope:

    def __init__(self, nc, tag):
        self.nc, self.tag, self.stack, self.sems = nc, tag, ExitStack(), []

    def __enter__(self):
        self.stack.__enter__()
        return self

    def __exit__(self, *a):
        self.nc.clear_and_free_semaphores(self.sems)
        self.nc.all_engine_barrier()
        return self.stack.__exit__(*a)

    def sb(self, name, shape, dt=F32):
        return self.stack.enter_context(self.nc.sbuf_tensor(f"{self.tag}_{name}", shape, dt))

    def ps(self, name, shape):
        bank = self.stack.enter_context(self.nc.psum_tensor(f"{self.tag}_{name}", [P, 512], F32))
        if len(shape) == 2:
            return bank[:, 0:shape[1]]
        return bank[:, 0:shape[1] * shape[2]].rearrange("p (a b) -> p a b", a=shape[1])

    def sem(self, name):
        self.sems.append(self.nc.alloc_semaphore(f"{self.tag}_{name}"))
        return self.sems[-1]

    def block(self):
        return self.nc.Block()


def rows(ap, first, count):
    return ap[bass.ds(first, count), :]


def setup(nc, a, g, s):
    sb, ps, sem = s.sb, s.ps, s.sem
    relt2 = sb("relt2", [P, P])
    wqt = sb("wqt", [P, KD, D])
    qcol = sb("qcol", [P, KD])
    qwide = sb("qwide", [P, KD, P])
    bqc = sb("bqc", [P, KD])
    bkv = sb("bkv", [P, 2 * D])
    cq = sb("cq", [P, KD])
    first = sb("first", [P, ET - 1], I32)
    firstw = sb("firstw", [P, ET - 1], I32)
    key = sb("key", [P, ET - 1])
    keyj = sb("keyj", [P, ET - 1])
    hit = sb("hit", [P, STEPS])
    sno = sb("sno", [P, SPC])
    wno = sb("wno", [P, 2])
    jf = sb("jf", [P, SPC])
    ji = sb("ji", [P, SPC], I32)
    wi = sb("wi", [P, SPC], I32)
    wrow = sb("wrow", [P, STEPS], I32)
    wf = sb("wf", [P, STEPS])
    lastf = sb("lastf", [P, 2])
    lasti = sb("lasti", [P, 2], I32)
    pno, rmi = sb("pno", [P, 1], I32), sb("rmi", [P, 1], I32)
    rec = sb("rec", [P, SPC, 3 * P], I32)
    w32 = sb("w32", [P, SPC])
    near = sb("near", [P, SPC, P])
    rec8 = sb("rec8", [P, SPC // 4, 2, 4, P], I8)
    srcf = sb("srcf", [P, SPC, P])
    pw = ps("pw", [P, 4, P])
    pc = ps("pc", [P, 8])
    pr = ps("pr", [P, 2 * D])
    pidx = [ps(f"pidx{i}", [P, 4, P]) for i in range(2)]
    loaded, first_in, made, zeroed = sem("loaded"), sem("first_in"), sem("made"), sem("zeroed")
    tables_out, tables_in, last_out = sem("tables_out"), sem("tables_in"), sem("last_out")
    recs_in, dt_out, src_ok, r8_ok, pidx_ok = sem("recs_in"), sem("dt_out"), sem("src_ok"), sem("r8_ok"), sem("pidx_ok")
    pe_done, chain, last_ok = sem("pe_done"), sem("chain"), sem("last_ok")
    LOADS = 17

    with s.block() as block:
        @block.sync
        def _(sp):
            load = lambda dst, src: sp.dma_start(dst, src).then_inc(loaded, 16)
            spread = lambda v: v.rearrange("(o n) -> o n", o=1).to_broadcast([P, v.shape[0]])
            sp.dma_start(first[:], spread(a["first"])).then_inc(first_in, 16)
            sp.wait_ge(zeroed, 1)
            for c in range(2):
                load(relt2[c * HD:(c + 1) * HD, c * N_REL:(c + 1) * N_REL], a["relT"])
            load(wqt[:], a["WqT"].rearrange("(c p) k -> p c k", p=P))
            load(g.wq[:], a["Wq"].rearrange("(c p) n -> p c n", p=P))
            load(g.wkv[:, :, 0:D], a["Wk"].rearrange("(c p) n -> p c n", p=P))
            load(g.wkv[:, :, D:2 * D], a["Wv"].rearrange("(c p) n -> p c n", p=P))
            load(qcol[:], a["q_emb"])
            load(bqc[:], a["bq"])
            load(bkv[:, 0:D], spread(a["bk"]))
            load(bkv[:, D:2 * D], spread(a["bv"]))
            load(g.wo[:], a["Wo"].rearrange("(h p) n -> p h n", p=HD))
            load(g.bo[:], spread(a["bo"]))
            load(g.gamma[:], spread(a["gamma"]))
            load(g.beta[:], spread(a["beta"]))
            load(g.br[:], spread(a["br"]))
            load(g.wr[:], a["Wr"].rearrange("(c p) n -> p c n", p=P))
            load(g.b2f[:], a["b2"])
            sp.wait_ge(made, 2)
            sp.dma_start(a["wtab"].rearrange("(p c) -> p c", p=P), wi[:]).then_inc(tables_out, 16)
            sp.wait_ge(tables_out, 16)
            sp.dma_start(wrow[:], spread(a["wtab"][0:STEPS])).then_inc(tables_in, 16)
            sp.dma_start(g.wreg[0:1, :], a["wtab"].rearrange("(o n) -> o n", o=1)).then_inc(tables_in, 16)
            sp.wait_ge(last_ok, 1)
            sp.dma_start(a["lasttab"].rearrange("(p c) -> p c", p=P), lasti[:]).then_inc(last_out, 16)
            sp.wait_ge(last_out, 16)
            sp.dma_start(g.lastreg[0:1, :], a["lasttab"][0:NWIN].rearrange("(o n) -> o n", o=1)).then_inc(tables_in, 16)
            sp.wait_ge(r8_ok, 1)
            sp.dma_start(a["dts"].rearrange("(p g) k -> p (g k)", p=P), rec8[:].rearrange("p g k c e -> p (g k c e)")).then_inc(dt_out, 16)
            sp.wait_ge(dt_out, 16)
            sp.wait_ge(tables_in, 48)

        @block.gpsimd
        def _(pool):
            made_of = [0]

            def link(ins):
                made_of[0] += 1
                ins.then_inc(g.gp, 1)
                pool.wait_ge(g.gp, made_of[0])
            imprecise = dict(allow_small_or_imprecise_dtypes=True)
            link(pool.iota(sno[:], pattern=[[1, SPC]], base=0, channel_multiplier=SPC, **imprecise))
            link(pool.iota(keyj[:], pattern=[[1, ET - 1]], base=1, channel_multiplier=0, **imprecise))
            link(pool.iota(wno[:], pattern=[[1, 2]], base=0, channel_multiplier=2, **imprecise))
            link(pool.iota(pno[:], pattern=[[0, 1]], base=0, channel_multiplier=1))
            link(pool.iota(g.tileno[:], pattern=[[1, MT]], base=0, channel_multiplier=0, **imprecise))
            link(pool.iota(g.iota8[:], pattern=[[1, E]], base=0, channel_multiplier=0, **imprecise))
            link(pool.memset(g.ident[:], 0.0))
            link(pool.memset(g.tri[:], 1.0))
            link(pool.affine_select(out=g.ident[:], in_=g.ident[:], compare_op=ALU.not_equal, fill=1.0, base=0,
                                    pattern=[[-1, P]], channel_multiplier=1))
            link(pool.affine_select(out=g.tri[:], in_=g.tri[:], compare_op=ALU.is_gt, fill=0.0, base=0,
                                    pattern=[[1, P]], channel_multiplier=-1))
            pool.wait_ge(made, 1)
            for c in range(SPC):
                pool.indirect_dma_start(out=rec[:, c, :], out_offset=None, in_=a["edges"],
                                        in_offset=bass.IndirectOffsetOnAxis(ap=ji[:, c:c + 1], axis=0)).then_inc(recs_in, 16)

        @block.vector
        def _(v):
            v.memset(relt2[:], 0.0).then_inc(zeroed, 1)
            v.memset(g.ones[:], 1.0).then_inc(zeroed, 1)
            v.memset(g.eps[:], EPS).then_inc(zeroed, 1)
            done = [0]

            def link(ins):
                done[0] += 1
                ins.then_inc(chain, 1)
                v.wait_ge(chain, done[0])
            v.wait_ge(first_in, 16)
            v.wait_ge(g.gp, 10)
            link(v.tensor_single_scalar(firstw[:], first[:], 5, ALU.arith_shift_right))
            link(v.tensor_tensor(key[:], firstw[:], keyj[:], ALU.add))
            for c in range(SPC):
                link(v.tensor_scalar(hit[:, 0:ET - 1], key[:], sno[:, c:c + 1], 0.0, ALU.is_le, ALU.add, accum_out=jf[:, c:c + 1]))
            v.tensor_copy(ji[:], jf[:]).then_inc(made, 1)
            link(v.tensor_tensor(wi[:], sno[:], jf[:], ALU.subtract))
            v.tensor_scalar(wi[:], wi[:], float(NWIN - 1), None, ALU.min).then_inc(made, 1)
            link(v.tensor_single_scalar(rmi[:], pno[:], N_REL - 1, ALU.bitwise_and))
            link(v.tensor_copy(g.rmod[:], rmi[:]))
            v.wait_ge(loaded, 16 * LOADS)
            v.wait_ge(zeroed, 3)
            v.tensor_scalar(relt2[:], relt2[:], 0.2, None, ALU.mult).then_inc(zeroed, 1)
            for c in range(KD):
                v.tensor_scalar(qwide[:, c, :], g.ones[:], qcol[:, c:c + 1], 0.1, ALU.mult, ALU.mult).then_inc(zeroed, 1)
            v.wait_ge(pe_done, 1)
            link(v.tensor_copy(g.wqr[:].rearrange("p k (c n) -> p k c n", c=2),
                               pw[:].rearrange("p (k c) n -> p k c n", c=2)))
            v.wait_ge(pe_done, 2)
            link(v.tensor_tensor(cq[:], pc[:, 0:2], bqc[:], ALU.add))
            v.tensor_scalar(g.ncq[:], cq[:], -SCALE, None, ALU.mult).then_inc(made, 1)
            link(v.tensor_tensor(g.ckv[:], pr[:], bkv[:], ALU.add))
            v.wait_ge(pe_done, 3)
            link(v.tensor_scalar(g.ncqr[:], pc[:, 4:6], -SCALE, None, ALU.mult))
            v.wait_ge(tables_in, 32)
            link(v.tensor_copy(wf[:], wrow[:]))
            link(v.tensor_tensor(hit[:, 1:STEPS], wf[:, 1:STEPS], wf[:, 0:STEPS - 1], ALU.not_equal))
            link(v.tensor_scalar(g.fresh[:, 1:STEPS], hit[:, 1:STEPS], FAR, None, ALU.mult))
            link(v.memset(g.fresh[:, 0:1], FAR))
            for c in range(2):
                link(v.tensor_scalar(hit[:], wf[:], wno[:, c:c + 1], -1.0, ALU.is_le, ALU.add, accum_out=lastf[:, c:c + 1]))
            v.tensor_copy(lasti[:], lastf[:]).then_inc(last_ok, 1)
            v.wait_ge(recs_in, 16 * SPC)
            v.tensor_copy(srcf[:], rec[:, :, 0:P]).then_inc(src_ok, 1)
            link(v.tensor_scalar(w32[:], wi[:], float(WIN), -1.0, ALU.mult, ALU.add))
            for c in range(SPC):
                link(v.tensor_scalar(near[:, c, :], rec[:, c, P:2 * P], w32[:, c:c + 1], 0.0, ALU.subtract, ALU.max))
            for i in range(SPC // 4):
                link(v.tensor_scalar(rec8[:, i, 1, :, :], near[:, 4 * i:4 * i + 4, :], float(WIN + 1), None, ALU.min))
                last = v.tensor_copy(rec8[:, i, 0, :, :], rec[:, 4 * i:4 * i + 4, 2 * P:3 * P])
            last.then_inc(r8_ok, 1)
            for i in range(2):
                v.wait_ge(pidx_ok, i + 1)
                v.tensor_copy(g.idx[:].rearrange("e (p c) -> e c p", c=SPC)[:, 4 * i:4 * i + 4, :], pidx[i])

        @block.tensor
        def _(pe):
            pe.wait_ge(zeroed, 6)
            for k in range(KD):
                for c in range(2):
                    last = nc.tensor.matmul(pw[:, 2 * k + c, :], wqt[:, c, k * P:(k + 1) * P], relt2[:], start=True, stop=True)
            last.then_inc(pe_done, 1)
            for c in range(2):
                for k in range(KD):
                    last = nc.tensor.matmul(pc[:, c:c + 1], g.wq[:, k, c * P:(c + 1) * P], qwide[:, k, 0:1],
                                            start=(k == 0), stop=(k == KD - 1))
            for k in range(KD):
                last = nc.tensor.matmul(pr[:], qwide[:, k, :], g.wkv[:, k, :], start=(k == 0), stop=(k == KD - 1))
            last.then_inc(pe_done, 1)
            pe.wait_ge(made, 3)
            for c in range(2):
                last = nc.tensor.matmul(pc[:, 4 + c:5 + c], relt2[:], cq[:, c:c + 1], start=True, stop=True)
            last.then_inc(pe_done, 1)
            pe.wait_ge(src_ok, 1)
            for c in range(SPC):
                last = nc.tensor.transpose(pidx[c // 4][:, c % 4, :], srcf[:, c, :], g.ident[:])
                if c % 4 == 3:
                    last.then_inc(pidx_ok, 1)


def nodes(nc, a, g, s):
    sb, ps, sem = s.sb, s.ps, s.sem
    four = range(4)
    xin = [sb(f"xin{i}", [P, D]) for i in four]
    x1s = [sb(f"x1s{i}", [P, D]) for i in four]
    stats = [sb(f"stats{i}", [P, 6]) for i in four]
    mv = [sb(f"mv{i}", [P, 2]) for i in four]
    sd = [sb(f"sd{i}", [P, 1]) for i in four]
    rs = [sb(f"rs{i}", [P, 1]) for i in four]
    xT = [sb(f"xT{i}", [P, KD, P]) for i in four]
    kv = [sb(f"kv{i}", [P, ROW]) for i in four]
    qo = [sb(f"qo{i}", [P, WPT, QREC]) for i in four]
    zero = sb("zero", [P, 2, D])
    pen = sb("pen", [P, HEADS, WIN])
    pT = [ps(f"pT{i}", [P, KD, P]) for i in range(2)]
    pkv = [ps(f"pkv{i}", [P, 2 * D]) for i in range(2)]
    pq = [ps(f"pq{i}", [P, 4, P]) for i in range(2)]
    x_in = [sem(f"x_in{i}") for i in four]
    stats_ok, mv_ok, sd_ok, rs_ok, x1_ok = sem("stats_ok"), sem("mv_ok"), sem("sd_ok"), sem("rs_ok"), sem("x1_ok")
    pT_ok, xT_ok, pkv_ok, pq_ok = sem("pT_ok"), sem("xT_ok"), sem("pkv_ok"), sem("pq_ok")
    kv_ok, qo_ok, ones_ok, x1_kept = sem("kv_ok"), sem("qo_ok"), sem("ones_ok"), sem("x1_kept")
    pen_ok, pen_in, zero_ok, xs_clear = sem("pen_ok"), sem("pen_in"), sem("zero_ok"), sem("xs_clear")
    x1_seen = sem("x1_seen")
    kv_out = [sem(f"kv_out{i}") for i in four]
    qo_out = [sem(f"qo_out{i}") for i in four]
    dve_seen = sem("dve_seen")

    with s.block() as block:
        @block.sync
        def _(sp):
            @tiles
            def load(t):
                wait(sp, x1_ok, t.n - 3)
                sp.dma_start(xin[t.slot][:], rows(a["x"], t.n * P, P)).then_inc(x_in[t.slot], 16)

            @tiles
            def store(t):
                sp.wait_ge(kv_ok, t.n + 1)
                sp.dma_start(rows(a["kvtab"], t.n * P, P), kv[t.slot][:]).then_inc(kv_out[t.slot], 16)
                sp.wait_ge(qo_ok, t.n + 1)
                sp.dma_start(a["qtab"][bass.ds(t.n * WPT, WPT), :, :].rearrange("w p n -> p w n"), qo[t.slot][:]).then_inc(qo_out[t.slot], 16)

            def clear(first, count):
                sp.dma_start(rows(a["xs"], first * P, count * P).rearrange("(t p) d -> p t d", p=P), zero[:, 0:count, :]).then_inc(xs_clear, 16)

            @tiles
            def clear_two(t):
                clear(t.n * 2, 2)

            def both(t):
                load(t + 3)
                store(t - 3)
                clear_two(t)
            sp.wait_ge(pen_in, 4 * WPT)
            sp.wait_ge(zero_ok, 1)
            walk(sp, -3, NT + 2, both, head=3, tail=6)
            for first in range(2 * NT, MT, 2):
                clear(first, min(2, MT - first))
            sp.wait_ge(xs_clear, 16 * (-(-MT // 2)))
            for i in four:
                n = (NT + 3 - i) // 4
                sp.wait_ge(kv_out[i], 16 * n)
                sp.wait_ge(qo_out[i], 16 * n)

        @block.vector
        def _(v):
            v.memset(zero[:], 0.0).then_inc(zero_ok, 1)
            for i in four:
                v.memset(kv[i][:, D:ROW], 1.0).then_inc(ones_ok, 1)
            v.wait_ge(ones_ok, 4)
            v.wait_ge(pen_ok, 2)
            for i in four:
                for w in range(WPT):
                    v.tensor_copy(qo[i][HD:P, w, HD:QREC], pen[HD:P, :, :].rearrange("p h n -> p (h n)")).then_inc(pen_in, 1)
            v.wait_ge(pen_in, 4 * WPT)

            @tiles
            def stats_of(t):
                v.wait_ge(x_in[t.slot], t.turn * 16 + 16)
                v.bn_stats(stats[t.slot][:], xin[t.slot][:]).then_inc(stats_ok, 1)

            @tiles
            def mv_of(t):
                v.wait_ge(stats_ok, t.n + 1)
                v.sem_inc(dve_seen, 1)
                v.bn_aggr(mv[t.slot][:], stats[t.slot][:]).then_inc(mv_ok, 1)

            @tiles
            def rs_of(t):
                v.wait_ge(sd_ok, t.n + 1)
                v.reciprocal(rs[t.slot][:], sd[t.slot][:]).then_inc(rs_ok, 1)

            @tiles
            def x1_of(t):
                b = t.slot
                v.wait_ge(rs_ok, t.n + 1)
                wait(v, pT_ok, t.n - 3)
                wait(v, x1_kept, t.n - 3)
                v.tensor_scalar(x1s[b][:], xin[b][:], mv[b][:, 0:1], rs[b][:, 0:1],
                                ALU.subtract, ALU.mult).then_inc(x1_ok, 1)

            @tiles
            def keep(t):
                b, p = t.slot, t.par
                v.wait_ge(pkv_ok, t.n + 1)
                wait(v, kv_out[b], t.turn * 16)
                v.tensor_tensor(kv[b][:, 0:D], pkv[p][:, 0:D], g.ckv[:, 0:D], ALU.add)
                v.tensor_tensor(kv[b][:, D:ROW].rearrange("p (h e) -> p h e", e=VW)[:, :, 0:HD],
                                pkv[p][:, D:2 * D].rearrange("p (h d) -> p h d", d=HD),
                                g.ckv[:, D:2 * D].rearrange("p (h d) -> p h d", d=HD), ALU.add).then_inc(kv_ok, 1)

            def body(t):
                rs_of(t - 1)
                stats_of(t)
                x1_of(t - 1)
                mv_of(t)
                keep(t - 3)
            walk(v, 0, NT + 2, body, head=2, tail=3)

        @block.gpsimd
        def _(pool):
            pool.memset(pen[:], FAR).then_inc(pen_ok, 1)
            pool.wait_ge(pen_ok, 1)
            pool.affine_select(out=pen[:], in_=pen[:], compare_op=ALU.not_equal, fill=0.0, base=-(HD + 1),
                               pattern=[[0, HEADS], [-1, WIN]], channel_multiplier=1).then_inc(pen_ok, 1)

            def keep(t):
                pool.wait_ge(x1_ok, t.n + 1)
                pool.sem_inc(x1_seen, 1)
                pool.tensor_tensor(g.x1[:, bass.ds(t.n * D, D)], x1s[t.slot][:], g.bo[:], ALU.add).then_inc(x1_kept, 1)
            walk(pool, 0, NT - 1, keep)

        @block.scalar
        def _(act):
            @tiles
            def sd_of(t):
                act.wait_ge(mv_ok, t.n + 1)
                act.activation(sd[t.slot][:], mv[t.slot][:, 1:2], ACT.Sqrt, bias=g.eps[:, 0:1]).then_inc(sd_ok, 1)

            @tiles
            def xT_of(t):
                act.wait_ge(pT_ok, t.n + 1)
                wait(act, pq_ok, t.n - 3)
                act.activation(xT[t.slot][:], pT[t.par][:], ACT.Copy).then_inc(xT_ok, 1)

            @tiles
            def q_of(t):
                b, p = t.slot, t.par
                act.wait_ge(pq_ok, t.n + 1)
                wait(act, qo_out[b], t.turn * 16)
                for c in range(2):
                    act.activation(qo[b][:, :, c * WIN:(c + 1) * WIN], pq[p][:, c, :].rearrange("p (w n) -> p w n", n=WIN),
                                   ACT.Identity, bias=g.ncq[:, c:c + 1], scale=-SCALE)
                for h in range(HEADS):
                    c, half = h // 2, slice(h % 2 * HD, (h % 2 + 1) * HD)
                    last = act.activation(qo[b][0:HD, :, HD + h * WIN:HD + (h + 1) * WIN],
                                          pq[p][half, 2 + c, :].rearrange("p (w n) -> p w n", n=WIN),
                                          ACT.Identity, bias=g.ncqr[half, c:c + 1], scale=-SCALE)
                last.then_inc(qo_ok, 1)

            def body(t):
                q_of(t - 3)
                sd_of(t)
                xT_of(t - 1)
            walk(act, 0, NT + 2, body, head=2, tail=3)

        @block.tensor
        def _(pe):
            @tiles
            def turn_x(t):
                pe.wait_ge(x1_ok, t.n + 1)
                wait(pe, xT_ok, t.n - 1)
                for c in range(KD):
                    last = nc.tensor.transpose(pT[t.par][:, c, :], x1s[t.slot][:, c * P:(c + 1) * P], g.ident[:])
                last.then_inc(pT_ok, 1)

            @tiles
            def products(t):
                b, p = t.slot, t.par
                pe.wait_ge(xT_ok, t.n + 1)
                wait(pe, kv_ok, t.n - 1)
                for k in range(KD):
                    last = nc.tensor.matmul(pkv[p][:], xT[b][:, k, :], g.wkv[:, k, :], start=(k == 0), stop=(k == KD - 1))
                last.then_inc(pkv_ok, 1)
                wait(pe, qo_ok, t.n - 1)
                for m in range(4):
                    w = g.wq if m < 2 else g.wqr
                    for k in range(KD):
                        last = nc.tensor.matmul(pq[p][:, m, :], w[:, k, (m % 2) * P:(m % 2 + 1) * P], xT[b][:, k, :],
                                                start=(k == 0), stop=(k == KD - 1))
                last.then_inc(pq_ok, 1)

            def body(t):
                products(t - 2)
                turn_x(t - 1)
            walk(pe, 1, NT + 1, body, head=2, tail=2)


def edges(nc, a, g, s):
    sb, ps, sem = s.sb, s.ps, s.sem
    two, four, eight = range(2), range(4), range(8)
    ix = [sb(f"ix{i}", [P, 4], I32) for i in two]
    dt = [sb(f"dt{i}", [P, 4, P], I8) for i in two]
    qc = [sb(f"qc{i}", [P, QREC]) for i in eight]
    q = [sb(f"q{i}", [P, 2, 2, WIN]) for i in four]
    kv = [sb(f"kv{i}", [P, ROW]) for i in range(16)]
    kT = [sb(f"kT{i}", [P, KD, P]) for i in four]
    rel = [sb(f"rel{i}", [P, P]) for i in four]
    mx = [sb(f"mx{i}", [P, 1]) for i in two]
    nm = [sb(f"nm{i}", [P, 1]) for i in two]
    old = [sb(f"old{i}", [P, 1]) for i in two]
    cor = [sb(f"cor{i}", [P, 1]) for i in four]
    pr = [sb(f"pr{i}", [P, P]) for i in two]
    prT = [sb(f"prT{i}", [P, P]) for i in two]
    acc = sb("acc", [P, 8, VW])
    pk = [ps(f"pk{i}", [P, KD, P]) for i in two]
    psc = [ps(f"psc{i}", [P, P]) for i in two]
    ppT = [ps(f"ppT{i}", [P, P]) for i in two]
    pav = [ps(f"pav{i}", [P, VW]) for i in two]
    dt_in = [sem(f"dt_in{i}") for i in two]
    acc_out = [sem(f"acc_out{i}") for i in two]
    q_in = [sem(f"q_in{i}") for i in eight]
    kv_in = [sem(f"kv_in{i}") for i in range(16)]
    ix_ok, pool_seen, pk_ok, kT_ok, rel_ok, sc_ok = (sem(x) for x in (
        "ix_ok", "pool_seen", "pk_ok", "kT_ok", "rel_ok", "sc_ok"))
    q_clear, upper_ok, lower_ok = sem("q_clear"), sem("upper_ok"), sem("lower_ok")
    mx_ok, nm_ok, old_ok, pr_ok, ppT_ok, prT_ok, av_ok, acc_ok, cor_ok, dve_seen = (sem(x) for x in (
        "mx_ok", "nm_ok", "old_ok", "pr_ok", "ppT_ok", "prT_ok", "av_ok", "acc_ok", "cor_ok", "dve_seen"))
    LAST = STEPS - 1

    def steps(op):
        return lambda t: op(t) if not isinstance(t.n, int) or 0 <= t.n <= LAST else None
    at = lambda n: Step(0, n, 8)

    with s.block() as block:
        @block.sync
        def _(sp):
            def load_q(t, w):
                wait(sp, sc_ok, t.n - 7)
                sp.dma_start(qc[t.slot][:], a["qtab"][bass.ds(w, 1), :, :].rearrange("o p k -> p (o k)")).then_inc(q_in[t.slot], 16)

            def load_dt(t):
                b = t.slot // 4
                wait(sp, rel_ok, t.n - 4)
                sp.dma_start(dt[b][:].rearrange("p c e -> p (c e)"),
                             a["dts"][bass.ds(t.quad, 1), :].rearrange("o (k e) -> (o k) e", k=2)[:, None, :].to_broadcast([2, HD, 4 * P])).then_inc(dt_in[b], 16)

            def store(t, n=4):
                b = t.slot // 4
                sp.wait_ge(acc_ok, t.n + 1 + n)
                sp.dma_start(a["acctab"][:, bass.ds(t.n * VW, n * VW)], acc[:, 4 * b:4 * b + n, :].rearrange("p s e -> p (s e)")).then_inc(acc_out[b], 16)

            windows = []

            def body(t):
                if t.slot % 4 == 0:
                    windows[:] = four_values(nc, g.wreg[0:1, bass.ds(t.n, 4)], NWIN - 1)
                    load_dt(t)
                load_q(t, windows[t.slot % 4])
                if t.slot % 4 == 3:
                    steps(store)(t - 15)
            walk(sp, 0, LAST, body, period=8, head=2)
            assert LAST % 4 == 1
            for n in (13, 9, 5):
                store(at(LAST - n))
            store(at(LAST - 1), 2)
            for b in two:
                sp.wait_ge(acc_out[b], 16 * ((LAST // 4 + 2 - b) // 2))

        @block.gpsimd
        def _(pool):
            def gather(t):
                half = t.slot // 4 % 2
                if t.slot % 4 == 0:
                    read = t - 5
                    wait(pool, kv_in[read.slot], read.turn * 16 + 16)
                    if not (isinstance(t.n, int) and t.n < 8):
                        pool.sem_inc(pool_seen, 1)
                    pool.tensor_copy(ix[half][:], g.idx[:, bass.ds(t.n, 4)]).then_inc(ix_ok, 1)
                    pool.wait_ge(ix_ok, t.quad + 1)
                    pool.sem_inc(pool_seen, 1)
                wait(pool, av_ok, t.n - 15)
                if not (isinstance(t.n, int) and t.n < 16):
                    pool.sem_inc(pool_seen, 1)
                pool.indirect_dma_start(out=kv[t.slot][:], out_offset=None, in_=a["kvtab"],
                                        in_offset=bass.IndirectOffsetOnAxis(ap=ix[half][:, t.slot % 4:t.slot % 4 + 1], axis=0)).then_inc(kv_in[t.slot], 16)
            walk(pool, 0, LAST, gather, period=16)

        @block.vector
        def _(v):
            v.memset(acc[:, 7, :], 0.0).then_inc(acc_ok, 1)
            v.memset(nm[1][:], 0.0).then_inc(nm_ok, 1)
            for i in four:
                v.memset(q[i][:], 0.0).then_inc(q_clear, 1)
            v.wait_ge(q_clear, 4)

            def masks(t):
                b, p = t.slot // 4, t.slot % 4
                if t.slot % 4 == 0:
                    v.wait_ge(dt_in[b], t.turn * 16 + 16)
                wait(v, sc_ok, t.n - 3)
                v.tensor_scalar(rel[p][:], dt[b][:, p, :], g.rmod[:, 0:1], None, ALU.is_equal).then_inc(rel_ok, 1)

            def upper(t):
                v.wait_ge(q_in[t.slot], t.turn * 16 + 16)
                wait(v, sc_ok, t.n - 3)
                v.tensor_copy(q[t.slot % 4][0:HD, :, 0, :], qc[t.slot][0:HD, 0:HD].rearrange("p (c n) -> p c n", n=WIN)).then_inc(upper_ok, 1)

            def maxima(t):
                p = t.par
                wait(v, cor_ok, t.n - 1)
                v.wait_ge(nm_ok, t.n + 1)
                v.tensor_scalar(old[p][:], nm[1 - p][:], g.fresh[:, bass.ds(t.n, 1)], None, ALU.add).then_inc(old_ok, 1)
                v.wait_ge(sc_ok, t.n + 1)
                v.tensor_reduce(mx[p][:], psc[p][:], AX.X, ALU.min).then_inc(mx_ok, 1)
                v.wait_ge(mx_ok, t.n + 1)
                v.scalar_tensor_tensor(out=nm[p][:], in0=mx[p][:], scalar=FLOOR, in1=old[p][:], op0=ALU.min, op1=ALU.min).then_inc(nm_ok, 1)

            def add(t):
                p = t.par
                if t.slot % 4 == 0:
                    wait(v, acc_out[t.slot // 4], t.turn * 16)
                v.wait_ge(av_ok, t.n + 1)
                v.wait_ge(acc_ok, t.n + 1)
                v.scalar_tensor_tensor(out=acc[:, t.slot, :], in0=acc[:, (t.slot - 1) % 8, :], scalar=cor[t.slot % 4][:, 0:1],
                                       in1=pav[p][:], op0=ALU.mult, op1=ALU.add).then_inc(acc_ok, 1)

            for n in two:
                upper(at(n))
                masks(at(n))

            @steps
            def prepare(t):
                upper(t)
                masks(t)

            def body(t):
                steps(add)(t - 3)
                prepare(t + 2)
                steps(maxima)(t)
            walk(v, 0, LAST + 3, body, period=8, tail=5)

        @block.scalar
        def _(act):
            def k_of(t):
                act.wait_ge(pk_ok, t.n + 1)
                wait(act, sc_ok, t.n - 3)
                act.activation(kT[t.slot % 4][:], pk[t.par][:], ACT.Copy).then_inc(kT_ok, 1)

            def lower(t):
                act.wait_ge(q_in[t.slot], t.turn * 16 + 16)
                wait(act, sc_ok, t.n - 3)
                act.activation(q[t.slot % 4][HD:P, :, 1, :], qc[t.slot][HD:P, 0:HD].rearrange("p (c n) -> p c n", n=WIN), ACT.Copy).then_inc(lower_ok, 1)

            def weights(t):
                p = t.par
                act.wait_ge(nm_ok, t.n + 2)
                wait(act, ppT_ok, t.n - 1)
                act.activation(pr[p][:], psc[p][:], ACT.Exp, bias=nm[p][:, 0:1], scale=-1.0).then_inc(pr_ok, 1)
                wait(act, acc_ok, t.n - 2)
                act.activation(cor[t.slot % 4][:], old[p][:], ACT.Exp, bias=nm[p][:, 0:1], scale=-1.0).then_inc(cor_ok, 1)

            def w_of(t):
                act.wait_ge(ppT_ok, t.n + 1)
                wait(act, av_ok, t.n - 1)
                act.activation(prT[t.par][:], ppT[t.par][:], ACT.Copy).then_inc(prT_ok, 1)

            act.wait_ge(q_clear, 4)
            for n in two:
                lower(at(n))
                k_of(at(n))

            def body(t):
                steps(lower)(t + 2)
                steps(k_of)(t + 2)
                steps(w_of)(t - 1)
                steps(weights)(t)
            walk(act, 0, LAST + 1, body, period=8, tail=4)

        @block.tensor
        def _(pe):
            def turn_k(t):
                b = t.slot
                pe.wait_ge(kv_in[b], t.turn * 16 + 16)
                wait(pe, kT_ok, t.n - 1)
                for c in range(KD):
                    last = nc.tensor.transpose(pk[t.par][:, c, :], kv[b][:, c * P:(c + 1) * P], g.ident[:])
                last.then_inc(pk_ok, 1)

            def scores(t):
                b, p = t.slot % 4, t.par
                pe.wait_ge(upper_ok, t.n + 1)
                pe.wait_ge(lower_ok, t.n + 1)
                pe.wait_ge(rel_ok, t.n + 1)
                wait(pe, pr_ok, t.n - 1)
                nc.tensor.matmul(psc[p][:], qc[t.slot % 8][:, HD:QREC], rel[b][:], start=True, stop=True)
                pe.wait_ge(kT_ok, t.n + 1)
                for c in range(KD):
                    last = nc.tensor.matmul(psc[p][c * HD:(c + 1) * HD, :], q[b][:, c, :, :].rearrange('p h n -> p (h n)'), kT[t.slot % 4][:, c, :],
                                            start=False, stop=True, tile_position=(0, c * HD), skip_group_check=True)
                last.then_inc(sc_ok, 1)

            def turn_w(t):
                pe.wait_ge(pr_ok, t.n + 1)
                wait(pe, prT_ok, t.n - 1)
                nc.tensor.transpose(ppT[t.par][:], pr[t.par][:], g.ident[:]).then_inc(ppT_ok, 1)

            def sums(t):
                p = t.par
                pe.wait_ge(prT_ok, t.n + 1)
                wait(pe, acc_ok, t.n)
                for h in range(HEADS):
                    last = nc.tensor.matmul(pav[p][h * WIN:(h + 1) * WIN, :], prT[p][:, h * WIN:(h + 1) * WIN],
                                            kv[t.slot][:, D + h * VW:D + (h + 1) * VW], start=True, stop=True,
                                            tile_position=(0, h * WIN))
                last.then_inc(av_ok, 1)

            turn_k(Step(0, 0, 16))
            turn_k(Step(0, 1, 16))

            def body(t):
                steps(turn_k)(t + 2)
                steps(scores)(t)
                steps(turn_w)(t - 1)
                steps(sums)(t - 2)
            walk(pe, 0, LAST + 2, body, period=16, tail=5)


def post(nc, a, g, s):
    sb, ps, sem = s.sb, s.ps, s.sem
    two, four = range(2), range(4)
    xin = [sb(f"xin{i}", [P, D]) for i in four]
    vin = [sb(f"vin{i}", [P, WPT, HD]) for i in four]
    st = [sb(f"st{i}", [P, WPT, VW]) for i in four]
    none = [sb(f"none{i}", [P, WPT]) for i in four]
    den = [sb(f"den{i}", [P, WPT]) for i in four]
    rden = [sb(f"rden{i}", [P, WPT]) for i in four]
    msg = [sb(f"msg{i}", [P, WPT, HD]) for i in four]
    alt = [sb(f"alt{i}", [P, WPT, HD]) for i in four]
    mT = [sb(f"mT{i}", [HD, HEADS, P]) for i in four]
    y = [sb(f"y{i}", [P, D]) for i in four]
    yn = [sb(f"yn{i}", [P, D]) for i in four]
    yg = [sb(f"yg{i}", [P, D]) for i in four]
    x2 = [sb(f"x2{i}", [P, D]) for i in four]
    z = [sb(f"z{i}", [P, D]) for i in four]
    zT = [sb(f"zT{i}", [P, KD, P]) for i in four]
    stats = [sb(f"stats{i}", [P, 6]) for i in four]
    mv = [sb(f"mv{i}", [P, 2]) for i in four]
    sd = [sb(f"sd{i}", [P, 1]) for i in four]
    rs = [sb(f"rs{i}", [P, 1]) for i in four]
    stats2 = [sb(f"stats2{i}", [P, 6]) for i in four]
    mv2 = [sb(f"mv2{i}", [P, 2]) for i in four]
    sd2 = [sb(f"sd2{i}", [P, 1]) for i in four]
    rs2 = [sb(f"rs2{i}", [P, 1]) for i in four]
    sd3 = [sb(f"sd3{i}", [P, 1]) for i in four]
    rs3 = [sb(f"rs3{i}", [P, 1]) for i in four]
    vz = [sb(f"vz{i}", [P, 1]) for i in four]
    lg = [sb(f"lg{i}", [P, E]) for i in four]
    t8 = [sb(f"t8{i}", [P, E]) for i in four]
    i8 = [sb(f"i8{i}", [P, E], U32) for i in four]
    pm = [ps(f"pm{i}", [P, 4, P]) for i in two]
    po = [ps(f"po{i}", [P, D]) for i in two]
    pz = [ps(f"pz{i}", [P, KD, P]) for i in two]
    pl = [ps(f"pl{i}", [P, E]) for i in two]
    x_in = [sem(f"x_in{i}") for i in four]
    v_in = [sem(f"v_in{i}") for i in four]
    st_in = [sem(f"st_in{i}") for i in four]
    x2_out = [sem(f"x2_out{i}") for i in four]
    names = ("none", "den", "rden", "msg", "alt", "mix", "pm", "mT", "po", "y", "stats", "mv", "sd", "rs", "yn", "yg",
             "yb2", "x2", "stats2", "mv2", "sd2", "rs2", "z", "vz", "sd3", "rs3", "xn", "pz", "zT", "pl", "lg", "t8", "i8", "keep", "x1s", "seen")
    o = {n: sem(n + "_ok") for n in names}
    dve_seen, pe_seen = sem("dve_seen"), sem("pe_seen")
    with s.block() as block:
        @block.sync
        def _(sp):
            @tiles
            def load_sums(t):
                wait(sp, o["msg"], t.n - 3)
                lasts = four_values(nc, g.lastreg[0:1, bass.ds(t.n * WPT, WPT)], STEPS - 1)
                for w, last in enumerate(lasts):
                    sp.dma_start(st[t.slot][:, w, :], a["acctab"][:, bass.ds(last * VW, VW)]).then_inc(st_in[t.slot], 16)

            walk(sp, 0, NT - 1, load_sums)

        @block.vector
        def _(v):
            @tiles
            def none_of(t):
                v.wait_ge(st_in[t.slot], t.turn * (16 * WPT) + 16 * WPT)
                v.tensor_scalar(none[t.slot][:], st[t.slot][:, :, HD], 0.0, None, ALU.is_equal).then_inc(o["none"], 1)

            @tiles
            def den_of(t):
                v.wait_ge(o["none"], t.n + 1)
                v.tensor_tensor(den[t.slot][:], st[t.slot][:, :, HD], none[t.slot][:], ALU.add).then_inc(o["den"], 1)

            @tiles
            def rden_of(t):
                v.wait_ge(o["den"], t.n + 1)
                v.reciprocal(rden[t.slot][:], den[t.slot][:]).then_inc(o["rden"], 1)

            @tiles
            def alt_of(t):
                b = t.slot
                v.wait_ge(v_in[b], t.turn * (16 * HEADS) + 16 * HEADS)
                v.tensor_tensor(alt[b][:], vin[b][:], none[b][:, :, None].to_broadcast([P, WPT, HD]), ALU.mult).then_inc(o["alt"], 1)

            @tiles
            def msg_of(t):
                b = t.slot
                v.wait_ge(o["rden"], t.n + 1)
                wait(v, o["pm"], t.n - 3)
                v.tensor_tensor(msg[b][:], st[b][:, :, 0:HD], rden[b][:, :, None].to_broadcast([P, WPT, HD]), ALU.mult).then_inc(o["msg"], 1)

            @tiles
            def mix_of(t):
                b = t.slot
                v.wait_ge(o["msg"], t.n + 1)
                v.wait_ge(o["alt"], t.n + 1)
                v.tensor_tensor(msg[b][:], msg[b][:], alt[b][:], ALU.add).then_inc(o["mix"], 1)

            @tiles
            def y_of(t):
                v.wait_ge(o["po"], t.n + 1)
                v.tensor_tensor(y[t.slot][:], po[t.par], g.x1[:, bass.ds(t.n * D, D)], ALU.add).then_inc(o["y"], 1)

            @tiles
            def stats_of(t):
                v.wait_ge(o["y"], t.n + 1)
                v.bn_stats(stats[t.slot][:], y[t.slot][:]).then_inc(o["stats"], 1)

            @tiles
            def mv_of(t):
                v.wait_ge(o["stats"], t.n + 1)
                v.sem_inc(dve_seen, 1)
                v.bn_aggr(mv[t.slot][:], stats[t.slot][:]).then_inc(o["mv"], 1)

            @tiles
            def rs_of(t):
                v.wait_ge(o["sd"], t.n + 1)
                v.reciprocal(rs[t.slot][:], sd[t.slot][:]).then_inc(o["rs"], 1)

            @tiles
            def yn_of(t):
                b = t.slot
                v.wait_ge(o["rs"], t.n + 1)
                wait(v, o["yg"], t.n - 3)
                v.tensor_scalar(yn[b][:], y[b][:], mv[b][:, 0:1], rs[b][:, 0:1], ALU.subtract, ALU.mult).then_inc(o["yn"], 1)

            @tiles
            def stats2_of(t):
                v.wait_ge(o["x2"], t.n + 1)
                v.bn_stats(stats2[t.slot][:], x2[t.slot][:]).then_inc(o["stats2"], 1)

            @tiles
            def mv2_of(t):
                v.wait_ge(o["stats2"], t.n + 1)
                v.sem_inc(dve_seen, 1)
                v.bn_aggr(mv2[t.slot][:], stats2[t.slot][:]).then_inc(o["mv2"], 1)

            @tiles
            def rs2_of(t):
                v.wait_ge(o["sd2"], t.n + 1)
                v.reciprocal(rs2[t.slot][:], sd2[t.slot][:]).then_inc(o["rs2"], 1)

            @tiles
            def z_of(t):
                b = t.slot
                v.wait_ge(o["rs2"], t.n + 1)
                wait(v, o["pz"], t.n - 3)
                v.tensor_scalar(z[b][:], x2[b][:], mv2[b][:, 0:1], rs2[b][:, 0:1], ALU.subtract, ALU.mult).then_inc(o["z"], 1)
                v.tensor_scalar(vz[b][:], mv2[b][:, 1:2], rs2[b][:, 0:1], rs2[b][:, 0:1], ALU.mult, ALU.mult).then_inc(o["vz"], 1)

            @tiles
            def rs3_of(t):
                v.wait_ge(o["sd3"], t.n + 1)
                v.reciprocal(rs3[t.slot][:], sd3[t.slot][:]).then_inc(o["rs3"], 1)

            @tiles
            def xn_of(t):
                v.wait_ge(o["rs3"], t.n + 1)
                v.tensor_scalar(g.x1[:, bass.ds(t.n * D, D)], z[t.slot][:], rs3[t.slot][:, 0:1], None, ALU.mult).then_inc(o["xn"], 1)

            @tiles
            def lg_of(t):
                v.wait_ge(o["pl"], t.n + 1)
                v.tensor_tensor(lg[t.slot][:], pl[t.par], g.br[:], ALU.add).then_inc(o["lg"], 1)

            @tiles
            def t8_of(t):
                v.wait_ge(o["lg"], t.n + 1)
                v.sem_inc(dve_seen, 1)
                v.max(t8[t.slot][:], lg[t.slot][:]).then_inc(o["t8"], 1)

            @tiles
            def i8_of(t):
                b = t.slot
                v.wait_ge(o["t8"], t.n + 1)
                v.sem_inc(dve_seen, 1)
                v.max_index(i8[b][:], t8[b][:], lg[b][:]).then_inc(o["i8"], 1)
                v.tensor_copy(g.top_l[:, bass.ds(t.n * 2, 2)], t8[b][:, 0:2])

            @tiles
            def keep(t):
                v.wait_ge(o["i8"], t.n + 1)
                v.tensor_copy(g.top_i[:, bass.ds(t.n * 2, 2)], i8[t.slot][:, 0:2]).then_inc(o["keep"], 1)

            def body(t):
                none_of(t + 1)
                rs2_of(t - 3)
                rs3_of(t - 4)
                rs_of(t - 1)
                den_of(t + 1)
                z_of(t - 3)
                yn_of(t - 1)
                rden_of(t + 1)
                alt_of(t + 1)
                msg_of(t + 1)
                stats2_of(t - 2)
                xn_of(t - 4)
                mix_of(t + 1)
                mv2_of(t - 2)
                lg_of(t - 4)
                y_of(t)
                t8_of(t - 4)
                stats_of(t)
                i8_of(t - 4)
                mv_of(t)
                keep(t - 4)
            walk(v, -1, NT + 3, body, head=3, tail=5)

        @block.gpsimd
        def _(pool):
            def residual(t):
                b = t.slot
                n1 = t.n + 1
                pool.wait_ge(o["yn"], n1)
                pool.tensor_tensor(yg[b][:], yn[b][:], g.gamma[:], ALU.mult).then_inc(o["yg"], 1)
                pool.wait_ge(o["yg"], n1)
                pool.tensor_tensor(yg[b][:], yg[b][:], g.beta[:], ALU.add).then_inc(o["yb2"], 1)
                pool.wait_ge(o["yb2"], n1)
                pool.sem_inc(o["seen"], 1)
                wait(pool, x2_out[b], t.turn * 16)
                pool.sem_inc(o["seen"], 1)
                wait(pool, o["z"], t.n - 3)
                pool.wait_ge(x_in[b], t.turn * 16 + 16)
                pool.sem_inc(o["seen"], 1)
                pool.tensor_tensor(x2[b][:], yg[b][:], xin[b][:], ALU.add).then_inc(o["x2"], 1)
            walk(pool, 0, NT - 1, residual)

        @block.scalar
        def _(act):
            @tiles
            def load_x(t):
                wait(act, o["x2"], t.n - 3)
                act.dma_start(xin[t.slot][:], rows(a["x"], t.n * P, P)).then_inc(x_in[t.slot], 16)

            @tiles
            def load_v(t):
                wait(act, o["alt"], t.n - 3)
                for h in range(HEADS):
                    act.dma_start(vin[t.slot][h * WIN:(h + 1) * WIN, :, :],
                                  rows(a["kvtab"], t.n * P, P)[:, D + h * VW:D + h * VW + HD].rearrange("(w n) d -> n w d", n=WIN)).then_inc(v_in[t.slot], 16)

            @tiles
            def store(t):
                act.wait_ge(o["x2"], t.n + 1)
                act.dma_start(rows(a["x2tab"], t.n * P, P), x2[t.slot][:]).then_inc(x2_out[t.slot], 16)

            @tiles
            def mT_of(t):
                act.wait_ge(o["pm"], t.n + 1)
                wait(act, o["po"], t.n - 1)
                act.activation(mT[t.par][:].rearrange("d h (w n) -> d w h n", n=WIN),
                               pm[t.par][0:HD, :, :].rearrange("d w (h n) -> d w h n", n=WIN), ACT.Copy).then_inc(o["mT"], 1)

            def sd_from(name, var, out):
                @tiles
                def op(t):
                    act.wait_ge(o[name], t.n + 1)
                    act.activation(out[t.slot][:], var(t.slot), ACT.Sqrt, bias=g.eps[:, 0:1]).then_inc(o[{"mv": "sd", "mv2": "sd2", "vz": "sd3"}[name]], 1)
                return op
            sd_of = sd_from("mv", lambda b: mv[b][:, 1:2], sd)
            sd2_of = sd_from("mv2", lambda b: mv2[b][:, 1:2], sd2)
            sd3_of = sd_from("vz", lambda b: vz[b][:], sd3)

            @tiles
            def zT_of(t):
                act.wait_ge(o["pz"], t.n + 1)
                wait(act, o["pl"], t.n - 1)
                act.activation(zT[t.par][:], pz[t.par], ACT.Copy).then_inc(o["zT"], 1)

            def body(t):
                load_v(t + 3)
                load_x(t + 2)
                sd3_of(t - 3)
                zT_of(t - 3)
                mT_of(t + 1)
                store(t - 2)
                sd2_of(t - 2)
                sd_of(t)
            walk(act, -3, NT + 2, body, head=3, tail=6)
            for i in four:
                act.wait_ge(x2_out[i], 16 * ((NT + 3 - i) // 4))

        @block.tensor
        def _(pe):
            @tiles
            def turn_m(t):
                pe.wait_ge(o["mix"], t.n + 1)
                wait(pe, o["mT"], t.n - 1)
                pe.sem_inc(pe_seen, 1)
                for w in range(WPT):
                    last = nc.tensor.transpose(pm[t.par][0:HD, w, :], msg[t.slot][:, w, :], g.ident[:])
                last.then_inc(o["pm"], 1)

            @tiles
            def out(t):
                pe.wait_ge(o["mT"], t.n + 1)
                wait(pe, o["y"], t.n - 1)
                for h in range(HEADS):
                    last = nc.tensor.matmul(po[t.par], mT[t.par][:, h, :], g.wo[:, h, :], start=(h == 0), stop=(h == HEADS - 1))
                last.then_inc(o["po"], 1)

            @tiles
            def turn_z(t):
                pe.wait_ge(o["z"], t.n + 1)
                wait(pe, o["zT"], t.n - 1)
                for c in range(KD):
                    last = nc.tensor.transpose(pz[t.par][:, c, :], z[t.slot][:, c * P:(c + 1) * P], g.ident[:])
                last.then_inc(o["pz"], 1)

            @tiles
            def router(t):
                pe.wait_ge(o["zT"], t.n + 1)
                wait(pe, o["lg"], t.n - 1)
                for c in range(KD):
                    last = nc.tensor.matmul(pl[t.par], zT[t.par][:, c, :], g.wr[:, c, :], start=(c == 0), stop=(c == KD - 1))
                last.then_inc(o["pl"], 1)

            def body(t):
                turn_z(t - 3)
                turn_m(t + 1)
                router(t - 3)
                out(t + 1)
            walk(pe, -1, NT + 2, body, head=3, tail=4)


def route(nc, a, g, s):
    sb, ps, sem = s.sb, s.ps, s.sem
    C = NT * E
    m1, m2, both_m = sb("m1", [P, NT, E]), sb("m2", [P, NT, E]), sb("both", [P, NT, E])
    tot, run, off = sb("tot", [P, NT, E]), sb("run", [P, NT, E]), sb("off", [P, NT, E])
    sel = sb("sel", [P, NT, E])
    one = sb("one", [P, NT])
    cnt, cnti, tiles_i = sb("cnt", [P, E]), sb("cnti", [P, E], I32), sb("tiles_i", [P, E], I32)
    tiles, cum, base = sb("tiles", [P, E]), sb("cum", [P, E]), sb("base", [P, E])
    posf = sb("posf", [P, 2, NT])
    eof = [sb(f"eof{i}", [P, MT]) for i in range(2)]
    dif = sb("dif", [P, NT])
    ex = sb("ex", [P, NT])
    row = [sb(f"row{i}", [P, D]) for i in range(4)]
    ix = [sb(f"ix{i}", [P, 2], I32) for i in range(4)]
    pin, ptot = ps("pin", [P, C]), ps("ptot", [P, C])
    chain, masks_ok, counts_ok, dif_ok, ex_ok = (sem(x) for x in ("chain", "masks_ok", "counts_ok", "dif_ok", "ex_ok"))
    row_ok, ix_ok, seen = sem("row_ok"), sem("ix_ok"), sem("seen")
    out = [sem(f"out{i}") for i in range(4)]
    pick, b2s = g.pick, g.b2s
    pieces = sb("pieces", [E, 3, D], BF16)
    left = [sb(f"left{i}", [E, D]) for i in range(2)]
    cleared, split_ok, pieces_in, pick_ok = sem("cleared"), sem("split_ok"), sem("pieces_in"), sem("pick_ok")

    with s.block() as block:
        @block.vector
        def _(v):
            done = [0]

            def link(ins):
                done[0] += 1
                ins.then_inc(chain, 1)
                v.wait_ge(chain, done[0])

            iota = g.iota8[:, None, :].to_broadcast([P, NT, E])
            choice = g.top_i[:].rearrange("p (t k) -> p k t", k=2)
            logit = g.top_l[:].rearrange("p (t k) -> p k t", k=2)
            v.tensor_tensor(dif[:], logit[:, 1, :], logit[:, 0, :], ALU.subtract).then_inc(dif_ok, 1)
            v.memset(one[:], 1.0)
            v.tensor_tensor(m1[:], iota, choice[:, 0, :, None].to_broadcast([P, NT, E]), ALU.is_equal)
            link(v.tensor_tensor(m2[:], iota, choice[:, 1, :, None].to_broadcast([P, NT, E]), ALU.is_equal))
            v.tensor_tensor(both_m[:], m1[:], m2[:], ALU.add).then_inc(masks_ok, 1)
            v.wait_ge(counts_ok, 1)
            link(v.tensor_copy(tot[:], ptot.rearrange("p (t e) -> p t e", e=E)))
            for e in range(E):
                last = v.tensor_tensor_scan(out=run[:, :, e], data0=one[:], data1=tot[:, :, e], initial=0.0, op0=ALU.mult, op1=ALU.add)
            link(last)
            link(v.tensor_copy(cnt[:], run[:, NT - 1, :]))
            link(v.tensor_tensor(run[:], run[:], tot[:], ALU.subtract))
            link(v.tensor_tensor(off[:], run[:], pin.rearrange("p (t e) -> p t e", e=E), ALU.add))
            link(v.tensor_scalar(cnti[:], cnt[:], float(P - 1), None, ALU.add))
            link(v.tensor_single_scalar(tiles_i[:], cnti[:], 7, ALU.arith_shift_right))
            link(v.tensor_copy(tiles[:], tiles_i[:]))
            link(v.tensor_tensor_scan(out=cum[:], data0=one[:, 0:E], data1=tiles[:], initial=0.0, op0=ALU.mult, op1=ALU.add))
            link(v.tensor_tensor(base[:], cum[:], tiles[:], ALU.subtract))
            link(v.tensor_scalar(base[:], base[:], float(P), None, ALU.mult))
            link(v.tensor_tensor(off[:], off[:], base[:, None, :].to_broadcast([P, NT, E]), ALU.add))
            for k, m in enumerate((m1, m2)):
                link(v.tensor_tensor(sel[:], m[:], off[:], ALU.mult))
                link(v.reduce_sum(posf[:, k, :], sel[:], AX.X))
            link(v.tensor_copy(g.pos[:].rearrange("p (t k) -> p k t", k=2), posf[:]))
            link(v.tensor_scalar(eof[0][:], g.tileno[:], cum[:, 0:1], None, ALU.is_ge))
            for e in range(1, E - 1):
                link(v.scalar_tensor_tensor(out=eof[e % 2][:], in0=g.tileno[:], scalar=cum[:, e:e + 1], in1=eof[(e + 1) % 2][:],
                                            op0=ALU.is_ge, op1=ALU.add))
            link(v.tensor_copy(g.expert[:], eof[(E - 2) % 2][:]))
            v.wait_ge(ex_ok, 1)
            link(v.tensor_scalar(dif[:], ex[:], 1.0, None, ALU.add))
            link(v.reciprocal(g.w1[:], dif[:]))
            link(v.tensor_tensor(g.w2[:], ex[:], g.w1[:], ALU.mult))

            def stage(t):
                b = t.slot
                wait(v, out[b], t.turn * 32)
                v.tensor_scalar(row[b][:], g.x1[:, bass.ds(t.n * D, D)], 1.0, None, ALU.mult).then_inc(row_ok, 1)
                v.tensor_scalar(ix[b][:], g.pos[:, bass.ds(t.n * 2, 2)], 1.0, None, ALU.mult).then_inc(ix_ok, 1)
            walk(v, 0, NT - 1, stage)
            v.memset(b2s[:], 0.0).then_inc(cleared, 1)
            rest = g.b2f
            for k in range(3):
                last = v.tensor_copy(pieces[:, k, :], rest[:])
                if k < 2:
                    link(last)
                    link(v.tensor_tensor(left[k][:], rest[:], pieces[:, k, :], ALU.subtract))
                    rest = left[k]
            last.then_inc(split_ok, 1)

        @block.sync
        def _(sp):
            sp.wait_ge(split_ok, 1)
            sp.wait_ge(cleared, 1)
            for k in range(3):
                sp.dma_start(b2s[k * E:(k + 1) * E, :], pieces[:, k, :]).then_inc(pieces_in, 16)
            sp.wait_ge(pieces_in, 16 * 3)

        @block.scalar
        def _(act):
            act.wait_ge(dif_ok, 1)
            act.activation(ex[:], dif[:], ACT.Exp).then_inc(ex_ok, 1)

        @block.tensor
        def _(pe):
            pe.wait_ge(masks_ok, 1)
            flat = both_m[:].rearrange("p t e -> p (t e)")
            nc.tensor.matmul(pin, g.tri[:], flat, start=True, stop=True)
            nc.tensor.matmul(ptot, g.ones[:], flat, start=True, stop=True).then_inc(counts_ok, 1)

        @block.gpsimd
        def _(pool):
            pool.memset(pick[:], 0.0).then_inc(pick_ok, 1)
            for k in range(3):
                pool.wait_ge(pick_ok, k + 1)
                pool.affine_select(out=pick[:].rearrange("p (e n) -> p e n", e=E), in_=pick[:].rearrange("p (e n) -> p e n", e=E),
                                   compare_op=ALU.not_equal, fill=1.0, base=-k * E, pattern=[[-1, E], [0, P]],
                                   channel_multiplier=1).then_inc(pick_ok, 1)

            def scatter(t):
                b = t.slot
                pool.wait_ge(row_ok, t.n + 1)
                pool.sem_inc(seen, 1)
                pool.wait_ge(ix_ok, t.n + 1)
                pool.sem_inc(seen, 1)
                for k in range(2):
                    pool.indirect_dma_start(out=a["xs"], out_offset=bass.IndirectOffsetOnAxis(ap=ix[b][:, k:k + 1], axis=0),
                                            in_=row[b][:], in_offset=None).then_inc(out[b], 16)
            walk(pool, 0, NT - 1, scatter)
            for i in range(4):
                pool.wait_ge(out[i], 32 * ((NT + 3 - i) // 4))


def experts(nc, a, g, s):
    sb, ps, sem = s.sb, s.ps, s.sem
    two, four = range(2), range(4)
    w1 = sb("w1", [P, E * KD * H])
    w2 = sb("w2", [P, E * KH * D])
    pick, b2s = g.pick, g.b2s
    w1t = [sb(f"w1t{i}", [P, KD * H]) for i in two]
    xs = [sb(f"xs{i}", [P, D]) for i in four]
    gb = [sb(f"gb{i}", [P, GREC]) for i in four]
    xT = [sb(f"xT{i}", [P, KD, P]) for i in two]
    hT = [sb(f"hT{i}", [P, KH, P]) for i in two]
    y = [sb(f"y{i}", [P, D]) for i in two]
    px = ps("px", [P, KD, P])
    ph = [[ps(f"ph{i}{j}", [P, 4, P]) for j in two] for i in two]
    py = ps("py", [P, D])
    w_ready = sem("w_ready")
    x_in = [sem(f"x_in{i}") for i in four]
    w_in = [sem(f"w_in{e}") for e in range(E)]
    y_out = [sem(f"y_out{i}") for i in two]
    px_ok, xT_ok, w1_ok, w1_seen, py_ok, y_ok = (sem(x) for x in ("px_ok", "xT_ok", "w1_ok", "w1_seen", "py_ok", "y_ok"))
    ph_ok = [sem(f"ph_ok{j}") for j in two]
    h_ok = [sem(f"h_ok{j}") for j in two]

    with s.block() as block:
        @block.sync
        def _(sp):
            def load(t):
                e = sp.value_load(g.expert[0:1, bass.ds(t.n, 1)], min_val=0, max_val=E - 1)
                wait(sp, px_ok, t.n - 3)
                sp.dma_start(xs[t.slot][:], rows(a["xs"], t.n * P, P)).then_inc(x_in[t.slot], 16)
                wait(sp, xT_ok, t.n - 3)
                wait(sp, h_ok[1], t.n - 3)
                sp.dma_start(gb[t.slot][:], a["lngb"][bass.ds(e, 1), :, :].rearrange("o p k -> p (o k)")).then_inc(x_in[t.slot], 16)

            def store(t):
                sp.wait_ge(y_ok, t.n + 1)
                sp.dma_start(rows(a["ys"], t.n * P, P), y[t.par][:]).then_inc(y_out[t.par], 16)

            for n in four:
                load(Step(0, n))

            def both(t):
                load(t + 4)
                store(t)
            walk(sp, 0, MT - 5, both)
            for n in range(MT - 4, MT):
                store(Step(0, n))
            for i in two:
                sp.wait_ge(y_out[i], 16 * ((MT + 1 - i) // 2))

        @block.gpsimd
        def _(pool):
            for e in range(E):
                pool.dma_start(w1[:, e * KD * H:(e + 1) * KD * H].rearrange("p (c n) -> p c n", c=KD),
                               a["W1"][e, :, :].rearrange("(c p) n -> p c n", p=P)).then_inc(w_in[e], 16)
                pool.dma_start(w2[:, e * KH * D:(e + 1) * KH * D].rearrange("p (c n) -> p c n", c=KH),
                               a["W2"][e, :, :].rearrange("(c p) n -> p c n", p=P)).then_inc(w_in[e], 16)
            for e in range(E):
                pool.wait_ge(w_in[e], 32)
                pool.sem_inc(w_ready, 1)

        @block.vector
        def _(v):
            def w1_of(t):
                ex = v.value_load(g.expert[0:1, bass.ds(t.n, 1)], min_val=0, max_val=E - 1)
                v.wait_ge(w_ready, ex + 1)
                v.sem_inc(w1_seen, 1)
                wait(v, ph_ok[1], t.n - 1)
                v.tensor_scalar(w1t[t.par][:], w1[:, bass.ds(ex * (KD * H), KD * H)], 1.0, None, ALU.mult).then_inc(w1_ok, 1)

            def xT_of(t):
                b, x = t.par, t.slot
                v.wait_ge(x_in[x], t.turn * 32 + 32)
                v.wait_ge(px_ok, t.n + 1)
                wait(v, ph_ok[1], t.n - 1)
                for c in range(KD):
                    last = v.tensor_scalar(xT[b][:, c, :], px[:, c, :], gb[x][:, c:c + 1], gb[x][:, KD + c:KD + c + 1], ALU.mult, ALU.add)
                last.then_inc(xT_ok, 1)

            def y_of(t):
                b = t.par
                v.wait_ge(py_ok, t.n + 1)
                wait(v, y_out[b], t.half * 16)
                v.tensor_copy(y[b][:], py[:]).then_inc(y_ok, 1)

            for n in two:
                w1_of(Step(0, n))
                xT_of(Step(0, n))

            def body(t):
                w1_of(t + 1)
                xT_of(t + 1)
                y_of(t - 1)
            walk(v, 1, MT - 2, body)
            for n in (MT - 2, MT - 1):
                y_of(Step(0, n))

        @block.scalar
        def _(act):
            def h_of(t):
                b = t.par
                for j in two:
                    act.wait_ge(ph_ok[j], t.n + 1)
                    if j == 0:
                        wait(act, py_ok, t.n - 1)
                        act.wait_ge(x_in[t.slot], t.turn * 32 + 32)
                    for m in range(4 * j, 4 * j + 4):
                        last = act.activation(hT[b][:, m, :], ph[b][j][:, m % 4, :], ACT.Gelu,
                                              bias=gb[t.slot][:, 2 * KD + m:2 * KD + m + 1])
                    last.then_inc(h_ok[j], 1)
            walk(act, 0, MT - 1, h_of)

        @block.tensor
        def _(pe):
            def turn_x(t):
                pe.wait_ge(x_in[t.slot], t.turn * 32 + 32)
                wait(pe, xT_ok, t.n)
                for c in range(KD):
                    last = nc.tensor.transpose(px[:, c, :], xs[t.slot][:, c * P:(c + 1) * P], g.ident[:])
                last.then_inc(px_ok, 1)

            def hidden(t):
                b = t.par
                pe.wait_ge(xT_ok, t.n + 1)
                pe.wait_ge(w1_ok, t.n + 1)
                for j in two:
                    wait(pe, h_ok[j], t.n - 1)
                    for m in range(4 * j, 4 * j + 4):
                        for c in range(KD):
                            last = nc.tensor.matmul(ph[b][j][:, m % 4, :], w1t[b][:, c * H + m * P:c * H + (m + 1) * P], xT[b][:, c, :],
                                                    start=(c == 0), stop=(c == KD - 1))
                    last.then_inc(ph_ok[j], 1)

            def back(t, e):
                b = t.par
                pe.wait_ge(w_ready, e + 1)
                wait(pe, y_ok, t.n)
                nc.tensor.matmul(py[:], pick[:, bass.ds(e * P, P)], b2s[:], start=True, stop=False)
                for c in range(KH):
                    if c % 4 == 0:
                        pe.wait_ge(h_ok[c // 4], t.n + 1)
                    last = nc.tensor.matmul(py[:], hT[b][:, c, :], w2[:, bass.ds(e * (KH * D) + c * D, D)], start=False, stop=(c == KH - 1))
                last.then_inc(py_ok, 1)

            def expert(t):
                return pe.value_load(g.expert[0:1, bass.ds(t.n, 1)], min_val=0, max_val=E - 1)

            turn_x(Step(0, 0))
            turn_x(Step(0, 1))
            hidden(Step(0, 0))

            def body(t):
                turn_x(t + 1)
                hidden(t)
                back(t - 1, expert(t - 1))
            walk(pe, 1, MT - 2, body)
            hidden(Step(0, MT - 1))
            back(Step(0, MT - 2), expert(Step(0, MT - 2)))
            back(Step(0, MT - 1), expert(Step(0, MT - 1)))


def combine(nc, a, g, s):
    sb, sem = s.sb, s.sem
    four = range(4)
    ix = [sb(f"ix{i}", [P, 2], I32) for i in four]
    y1 = [sb(f"y1{i}", [P, D]) for i in four]
    y2 = [sb(f"y2{i}", [P, D]) for i in four]
    x2 = [sb(f"x2{i}", [P, D]) for i in four]
    m = [sb(f"m{i}", [P, D]) for i in four]
    o = [sb(f"o{i}", [P, D]) for i in four]
    y_in = [sem(f"y_in{i}") for i in four]
    x_in = [sem(f"x_in{i}") for i in four]
    stored = [sem(f"stored{i}") for i in four]
    ix_ok, m_ok, o_ok, seen = sem("ix_ok"), sem("m_ok"), sem("o_ok"), sem("seen")

    with s.block() as block:
        @block.sync
        def _(sp):
            def load(t):
                wait(sp, m_ok, t.n - 3)
                sp.dma_start(x2[t.slot][:], rows(a["x2tab"], t.n * P, P)).then_inc(x_in[t.slot], 16)
            walk(sp, 0, NT - 1, load)

        @block.gpsimd
        def _(pool):
            def gather(t):
                b = t.slot
                wait(pool, o_ok, t.n - 3)
                pool.sem_inc(seen, 1)
                pool.wait_ge(ix_ok, t.n + 1)
                pool.sem_inc(seen, 1)
                for k, y in enumerate((y1, y2)):
                    pool.indirect_dma_start(out=y[b][:], out_offset=None, in_=a["ys"],
                                            in_offset=bass.IndirectOffsetOnAxis(ap=ix[b][:, k:k + 1], axis=0)).then_inc(y_in[b], 16)
            walk(pool, 0, NT - 1, gather)

        @block.vector
        def _(v):
            def index(t):
                wait(v, y_in[t.slot], t.turn * 32)
                v.tensor_scalar(ix[t.slot][:], g.pos[:, bass.ds(t.n * 2, 2)], 1.0, None, ALU.mult).then_inc(ix_ok, 1)

            def add(t):
                b = t.slot
                v.wait_ge(y_in[b], t.turn * 32 + 32)
                v.wait_ge(x_in[b], t.turn * 16 + 16)
                v.scalar_tensor_tensor(out=m[b][:], in0=y1[b][:], scalar=g.w1[:, bass.ds(t.n, 1)], in1=x2[b][:], op0=ALU.mult, op1=ALU.add).then_inc(m_ok, 1)
                v.wait_ge(m_ok, t.n + 1)
                wait(v, stored[b], t.turn * 16)
                v.scalar_tensor_tensor(out=o[b][:], in0=y2[b][:], scalar=g.w2[:, bass.ds(t.n, 1)], in1=m[b][:], op0=ALU.mult, op1=ALU.add).then_inc(o_ok, 1)

            for n in range(3):
                index(Step(0, n))

            def body(t):
                index(t + 3)
                add(t)
            walk(v, 0, NT - 4, body)
            for n in range(NT - 3, NT):
                add(Step(0, n))

        @block.scalar
        def _(act):
            def store(t):
                act.wait_ge(o_ok, t.n + 1)
                act.dma_start(rows(a["out"], t.n * P, P), o[t.slot][:]).then_inc(stored[t.slot], 16)
            walk(act, 0, NT - 1, store)
            for i in four:
                act.wait_ge(stored[i], 16 * ((NT + 3 - i) // 4))


class Kept:
    pass


def program(nc, a):
    with ExitStack() as whole:
        g = Kept()

        def buf(stack, name, shape, dt=F32):
            return stack.enter_context(nc.sbuf_tensor("g_" + name, shape, dt))

        g.gp = whole.enter_context(nc.semaphore("gp"))
        g.ident = buf(whole, "ident", [P, P])
        g.tri = buf(whole, "tri", [P, P])
        g.ones = buf(whole, "ones", [P, P])
        g.eps = buf(whole, "eps", [P, 1])
        g.iota8 = buf(whole, "iota8", [P, E])
        g.tileno = buf(whole, "tileno", [P, MT])
        g.bo = buf(whole, "bo", [P, D])
        g.gamma = buf(whole, "gamma", [P, D])
        g.beta = buf(whole, "beta", [P, D])
        g.br = buf(whole, "br", [P, E])
        g.wr = buf(whole, "wr", [P, KD, E])
        g.wo = buf(whole, "wo", [HD, HEADS, D])
        g.b2f = buf(whole, "b2f", [E, D])
        g.pick = buf(whole, "pick", [P, E * P], BF16)
        g.b2s = buf(whole, "b2s", [P, D], BF16)
        g.top_l = buf(whole, "top_l", [P, NT * 2])
        g.top_i = buf(whole, "top_i", [P, NT * 2])
        g.pos = buf(whole, "pos", [P, NT * 2])
        g.w1 = buf(whole, "w1", [P, NT])
        g.w2 = buf(whole, "w2", [P, NT])
        g.expert = buf(whole, "expert", [P, MT], I32)
        with ExitStack() as rows_kept:
            g.x1 = buf(rows_kept, "x1", [P, NT * D])
            with ExitStack() as graph:
                g.idx = buf(graph, "idx", [P, STEPS_PAD], I32)
                g.wreg = buf(graph, "wreg", [1, STEPS_PAD], I32)
                g.lastreg = buf(graph, "lastreg", [1, NWIN], I32)
                g.fresh = buf(graph, "fresh", [P, STEPS])
                g.rmod = buf(graph, "rmod", [P, 1])
                with ExitStack() as proj:
                    g.wq = buf(proj, "wq", [P, KD, D])
                    g.wkv = buf(proj, "wkv", [P, KD, 2 * D])
                    g.wqr = buf(proj, "wqr", [P, KD, D])
                    g.ncq = buf(proj, "ncq", [P, 2])
                    g.ncqr = buf(proj, "ncqr", [P, 2])
                    g.ckv = buf(proj, "ckv", [P, 2 * D])
                    with Scope(nc, "setup") as s:
                        setup(nc, a, g, s)
                    with Scope(nc, "nodes") as s:
                        nodes(nc, a, g, s)
                with Scope(nc, "edges") as s:
                    edges(nc, a, g, s)
                with Scope(nc, "post") as s:
                    post(nc, a, g, s)
            with Scope(nc, "route") as s:
                route(nc, a, g, s)
        with Scope(nc, "experts") as s:
            experts(nc, a, g, s)
        with Scope(nc, "combine") as s:
            combine(nc, a, g, s)


def kernel(**inputs):
    import concourse.bacc as bacc
    from concourse.bass_utils import run_bass_kernel_spmd as run

    nc = bacc.Bacc("TRN2", target_bir_lowering=False, num_devices=1)
    raw = {k: np.asarray(v) for k, v in inputs.items()}

    def padded(v, n, fill):
        out = np.full((n,) + v.shape[1:], fill, v.dtype)
        out[:len(v)] = v
        return out

    dst = padded(raw["dst"], ET_PAD * P, PAD_DST)
    ins = {
        "x": padded(raw["x"], NPAD, 0),
        "edges": np.stack([e.reshape(ET_PAD, P) for e in (
            padded(raw["src"], ET_PAD * P, 0), dst, padded(raw["edge_type_64"], ET_PAD * P, 0))], 1).reshape(ET_PAD, 3 * P),
        "first": dst[P:ET * P:P],
        "q_emb": raw["L0_gnn_query_emb"].reshape(KD, P).T,
        "bq": raw["L0_gnn_bq"].reshape(KD, P).T,
        "WqT": raw["L0_gnn_Wq"].T,
        "relT": raw["L0_gnn_rel_w"].T,
    }
    for name in ("Wq", "Wk", "bk", "Wv", "bv", "Wo", "bo", "gamma", "beta"):
        ins[name] = raw["L0_gnn_" + name]
    for name in ("Wr", "br", "W1", "W2", "b2"):
        ins[name] = raw["L0_ffn_" + name]
    ins["lngb"] = np.concatenate([raw["L0_ffn_" + n].reshape(E, -1, P) for n in ("ln_g", "ln_b", "b1")], 1).transpose(0, 2, 1)
    ins = {k: np.ascontiguousarray(v) for k, v in ins.items()}
    a = {k: nc.dram_tensor(k, v.shape, mybir.dt.from_np(v.dtype), kind="ExternalInput").ap() for k, v in ins.items()}
    a["out"] = nc.dram_tensor("out", (NPAD, D), F32, kind="ExternalOutput").ap()
    for name, shape, dt in (("kvtab", (NPAD, ROW), F32), ("qtab", (NWIN, P, QREC), F32), ("acctab", (P, STEPS * VW), F32),
                            ("dts", (STEPS_PAD // 4, 8 * P), I8), ("wtab", (STEPS_PAD,), I32), ("lasttab", (2 * P,), I32),
                            ("x2tab", (NPAD, D), F32), ("xs", (MT * P, D), F32), ("ys", (MT * P, D), F32)):
        a[name] = nc.dram_tensor(name, shape, dt, kind="Internal").ap()
    program(nc, a)
    r = run(nc, [ins], core_ids=[0])
    return r.results[0]["out"][:N_NODES]
```
